# Optimizing a Trainium2 kernel written in Bass

```python
import numpy as np
import jax
import jax.numpy as jnp

def _softmax(x, axis=-1):
    return jax.nn.softmax(x, axis=axis)

def _gelu(x):
    return jax.nn.gelu(x, approximate=True)

def _silu(x):
    return jax.nn.silu(x)

def _sigmoid(x):
    return jax.nn.sigmoid(x)

def _layernorm(x, axis=-1, eps=1e-05):
    m = jnp.mean(x, axis=axis, keepdims=True)
    v = jnp.var(x, axis=axis, keepdims=True)
    return (x - m) / jnp.sqrt(v + eps)

def _scatter_add(tgt, idx, src, axis=0):
    return tgt.at[idx].add(src)

def _segment_sum(src, seg, n):
    return jax.ops.segment_sum(src, seg, n)
kernel_name = 'mk_gnn_preln_d4_gnn_r32_aac218'

def setup_inputs(seed: int=0):
    np.random.seed(seed)
    _w = jnp.asarray

    def _rec_inputs():
        import jax
        import jax.numpy as jnp
        _gk = jax.random.key(seed)
        x = 8.953e-05 + 1 * jax.random.normal(jax.random.fold_in(_gk, 1), (3125, 64), jnp.float32)
        src = jax.random.randint(jax.random.fold_in(_gk, 2), (100000,), 0, 3125, jnp.int32)
        dst = jax.random.randint(jax.random.fold_in(_gk, 3), (100000,), 0, 3125, jnp.int32)
        _o = jnp.argsort(dst, stable=True)
        src = src[_o]
        dst = dst[_o]
        edge_attr_32 = 0.000196303 + 1.00016 * jax.random.normal(jax.random.fold_in(_gk, 11), (100000, 32), jnp.float32)
        edge_attr_64 = 1.36993e-05 + 0.999972 * jax.random.normal(jax.random.fold_in(_gk, 12), (100000, 64), jnp.float32)
        edge_attr_9 = 0.000739051 + 0.999958 * jax.random.normal(jax.random.fold_in(_gk, 13), (100000, 9), jnp.float32)
        edge_weight = jax.random.uniform(jax.random.fold_in(_gk, 15), (100000,), jnp.float32, 0.0, 0.999998)
        return (x, src, dst, edge_attr_32, edge_attr_64, edge_attr_9, edge_weight)
    x, src, dst, edge_attr_32, edge_attr_64, edge_attr_9, edge_weight = _rec_inputs()

    def _L0_gnn_setup():
        import jax, jax.numpy as jnp
        import numpy as np
        N, E = (10000, 10000)
        D, S, HE = (64, 9, 64)
        H, DQK, DV = (8, 16, 16)
        OK, OV = (H * DQK, H * DV)
        EPS_BN = 1e-05

        def tensor_product(x_e, sh, w, C):
            acc = sh[:, 0:1] * (x_e @ C[:, 0, :])
            for s in range(1, S):
                acc = acc + sh[:, s:s + 1] * (x_e @ C[:, s, :])
            return acc * w

        def mlp2(x, w1, b1, w2, b2):
            return jax.nn.relu(x @ w1 + b1) @ w2 + b2
        key = jax.random.key(seed)
        ks = jax.random.split(key, 20)
        g = lambda k, shape, fan: jax.random.normal(k, shape, jnp.float32) / np.float32(np.sqrt(fan))
        return {'tfn_features': jax.random.normal(ks[0], (N, D), jnp.float32), 'edge_features': jax.random.normal(ks[1], (E, HE), jnp.float32), 'edge_sh': jax.random.normal(ks[2], (E, S), jnp.float32), 'Wq': g(ks[3], (D, OK), D), 'Cqk': g(ks[4], (D, S, OK), D * S), 'Cv': g(ks[5], (D, S, OV), D * S), 'k_w1': g(ks[6], (HE, HE), HE), 'k_b1': jnp.zeros((HE,), jnp.float32), 'k_w2': g(ks[7], (HE, OK), HE), 'k_b2': jnp.zeros((OK,), jnp.float32), 'v_w1': g(ks[8], (HE, HE), HE), 'v_b1': jnp.zeros((HE,), jnp.float32), 'v_w2': g(ks[9], (HE, OV), HE), 'v_b2': jnp.zeros((OV,), jnp.float32), 'W_out': g(ks[10], (OV, D), OV), 'W_self': g(ks[11], (D, D), D), 'gamma': jnp.ones((D,), jnp.float32), 'beta': jnp.zeros((D,), jnp.float32), 'edge_index': jax.random.randint(ks[12], (2, E), 0, N, dtype=jnp.int32)}
    _L0_gnn_all = _L0_gnn_setup()
    _L0_gnn_in = {k: v for k, v in _L0_gnn_all.items() if k in ('Wq', 'Cqk', 'Cv', 'k_w1', 'k_b1', 'k_w2', 'k_b2', 'v_w1', 'v_b1', 'v_w2', 'v_b2', 'W_out', 'W_self', 'gamma', 'beta')}
    del _L0_gnn_all

    def _L1_gnn_setup():
        import jax, jax.numpy as jnp
        import numpy as np
        N_NODES = 3125
        N_EDGES = 25000
        C = 64
        H = 4
        LN_EPS = 1e-05
        SM_EPS = 1e-08
        key = jax.random.key(seed)
        ks = jax.random.split(key, 8)
        return {'x': jax.random.normal(ks[0], (N_NODES, C), dtype=jnp.float32), 'edge_index': jax.random.randint(ks[1], (2, N_EDGES), 0, N_NODES, dtype=jnp.int64), 'edge_time': jax.random.uniform(ks[2], (N_EDGES,), dtype=jnp.float32), 'current_time': 1, 'W_w': jax.random.normal(ks[3], (C, C), dtype=jnp.float32) * (1.0 / np.sqrt(C)), 'W_b': jnp.zeros((C,), dtype=jnp.float32), 'attn_w': jax.random.normal(ks[4], (2 * C, H), dtype=jnp.float32) * (1.0 / np.sqrt(2 * C)), 'attn_b': jnp.zeros((H,), dtype=jnp.float32), 'decay_rate': jnp.full((1,), 0.1, dtype=jnp.float32), 'proj_w': jax.random.normal(ks[5], (C * H, C), dtype=jnp.float32) * (1.0 / np.sqrt(C * H)), 'proj_b': jnp.zeros((C,), dtype=jnp.float32), 'ln_g': jnp.ones((C,), dtype=jnp.float32), 'ln_b': jnp.zeros((C,), dtype=jnp.float32)}
    _L1_gnn_all = _L1_gnn_setup()
    _L1_gnn_in = {k: v for k, v in _L1_gnn_all.items() if k in ('W_w', 'W_b', 'attn_w', 'attn_b', 'decay_rate', 'proj_w', 'proj_b', 'ln_g', 'ln_b')}
    del _L1_gnn_all

    def _L2_gnn_setup():
        import jax, jax.numpy as jnp
        import numpy as np
        N_NODES = 3125
        N_EDGES = 1250000
        D = 64
        L = 3
        BN_EPS = 1e-05
        key = jax.random.key(seed)
        ks = jax.random.split(key, 5)
        x = jax.random.normal(ks[0], (N_NODES, D), dtype=jnp.float32)
        edge_index = jax.random.randint(ks[1], (2, N_EDGES), 0, N_NODES, dtype=jnp.int64)
        W1 = jax.random.normal(ks[2], (L, D, D), dtype=jnp.float32) * 0.1
        W2 = jax.random.normal(ks[3], (L, D, D), dtype=jnp.float32) * 0.1
        gamma = jnp.ones((L, D), dtype=jnp.float32)
        beta = jnp.zeros((L, D), dtype=jnp.float32)
        eps = jnp.zeros((L,), dtype=jnp.float32)
        return {'x': x, 'edge_index': edge_index, 'W1': W1, 'W2': W2, 'gamma': gamma, 'beta': beta, 'eps': eps}
    _L2_gnn_all = _L2_gnn_setup()
    _L2_gnn_in = {k: v for k, v in _L2_gnn_all.items() if k in ('W1', 'W2', 'gamma', 'beta', 'eps')}
    del _L2_gnn_all

    def _L3_gnn_setup():
        import jax, jax.numpy as jnp
        import numpy as np
        N, E = (3125, 25000)
        NODE_DIM, EDGE_DIM, HIDDEN = (64, 32, 128)
        LN_EPS = 1e-05

        def _linear_params(key, fan_in, fan_out):
            kw, kb = jax.random.split(key)
            bound = 1.0 / np.sqrt(fan_in)
            W = jax.random.uniform(kw, (fan_in, fan_out), jnp.float32, -bound, bound)
            b = jax.random.uniform(kb, (fan_out,), jnp.float32, -bound, bound)
            return (W, b)

        def _layer_norm(h, gamma, beta):
            mu = jnp.mean(h, axis=-1, keepdims=True)
            var = jnp.mean(jnp.square(h - mu), axis=-1, keepdims=True)
            return (h - mu) * jax.lax.rsqrt(var + LN_EPS) * gamma + beta

        def _mlp(h, W1, b1, gamma, beta, W2, b2):
            h = h @ W1 + b1
            h = jax.nn.silu(_layer_norm(h, gamma, beta))
            return h @ W2 + b2
        key = jax.random.key(seed)
        ks = jax.random.split(key, 8)
        x = jax.random.normal(ks[0], (N, NODE_DIM), jnp.float32)
        edge_index = jax.random.randint(ks[1], (2, E), 0, N, jnp.int32)
        edge_attr = jax.random.normal(ks[2], (E, EDGE_DIM), jnp.float32)
        msg_in = 2 * NODE_DIM + EDGE_DIM
        W_msg1, b_msg1 = _linear_params(ks[3], msg_in, HIDDEN)
        g_msg = jnp.ones((HIDDEN,), jnp.float32)
        be_msg = jnp.zeros((HIDDEN,), jnp.float32)
        W_msg2, b_msg2 = _linear_params(ks[4], HIDDEN, HIDDEN)
        upd_in = NODE_DIM + HIDDEN
        W_upd1, b_upd1 = _linear_params(ks[5], upd_in, HIDDEN)
        g_upd = jnp.ones((HIDDEN,), jnp.float32)
        be_upd = jnp.zeros((HIDDEN,), jnp.float32)
        W_upd2, b_upd2 = _linear_params(ks[6], HIDDEN, NODE_DIM)
        return {'x': x, 'edge_index': edge_index, 'edge_attr': edge_attr, 'W_msg1': W_msg1, 'b_msg1': b_msg1, 'g_msg': g_msg, 'be_msg': be_msg, 'W_msg2': W_msg2, 'b_msg2': b_msg2, 'W_upd1': W_upd1, 'b_upd1': b_upd1, 'g_upd': g_upd, 'be_upd': be_upd, 'W_upd2': W_upd2, 'b_upd2': b_upd2}
    _L3_gnn_all = _L3_gnn_setup()
    _L3_gnn_in = {k: v for k, v in _L3_gnn_all.items() if k in ('W_msg1', 'b_msg1', 'g_msg', 'be_msg', 'W_msg2', 'b_msg2', 'W_upd1', 'b_upd1', 'g_upd', 'be_upd', 'W_upd2', 'b_upd2')}
    del _L3_gnn_all
    return {'x': x, 'src': src, 'dst': dst, 'edge_attr_32': edge_attr_32, 'edge_attr_64': edge_attr_64, 'edge_attr_9': edge_attr_9, 'edge_weight': edge_weight, 'L0_gnn_Wq': _L0_gnn_in['Wq'], 'L0_gnn_Cqk': _L0_gnn_in['Cqk'], 'L0_gnn_Cv': _L0_gnn_in['Cv'], 'L0_gnn_k_w1': _L0_gnn_in['k_w1'], 'L0_gnn_k_b1': _L0_gnn_in['k_b1'], 'L0_gnn_k_w2': _L0_gnn_in['k_w2'], 'L0_gnn_k_b2': _L0_gnn_in['k_b2'], 'L0_gnn_v_w1': _L0_gnn_in['v_w1'], 'L0_gnn_v_b1': _L0_gnn_in['v_b1'], 'L0_gnn_v_w2': _L0_gnn_in['v_w2'], 'L0_gnn_v_b2': _L0_gnn_in['v_b2'], 'L0_gnn_W_out': _L0_gnn_in['W_out'], 'L0_gnn_W_self': _L0_gnn_in['W_self'], 'L0_gnn_gamma': _L0_gnn_in['gamma'], 'L0_gnn_beta': _L0_gnn_in['beta'], 'L1_gnn_W_w': _L1_gnn_in['W_w'], 'L1_gnn_W_b': _L1_gnn_in['W_b'], 'L1_gnn_attn_w': _L1_gnn_in['attn_w'], 'L1_gnn_attn_b': _L1_gnn_in['attn_b'], 'L1_gnn_decay_rate': _L1_gnn_in['decay_rate'], 'L1_gnn_proj_w': _L1_gnn_in['proj_w'], 'L1_gnn_proj_b': _L1_gnn_in['proj_b'], 'L1_gnn_ln_g': _L1_gnn_in['ln_g'], 'L1_gnn_ln_b': _L1_gnn_in['ln_b'], 'L2_gnn_W1': _L2_gnn_in['W1'], 'L2_gnn_W2': _L2_gnn_in['W2'], 'L2_gnn_gamma': _L2_gnn_in['gamma'], 'L2_gnn_beta': _L2_gnn_in['beta'], 'L2_gnn_eps': _L2_gnn_in['eps'], 'L3_gnn_W_msg1': _L3_gnn_in['W_msg1'], 'L3_gnn_b_msg1': _L3_gnn_in['b_msg1'], 'L3_gnn_g_msg': _L3_gnn_in['g_msg'], 'L3_gnn_be_msg': _L3_gnn_in['be_msg'], 'L3_gnn_W_msg2': _L3_gnn_in['W_msg2'], 'L3_gnn_b_msg2': _L3_gnn_in['b_msg2'], 'L3_gnn_W_upd1': _L3_gnn_in['W_upd1'], 'L3_gnn_b_upd1': _L3_gnn_in['b_upd1'], 'L3_gnn_g_upd': _L3_gnn_in['g_upd'], 'L3_gnn_be_upd': _L3_gnn_in['be_upd'], 'L3_gnn_W_upd2': _L3_gnn_in['W_upd2'], 'L3_gnn_b_upd2': _L3_gnn_in['b_upd2']}

def reference(x, src, dst, edge_attr_32, edge_attr_64, edge_attr_9, edge_weight, L0_gnn_Wq, L0_gnn_Cqk, L0_gnn_Cv, L0_gnn_k_w1, L0_gnn_k_b1, L0_gnn_k_w2, L0_gnn_k_b2, L0_gnn_v_w1, L0_gnn_v_b1, L0_gnn_v_w2, L0_gnn_v_b2, L0_gnn_W_out, L0_gnn_W_self, L0_gnn_gamma, L0_gnn_beta, L1_gnn_W_w, L1_gnn_W_b, L1_gnn_attn_w, L1_gnn_attn_b, L1_gnn_decay_rate, L1_gnn_proj_w, L1_gnn_proj_b, L1_gnn_ln_g, L1_gnn_ln_b, L2_gnn_W1, L2_gnn_W2, L2_gnn_gamma, L2_gnn_beta, L2_gnn_eps, L3_gnn_W_msg1, L3_gnn_b_msg1, L3_gnn_g_msg, L3_gnn_be_msg, L3_gnn_W_msg2, L3_gnn_b_msg2, L3_gnn_W_upd1, L3_gnn_b_upd1, L3_gnn_g_upd, L3_gnn_be_upd, L3_gnn_W_upd2, L3_gnn_b_upd2):
    import jax
    import jax.numpy as jnp

    def _L0_gnn_ref(tfn_features, edge_features, edge_sh, Wq, Cqk, Cv, k_w1, k_b1, k_w2, k_b2, v_w1, v_b1, v_w2, v_b2, W_out, W_self, gamma, beta, edge_index):
        import jax, jax.numpy as jnp
        import numpy as np
        N, E = (10000, 10000)
        D, S, HE = (64, 9, 64)
        H, DQK, DV = (8, 16, 16)
        OK, OV = (H * DQK, H * DV)
        EPS_BN = 1e-05

        def tensor_product(x_e, sh, w, C):
            acc = sh[:, 0:1] * (x_e @ C[:, 0, :])
            for s in range(1, S):
                acc = acc + sh[:, s:s + 1] * (x_e @ C[:, s, :])
            return acc * w

        def mlp2(x, w1, b1, w2, b2):
            return jax.nn.relu(x @ w1 + b1) @ w2 + b2
        edge_dst, edge_src = (edge_index[0], edge_index[1])
        n = tfn_features.shape[0]
        q = (tfn_features @ Wq).reshape(n, H, DQK)
        x_dst = tfn_features[edge_dst]
        wk = mlp2(edge_features, k_w1, k_b1, k_w2, k_b2)
        wv = mlp2(edge_features, v_w1, v_b1, v_w2, v_b2)
        k = tensor_product(x_dst, edge_sh, wk, Cqk).reshape(-1, H, DQK)
        v = tensor_product(x_dst, edge_sh, wv, Cv).reshape(-1, H, DV)
        attn = jnp.einsum('ehd,ehd->eh', q[edge_src], k)
        amax = jax.ops.segment_max(attn, edge_src, num_segments=n)
        ex = jnp.exp(attn - amax[edge_src])
        denom = jax.ops.segment_sum(ex, edge_src, num_segments=n)
        alpha = ex / (denom[edge_src] + 1e-16)
        upd = jax.ops.segment_sum(v * alpha[..., None], edge_src, num_segments=n)
        upd = upd.reshape(n, OV) @ W_out
        out = tfn_features @ W_self + upd
        mu = out.mean(axis=0)
        var = out.var(axis=0)
        return (out - mu) * jax.lax.rsqrt(var + EPS_BN) * gamma + beta

    def _L1_gnn_ref(x, edge_index, edge_time, current_time, W_w, W_b, attn_w, attn_b, decay_rate, proj_w, proj_b, ln_g, ln_b):
        import jax, jax.numpy as jnp
        import numpy as np
        N_NODES = 3125
        N_EDGES = 25000
        C = 64
        H = 4
        LN_EPS = 1e-05
        SM_EPS = 1e-08
        num_nodes = x.shape[0]
        src, dst = (edge_index[0], edge_index[1])
        h = x @ W_w + W_b
        h_src = h[src]
        h_dst = h[dst]
        logits = h_src @ attn_w[:C] + h_dst @ attn_w[C:] + attn_b
        scores = jax.nn.leaky_relu(logits, negative_slope=0.2)
        delta_t = jnp.float32(current_time) - edge_time
        lam = jax.nn.softplus(decay_rate[0])
        scores = scores * jnp.exp(-lam * delta_t)[:, None]
        smax = jax.ops.segment_max(scores, dst, num_segments=num_nodes)
        e = jnp.exp(scores - smax[dst])
        ssum = jax.ops.segment_sum(e, dst, num_segments=num_nodes)
        attn = e / (ssum[dst] + SM_EPS)
        msg = (h_src[:, :, None] * attn[:, None, :]).reshape(-1, C * H)
        agg = jax.ops.segment_sum(msg, dst, num_segments=num_nodes)
        out = agg @ proj_w + proj_b
        z = out + x
        mu = jnp.mean(z, axis=-1, keepdims=True)
        var = jnp.mean(jnp.square(z - mu), axis=-1, keepdims=True)
        y = ln_g * (z - mu) * jax.lax.rsqrt(var + LN_EPS) + ln_b
        return jax.nn.relu(y)

    def _L2_gnn_ref(x, edge_index, W1, W2, gamma, beta, eps):
        import jax, jax.numpy as jnp
        import numpy as np
        N_NODES = 3125
        N_EDGES = 1250000
        D = 64
        L = 3
        BN_EPS = 1e-05
        src = edge_index[0]
        dst = edge_index[1]
        n = x.shape[0]
        h = x
        for l in range(W1.shape[0]):
            agg = jax.ops.segment_sum(h[src], dst, num_segments=n)
            z = (1.0 + eps[l]) * h + agg
            z = jax.nn.relu(z @ W1[l].T)
            z = jax.nn.relu(z @ W2[l].T)
            mean = jnp.mean(z, axis=0)
            var = jnp.var(z, axis=0)
            h = (z - mean) * jax.lax.rsqrt(var + BN_EPS) * gamma[l] + beta[l]
        return h

    def _L3_gnn_ref(x, edge_index, edge_attr, W_msg1, b_msg1, g_msg, be_msg, W_msg2, b_msg2, W_upd1, b_upd1, g_upd, be_upd, W_upd2, b_upd2):
        import jax, jax.numpy as jnp
        import numpy as np
        N, E = (3125, 25000)
        NODE_DIM, EDGE_DIM, HIDDEN = (64, 32, 128)
        LN_EPS = 1e-05

        def _linear_params(key, fan_in, fan_out):
            kw, kb = jax.random.split(key)
            bound = 1.0 / np.sqrt(fan_in)
            W = jax.random.uniform(kw, (fan_in, fan_out), jnp.float32, -bound, bound)
            b = jax.random.uniform(kb, (fan_out,), jnp.float32, -bound, bound)
            return (W, b)

        def _layer_norm(h, gamma, beta):
            mu = jnp.mean(h, axis=-1, keepdims=True)
            var = jnp.mean(jnp.square(h - mu), axis=-1, keepdims=True)
            return (h - mu) * jax.lax.rsqrt(var + LN_EPS) * gamma + beta

        def _mlp(h, W1, b1, gamma, beta, W2, b2):
            h = h @ W1 + b1
            h = jax.nn.silu(_layer_norm(h, gamma, beta))
            return h @ W2 + b2
        src, dst = (edge_index[0], edge_index[1])
        msg_input = jnp.concatenate([x[src], x[dst], edge_attr], axis=-1)
        msgs = _mlp(msg_input, W_msg1, b_msg1, g_msg, be_msg, W_msg2, b_msg2)
        agg = jax.ops.segment_sum(msgs, dst, num_segments=x.shape[0])
        upd_input = jnp.concatenate([x, agg], axis=-1)
        return x + _mlp(upd_input, W_upd1, b_upd1, g_upd, be_upd, W_upd2, b_upd2)
    edge_index = jnp.stack([src, dst])
    h = jnp.maximum(_layernorm(x, axis=-1), 0.0)
    x = x + _L0_gnn_ref(h, edge_attr_64, edge_attr_9, L0_gnn_Wq, L0_gnn_Cqk, L0_gnn_Cv, L0_gnn_k_w1, L0_gnn_k_b1, L0_gnn_k_w2, L0_gnn_k_b2, L0_gnn_v_w1, L0_gnn_v_b1, L0_gnn_v_w2, L0_gnn_v_b2, L0_gnn_W_out, L0_gnn_W_self, L0_gnn_gamma, L0_gnn_beta, edge_index)
    h = jnp.maximum(_layernorm(x, axis=-1), 0.0)
    x = x + _L1_gnn_ref(h, edge_index, edge_weight, 1, L1_gnn_W_w, L1_gnn_W_b, L1_gnn_attn_w, L1_gnn_attn_b, L1_gnn_decay_rate, L1_gnn_proj_w, L1_gnn_proj_b, L1_gnn_ln_g, L1_gnn_ln_b)
    h = jnp.maximum(_layernorm(x, axis=-1), 0.0)
    x = x + _L2_gnn_ref(h, edge_index, L2_gnn_W1, L2_gnn_W2, L2_gnn_gamma, L2_gnn_beta, L2_gnn_eps)
    h = jnp.maximum(_layernorm(x, axis=-1), 0.0)
    x = x + _L3_gnn_ref(h, edge_index, edge_attr_32, L3_gnn_W_msg1, L3_gnn_b_msg1, L3_gnn_g_msg, L3_gnn_be_msg, L3_gnn_W_msg2, L3_gnn_b_msg2, L3_gnn_W_upd1, L3_gnn_b_upd1, L3_gnn_g_upd, L3_gnn_be_upd, L3_gnn_W_upd2, L3_gnn_b_upd2)
    return x

_drawn_inputs = setup_inputs


def setup_inputs(seed=0):
    import zlib

    import numpy as np

    out = dict(_drawn_inputs(seed))
    spreads = {'L0_gnn_k_b1': (0.0, 0.1),
     'L0_gnn_k_b2': (0.0, 0.1),
     'L0_gnn_v_b1': (0.0, 0.1),
     'L0_gnn_v_b2': (0.0, 0.1),
     'L0_gnn_gamma': (1.0, 0.2),
     'L0_gnn_beta': (0.0, 0.1),
     'L1_gnn_W_b': (0.0, 0.1),
     'L1_gnn_attn_b': (0.0, 0.8),
     'L1_gnn_proj_b': (0.0, 0.1),
     'L1_gnn_ln_g': (1.0, 0.2),
     'L1_gnn_ln_b': (0.0, 0.1),
     'L2_gnn_gamma': (1.0, 0.2),
     'L2_gnn_beta': (0.0, 0.1),
     'L2_gnn_eps': (0.0, 0.491),
     'L3_gnn_g_msg': (1.0, 0.6),
     'L3_gnn_be_msg': (0.0, 0.609),
     'L3_gnn_g_upd': (1.0, 0.6),
     'L3_gnn_be_upd': (0.0, 0.669)}
    factors = {'edge_attr_32': 3.868,
     'edge_weight': 6.656,
     'L3_gnn_b_msg1': 8.63,
     'L3_gnn_b_msg2': 2.918,
     'L3_gnn_b_upd1': 45.444,
     'L3_gnn_b_upd2': 3.423}
    for name, (base, spread) in spreads.items():
        noise = np.random.default_rng([zlib.crc32(name.encode()), seed]).standard_normal(out[name].shape)
        drawn = base * np.exp(spread * noise) if base else spread * noise
        out[name] = jnp.asarray(drawn.astype(out[name].dtype))
    for name, factor in factors.items():
        out[name] = (out[name] * factor).astype(out[name].dtype)
    return out
```

```python
from contextlib import ExitStack

import numpy as np

import concourse.bass as bass
from concourse import mybir

F32 = mybir.dt.float32
I32 = mybir.dt.int32
ALU = mybir.AluOpType
ACT = mybir.ActivationFunctionType
AX_X = mybir.AxisListType.X

P = 128
N, D, E = 3125, 64, 100000
NB = 25
NP = P * NB
PV = N // NB
SC = 512
CH = SC // P
T = 2 * -(-E // (2 * SC))
EP = T * SC
NC_ = EP // P
HALF = EP // 2
T2 = T // 2
HEADS0, DH0 = 8, 16
HEADS1 = 4
S9 = 9
ZPAIRS = (S9 + 1) // 2
W0 = P + HEADS0
W1 = HEADS1 * D + HEADS1
HID = 128
BIG = 1e30
EPS = 1e-5


class Sem:

    def __init__(self, nc, ctx, name):
        self.h = ctx.enter_context(nc.semaphore(name))
        self.base = 0

    def at(self, n):
        return n + self.base

    def passed(self, n):
        self.base += n


def known_ge(t, k):
    return t >= k if isinstance(t, int) else True


def known_lt(t, k):
    return t < k if isinstance(t, int) else True


def run_steps(eng, body, steps, before=0, after=0):
    for t in range(-before, 4):
        body(t, t % 2, t // 2)
    with eng.Fori(2, steps // 2 - 1) as i:
        body(i * 2, 0, i)
        body(i * 2 + 1, 1, i)
    for t in range(steps - 2, steps + after):
        body(t, t % 2, t // 2)


def build(nc, a, out):
    with ExitStack() as top:
        dram = lambda name, shape, dt=F32: nc.dram_tensor(name, shape, dt).ap()
        tab_dup = dram("tab_dup", (NP, 2 * D))
        tab_row = dram("tab_row", (NP, D))
        tab_q = dram("tab_q", (NP, P))
        rows0 = dram("rows0", (EP + 1, W0))
        rows1 = dram("rows1", (EP + 1, W1))
        rows2 = dram("rows2", (HALF + 1, 2 * D))
        rows3 = dram("rows3", (EP + 1, HID))
        reset_add = dram("reset_add", (EP,))
        keep_mul = dram("keep_mul", (EP,))
        decay_row = dram("decay_row", (EP,))

        def sb(ctx, name, shape, dt=F32):
            return ctx.enter_context(nc.sbuf_tensor(name, shape, dt))

        bank = [top.enter_context(nc.psum_tensor(f"bank{i}", [P, 512], F32)) for i in range(8)]

        names = {}

        def S(name):
            if name not in names:
                names[name] = Sem(nc, top, name)
            return names[name]

        ident = sb(top, "ident", [P, P])
        xn = sb(top, "xn", [P, NB, D])
        hn = sb(top, "hn", [P, NB, D])
        tmp_n = sb(top, "tmp_n", [P, NB, P])
        hT = sb(top, "hT", [D, NP])
        last_row = sb(top, "last_row", [P, NB], I32)
        last_row2 = sb(top, "last_row2", [P, NB], I32)
        carry_row2 = sb(top, "carry_row2", [P, NB], I32)
        degree = sb(top, "degree", [P, NB])
        stat = [sb(top, f"stat{i}", [P, NB]) for i in range(4)]
        chain_sem = S("chain")

        def chain(eng, ins):
            ins.then_inc(chain_sem.h, 1)
            chain_sem.passed(1)
            eng.wait_ge(chain_sem.h, chain_sem.base)

        def load_all(pairs):
            sem = S("loaded")
            with nc.Block() as block:
                @block.sync
                def _(sp):
                    for dst, src in pairs:
                        sp.dma_start(dst, src).then_inc(sem.h, 16)
                    sp.wait_ge(sem.h, sem.at(16 * len(pairs)))
            sem.passed(16 * len(pairs))

        def node_rows(d, w):
            return d.rearrange("(p b) w -> p b w", b=NB)[:, :, 0:w] if w != d.shape[1] else d.rearrange("(p b) w -> p b w", b=NB)

        def norm_rows(dve, src, w, dst, scratch, rs_sem, sd_sem):
            s, m, v, r = (t[:] for t in stat)
            chain(dve, nc.vector.reduce_sum(s, src, AX_X))
            chain(dve, nc.vector.tensor_scalar(m, s, 1.0 / w, None, ALU.mult))
            chain(dve, nc.vector.tensor_tensor(dst, src, m.unsqueeze(2).to_broadcast([P, NB, w]), ALU.subtract))
            chain(dve, nc.vector.tensor_tensor(scratch, dst, dst, ALU.mult))
            chain(dve, nc.vector.reduce_sum(s, scratch, AX_X))
            nc.vector.tensor_scalar(v, s, 1.0 / w, EPS, ALU.mult, ALU.add).then_inc(rs_sem.h, 1)
            dve.wait_ge(sd_sem.h, sd_sem.at(1))
            chain(dve, nc.vector.reciprocal(m, r))
            chain(dve, nc.vector.tensor_tensor(dst, dst, m.unsqueeze(2).to_broadcast([P, NB, w]), ALU.mult))

        def root(act, rs_sem, sd_sem, n=P, tiles=(2, 3), w=NB):
            act.wait_ge(rs_sem.h, rs_sem.at(1))
            nc.scalar.activation(stat[tiles[1]][0:n, 0:w], stat[tiles[0]][0:n, 0:w], ACT.Sqrt).then_inc(sd_sem.h, 1)

        def pre_norm():
            rs_sem, sd_sem = S("var_ready"), S("root_ready")
            with nc.Block() as block:
                @block.vector
                def _(dve):
                    norm_rows(dve, xn[:], D, hn[:], tmp_n[:, :, 0:D], rs_sem, sd_sem)
                    nc.vector.tensor_scalar(hn[:], hn[:], 0.0, None, ALU.max)

                @block.scalar
                def _(act):
                    root(act, rs_sem, sd_sem)
            rs_sem.passed(1)
            sd_sem.passed(1)

        def turn(jobs):
            turned, emptied = S("turned"), S("emptied")
            work = []
            for src, dst, w, back in jobs:
                per = 512 // w if back else CH
                for g in range(0, NB, per):
                    work.append((src, dst, w, back, g, min(per, NB - g)))
            with nc.Block() as block:
                @block.tensor
                def _(pe):
                    for k, (src, dst, w, back, g, n) in enumerate(work):
                        if k >= 2:
                            pe.wait_ge(emptied.h, emptied.at(k - 1))
                        for j in range(n):
                            if back:
                                mm = nc.tensor.transpose(bank[k % 2][:, j * w:(j + 1) * w],
                                                         src[:, (g + j) * P:(g + j + 1) * P], ident[0:w, 0:w])
                            else:
                                mm = nc.tensor.transpose(bank[k % 2][0:w, j * P:(j + 1) * P],
                                                         src[:, g + j, :], ident[:])
                        mm.then_inc(turned.h, 1)

                @block.scalar
                def _(act):
                    for k, (src, dst, w, back, g, n) in enumerate(work):
                        act.wait_ge(turned.h, turned.at(k + 1))
                        if back:
                            o, i = dst[:, g:g + n, :], bank[k % 2][:, 0:n * w].rearrange("p (b w) -> p b w", w=w)
                        else:
                            o, i = dst[:, g * P:(g + n) * P], bank[k % 2][0:w, 0:n * P]
                        nc.scalar.activation(o, i, ACT.Copy).then_inc(emptied.h, 1)
            turned.passed(len(work))
            emptied.passed(len(work))

        def product_T(terms, m, dst, func=ACT.Copy):
            made, emptied = S("turned"), S("emptied")
            cuts = [(c, min(512, NP - c)) for c in range(0, NP, 512)]
            with nc.Block() as block:
                @block.tensor
                def _(pe):
                    for k, (c, n) in enumerate(cuts):
                        if k >= 2:
                            pe.wait_ge(emptied.h, emptied.at(k - 1))
                        for j, (lhsT, rhs) in enumerate(terms):
                            mm = nc.tensor.matmul(bank[k % 2][0:m, 0:n], lhsT, rhs[:, c:c + n],
                                                  start=(j == 0), stop=(j == len(terms) - 1))
                        mm.then_inc(made.h, 1)

                @block.scalar
                def _(act):
                    for k, (c, n) in enumerate(cuts):
                        act.wait_ge(made.h, made.at(k + 1))
                        nc.scalar.activation(dst[:, c:c + n], bank[k % 2][0:m, 0:n], func).then_inc(emptied.h, 1)
            made.passed(len(cuts))
            emptied.passed(len(cuts))

        def product_rows(terms, w, dst, bias=None):
            made, emptied = S("turned"), S("emptied")
            per = 512 // w
            cuts = [(g, min(per, NB - g)) for g in range(0, NB, per)]
            with nc.Block() as block:
                @block.tensor
                def _(pe):
                    for k, (g, n) in enumerate(cuts):
                        if k >= 2:
                            pe.wait_ge(emptied.h, emptied.at(k - 1))
                        for b in range(n):
                            for j, (tform, weights) in enumerate(terms):
                                mm = nc.tensor.matmul(bank[k % 2][:, b * w:(b + 1) * w],
                                                      tform[:, (g + b) * P:(g + b + 1) * P], weights,
                                                      start=(j == 0), stop=(j == len(terms) - 1))
                        mm.then_inc(made.h, 1)

                @block.vector
                def _(dve):
                    for k, (g, n) in enumerate(cuts):
                        dve.wait_ge(made.h, made.at(k + 1))
                        i = bank[k % 2][:, 0:n * w].rearrange("p (b w) -> p b w", w=w)
                        if bias is None:
                            nc.vector.tensor_copy(dst[:, g:g + n, :], i).then_inc(emptied.h, 1)
                        else:
                            nc.vector.tensor_tensor(dst[:, g:g + n, :], i,
                                                    bias.unsqueeze(1).to_broadcast([P, n, w]),
                                                    ALU.add).then_inc(emptied.h, 1)
            made.passed(len(cuts))
            emptied.passed(len(cuts))

        def store_tables(pairs):
            sem = S("loaded")
            with nc.Block() as block:
                @block.sync
                def _(sp):
                    for dst, src in pairs:
                        sp.dma_start(dst, src).then_inc(sem.h, 16)
                    sp.wait_ge(sem.h, sem.at(16 * len(pairs)))
            sem.passed(16 * len(pairs))

        def read_rows(jobs):
            sem = S("rows_read")
            with nc.Block() as block:
                @block.gpsimd
                def _(pool):
                    for table, index, dst in jobs:
                        for b in range(NB):
                            nc.gpsimd.indirect_dma_start(
                                out=dst[:, b, :], out_offset=None, in_=table,
                                in_offset=bass.IndirectOffsetOnAxis(ap=index[:, b:b + 1], axis=0),
                            ).then_inc(sem.h, 16)
                    pool.wait_ge(sem.h, sem.at(16 * NB * len(jobs)))
            sem.passed(16 * NB * len(jobs))

        def batch_norm(vT, gamma, beta, dst, scratch):
            rs_sem, sd_sem = S("var_ready"), S("root_ready")
            real = lambda t: t.rearrange("d (b p) -> d b p", p=P)[:, :, 0:PV]
            s, m, v, r = (t[0:D, 0:1] for t in stat)
            part = stat[0][0:D, 0:NB]
            with nc.Block() as block:
                @block.vector
                def _(dve):
                    chain(dve, nc.vector.reduce_sum(part, real(vT), AX_X))
                    chain(dve, nc.vector.reduce_sum(m, part, AX_X))
                    chain(dve, nc.vector.tensor_scalar(m, m, 1.0 / N, None, ALU.mult))
                    chain(dve, nc.vector.tensor_scalar(dst, vT, m, None, ALU.subtract))
                    chain(dve, nc.vector.tensor_tensor(scratch, dst, dst, ALU.mult))
                    chain(dve, nc.vector.reduce_sum(part, real(scratch), AX_X))
                    chain(dve, nc.vector.reduce_sum(m, part, AX_X))
                    nc.vector.tensor_scalar(v, m, 1.0 / N, EPS, ALU.mult, ALU.add).then_inc(rs_sem.h, 1)
                    dve.wait_ge(sd_sem.h, sd_sem.at(1))
                    chain(dve, nc.vector.reciprocal(m, r))
                    chain(dve, nc.vector.tensor_tensor(m, m, gamma, ALU.mult))
                    nc.vector.tensor_scalar(dst, dst, m, beta, ALU.mult, ALU.add)

                @block.scalar
                def _(act):
                    root(act, rs_sem, sd_sem, n=D, w=1)
            rs_sem.passed(1)
            sd_sem.passed(1)

        def prepare():
            with ExitStack() as ctx:
                dst_f = sb(ctx, "dst_f", [P, NC_])
                d_now = sb(ctx, "d_now", [P, NC_], I32)
                d_bef = sb(ctx, "d_bef", [P, NC_], I32)
                same = sb(ctx, "same", [P, NC_])
                reset = sb(ctx, "reset", [P, NC_])
                ew = sb(ctx, "ew", [P, NC_])
                chunk_last = sb(ctx, "chunk_last", [P, NC_], I32)
                rate = sb(ctx, "rate", [P, 1])
                zero = sb(ctx, "zero", [1, W1])
                node_i = sb(ctx, "node_i", [P, NB], I32)
                bound = sb(ctx, "bound", [P, 2, NB])
                before = sb(ctx, "before", [P, 2, NB])
                before_i = sb(ctx, "before_i", [P, 2, NB], I32)
                rows = sb(ctx, "rows", [P, 2 * NB, P], I32)
                inside = sb(ctx, "inside", [P, 2, NB])
                edge = sb(ctx, "edge", [P, 2, NB])
                flag = sb(ctx, "flag", [P, NB])
                flag2 = sb(ctx, "flag2", [P, NB])
                k1 = sb(ctx, "k1", [P, NB])
                junk = sb(ctx, "junk", [P, NC_])
                load_all([(ident[:], a["ident"]), (xn[:], node_rows(a["x"], D)),
                          (d_now[:], a["dst_now"]), (d_bef[:], a["dst_before"]),
                          (ew[:], a["edge_weight"]), (chunk_last[:], a["chunk_last"].partition_broadcast(P)),
                          (rate[:], a["decay_rate"].partition_broadcast(P))])
                made, expd, rd = S("var_ready"), S("root_ready"), S("rows_read")
                sent, counted, iota = S("loaded"), S("counted"), S("iota_ready")
                with nc.Block() as block:
                    @block.gpsimd
                    def _(pool):
                        nc.gpsimd.iota(node_i[:], pattern=[[1, NB]], base=0,
                                       channel_multiplier=NB).then_inc(iota.h, 1)
                        pool.wait_ge(counted.h, counted.at(1))
                        for j in range(2 * NB):
                            nc.gpsimd.indirect_dma_start(
                                out=rows[:, j, :], out_offset=None, in_=a["dst_rows"],
                                in_offset=bass.IndirectOffsetOnAxis(ap=before_i[:, j // NB, j % NB:j % NB + 1], axis=0),
                            ).then_inc(rd.h, 16)

                    @block.vector
                    def _(dve):
                        chain(dve, nc.vector.tensor_copy(dst_f[:], d_now[:]))
                        chain(dve, nc.vector.tensor_copy(reset[:], d_bef[:]))
                        chain(dve, nc.vector.tensor_tensor(same[:], dst_f[:], reset[:], ALU.is_equal))
                        chain(dve, nc.vector.tensor_scalar(reset[:], same[:], -1.0, BIG, ALU.add, ALU.mult))
                        chain(dve, nc.vector.memset(zero[:], 0.0))
                        chain(dve, nc.vector.tensor_scalar(stat[0][:, 0:1], rate[:], -1.0, None, ALU.mult))
                        chain(dve, nc.vector.tensor_tensor(stat[0][:, 0:1], stat[0][:, 0:1], rate[:], ALU.max))
                        nc.vector.tensor_scalar(rate[:], rate[:], 0.0, None, ALU.max).then_inc(made.h, 1)
                        dve.wait_ge(iota.h, iota.at(1))
                        chain(dve, nc.vector.tensor_copy(bound[:, 0, :], node_i[:]))
                        chain(dve, nc.vector.tensor_scalar(bound[:, 1, :], bound[:, 0, :], 1.0, None, ALU.add))
                        chain(dve, nc.vector.tensor_copy(dst_f[:], chunk_last[:]))
                        for k in range(2):
                            for b in range(NB):
                                chain(dve, nc.vector.tensor_scalar(junk[:], dst_f[:], bound[:, k, b:b + 1], 0.0,
                                                                   ALU.is_lt, ALU.add,
                                                                   accum_out=before[:, k, b:b + 1]))
                        nc.vector.tensor_copy(before_i[:], before[:]).then_inc(counted.h, 1)
                        dve.wait_ge(expd.h, expd.at(2))
                        chain(dve, nc.vector.tensor_tensor(rate[:], rate[:], stat[1][:, 0:1], ALU.add))
                        nc.vector.tensor_scalar(ew[:], ew[:], -1.0, rate[:, 0:1], ALU.add, ALU.mult).then_inc(made.h, 1)
                        dve.wait_ge(rd.h, rd.at(32 * NB))
                        for k in range(2):
                            for b in range(NB):
                                chain(dve, nc.vector.tensor_copy(junk[:, 0:P], rows[:, k * NB + b, :]))
                                chain(dve, nc.vector.tensor_scalar(junk[:, P:2 * P], junk[:, 0:P], bound[:, k, b:b + 1], 0.0,
                                                                   ALU.is_lt, ALU.add,
                                                                   accum_out=inside[:, k, b:b + 1]))
                        chain(dve, nc.vector.tensor_scalar(edge[:], before[:], float(P), None, ALU.mult))
                        chain(dve, nc.vector.tensor_tensor(edge[:], edge[:], inside[:], ALU.add))
                        chain(dve, nc.vector.tensor_tensor(degree[:], edge[:, 1, :], edge[:, 0, :], ALU.subtract))
                        chain(dve, nc.vector.tensor_scalar(flag[:], degree[:], 1.0, None, ALU.min))
                        chain(dve, nc.vector.tensor_scalar(k1[:], edge[:, 1, :], float(-1 - EP), None, ALU.add))
                        chain(dve, nc.vector.tensor_tensor(k1[:], k1[:], flag[:], ALU.mult))
                        chain(dve, nc.vector.tensor_scalar(k1[:], k1[:], float(EP), None, ALU.add))
                        chain(dve, nc.vector.tensor_copy(last_row[:], k1[:]))
                        chain(dve, nc.vector.tensor_scalar(flag2[:], k1[:], float(HALF), None, ALU.is_ge))
                        chain(dve, nc.vector.tensor_tensor(flag2[:], flag2[:], flag[:], ALU.mult))
                        chain(dve, nc.vector.tensor_scalar(k1[:], edge[:, 1, :], 2.0, float(-2 - EP), ALU.mult, ALU.add))
                        chain(dve, nc.vector.tensor_tensor(k1[:], k1[:], flag[:], ALU.mult))
                        chain(dve, nc.vector.tensor_scalar(junk[:, 0:NB], flag2[:], float(1 - 2 * HALF), float(EP), ALU.mult, ALU.add))
                        chain(dve, nc.vector.tensor_tensor(k1[:], k1[:], junk[:, 0:NB], ALU.add))
                        chain(dve, nc.vector.tensor_copy(last_row2[:], k1[:]))
                        chain(dve, nc.vector.tensor_scalar(flag[:], edge[:, 0, :], float(HALF), None, ALU.is_lt))
                        chain(dve, nc.vector.tensor_tensor(flag[:], flag[:], flag2[:], ALU.mult))
                        chain(dve, nc.vector.tensor_scalar(k1[:], flag[:], -2.0, float(EP), ALU.mult, ALU.add))
                        chain(dve, nc.vector.tensor_copy(carry_row2[:], k1[:]))

                    @block.scalar
                    def _(act):
                        act.wait_ge(made.h, made.at(1))
                        nc.scalar.activation(stat[2][:, 0:1], stat[0][:, 0:1], ACT.Exp, scale=-1.0).then_inc(expd.h, 1)
                        act.wait_ge(expd.h, expd.at(1))
                        nc.scalar.activation(stat[1][:, 0:1], stat[2][:, 0:1], ACT.Ln, bias=1.0).then_inc(expd.h, 1)
                        act.wait_ge(made.h, made.at(2))
                        nc.scalar.activation(ew[:], ew[:], ACT.Exp).then_inc(expd.h, 1)

                    @block.sync
                    def _(sp):
                        sp.wait_ge(made.h, made.at(1))
                        row = lambda d: d.rearrange("(p c) -> p c", c=NC_)
                        sp.dma_start(row(keep_mul), same[:]).then_inc(sent.h, 16)
                        sp.dma_start(row(reset_add), reset[:]).then_inc(sent.h, 16)
                        sp.dma_start(rows0[EP:EP + 1, :], zero[:, 0:W0]).then_inc(sent.h, 16)
                        sp.dma_start(rows1[EP:EP + 1, :], zero[:, 0:W1]).then_inc(sent.h, 16)
                        sp.dma_start(rows2[HALF:HALF + 1, :], zero[:, 0:2 * D]).then_inc(sent.h, 16)
                        sp.dma_start(rows3[EP:EP + 1, :], zero[:, 0:HID]).then_inc(sent.h, 16)
                        sp.wait_ge(expd.h, expd.at(3))
                        sp.dma_start(row(decay_row), ew[:]).then_inc(sent.h, 16)
                        sp.wait_ge(sent.h, sent.at(16 * 7))
                made.passed(2)
                expd.passed(3)
                rd.passed(32 * NB)
                sent.passed(16 * 7)
                counted.passed(1)
                iota.passed(1)

        def gather_step(pool, t, par, i, what, steps, idx_in, slots_free, gathered):
            if not (known_ge(t, 0) and known_lt(t, steps)):
                return
            pool.wait_ge(idx_in[par].h, idx_in[par].at((i + 1) * 16))
            if known_ge(t, 2):
                for sem in slots_free:
                    pool.wait_ge(sem.h, sem.at(t - 1))
            nc.gpsimd.sem_inc(S("pool_turn").h, 1)
            for dst, table, index in what(par):
                nc.gpsimd.indirect_dma_start(out=dst, out_offset=None, in_=table,
                                             in_offset=bass.IndirectOffsetOnAxis(ap=index, axis=0)
                                             ).then_inc(gathered[par].h, 16)

        def edges(d, t):
            return d[bass.ds(t * SC, SC)]

        def layer0_edges():
            with ExitStack() as ctx:
                ck = sb(ctx, "ck", [P, ZPAIRS, P])
                cv = sb(ctx, "cv", [P, ZPAIRS, P])
                w1 = sb(ctx, "w1", [D, 2 * D])
                b1 = sb(ctx, "b1", [P, 1])
                w2 = sb(ctx, "w2", [P, P])
                b2 = sb(ctx, "b2", [P, 2])
                headsum = sb(ctx, "headsum", [P, P])
                pick = sb(ctx, "pick", [P, HEADS0])
                idx = sb(ctx, "idx", [P, 2, 2 * CH], I32)
                gx = sb(ctx, "gx", [P, 2, CH, 2 * D])
                gq = sb(ctx, "gq", [P, 2, CH, P])
                ef = sb(ctx, "ef", [D, 2, SC])
                sh = sb(ctx, "sh", [P, 2, ZPAIRS, SC])
                z = sb(ctx, "z", [P, 2, ZPAIRS, SC])
                rst = sb(ctx, "rst", [P, 2, SC])
                hid = sb(ctx, "hid", [P, 2, SC])
                wk = sb(ctx, "wk", [P, SC])
                wv = sb(ctx, "wv", [P, SC])
                kw = sb(ctx, "kw", [P, SC])
                qk = sb(ctx, "qk", [P, SC])
                val = sb(ctx, "val", [P, 2, SC])
                mx = sb(ctx, "mx", [P, 2, SC + 1])
                arg = sb(ctx, "arg", [P, 2, 2 * SC])
                pd = sb(ctx, "pd", [P, 2, 2 * SC])
                pv = sb(ctx, "pv", [P, SC])
                num = sb(ctx, "num", [P, 2, SC])
                den = sb(ctx, "den", [P, 2, SC])
                o = sb(ctx, "o", [P, 2, CH, W0])
                pairs = [(ck[0:D, j, :], a["Cqk"][2 * j]) for j in range(ZPAIRS)]
                pairs += [(ck[D:P, j, :], a["Cqk"][2 * j + 1]) for j in range(ZPAIRS - 1)]
                pairs += [(cv[0:D, j, :], a["Cv"][2 * j]) for j in range(ZPAIRS)]
                pairs += [(cv[D:P, j, :], a["Cv"][2 * j + 1]) for j in range(ZPAIRS - 1)]
                pairs += [(w1[:, 0:D], a["k_w1"]), (w1[:, D:2 * D], a["v_w1"]), (b1[0:D, :], a["k_b1"]),
                          (b1[D:P, :], a["v_b1"]), (w2[0:D, :], a["k_w2"]), (w2[D:P, :], a["v_w2"]),
                          (b2[:, 0:1], a["k_b2"]), (b2[:, 1:2], a["v_b2"]),
                          (headsum[:], a["headsum"]), (pick[:], a["pick0"])]
                load_all(pairs)
                bX, bQ, bH, bW, bK, bV, bS, bO = bank
                idx_in, ef_in, sh_in, rst_in = ([S(f"{n}{j}") for j in range(2)] for n in ("idx_in", "feat_in", "sh_in", "rst_in"))
                gathered, stored = ([S(f"{n}{j}") for j in range(2)] for n in ("gathered", "stored"))
                xT, qT, h_ps, hid_ok, wk_ps, wk_ok, wv_ps, wv_ok = (S(n) for n in (
                    "xT", "qT", "h_ps", "hid_ok", "wk_ps", "wk_ok", "wv_ps", "wv_ok"))
                z_ok, k_ps, v_ps, kw_ok, qk_ok, s_ps, mx_ok, arg_ok = (S(n) for n in (
                    "z_ok", "k_ps", "v_ps", "kw_ok", "qk_ok", "s_ps", "mx_ok", "arg_ok"))
                pd_ok, val_ok, pv_ok, scanned, o_ps, o_ok, tmp_ok, sub_ok = (S(n) for n in (
                    "pd_ok", "val_ok", "pv_ok", "scanned", "o_ps", "o_ok", "tmp_ok", "sub_ok"))

                def gathers(par):
                    for j in range(CH):
                        yield gx[:, par, j, :], tab_dup, idx[:, par, j:j + 1]
                    for j in range(CH):
                        yield gq[:, par, j, :], tab_q, idx[:, par, CH + j:CH + j + 1]

                with nc.Block() as block:
                    @block.sync
                    def _(sp):
                        def body(t, par, i):
                            if known_lt(t, T):
                                if known_ge(t, 2):
                                    sp.wait_ge(gathered[par].h, gathered[par].at(i * (16 * 2 * CH)))
                                sp.dma_start(idx[:, par, :], a["idx"][bass.ds(t, 1)].rearrange("t p j -> p (t j)")).then_inc(idx_in[par].h, 16)
                                if known_ge(t, 2):
                                    sp.wait_ge(h_ps.h, h_ps.at(t - 1))
                                sp.dma_start(ef[:, par, :], a["ef"][:, bass.ds(t * SC, SC)]).then_inc(ef_in[par].h, 16)
                                if known_ge(t, 2):
                                    sp.wait_ge(z_ok.h, z_ok.at(t - 1))
                                sp.dma_start(sh[0:D, par, :, :], a["sh"][0:S9:2, bass.ds(t * SC, SC)].partition_broadcast(D)).then_inc(sh_in[par].h, 16)
                                sp.dma_start(sh[D:P, par, 0:ZPAIRS - 1, :], a["sh"][1:S9:2, bass.ds(t * SC, SC)].partition_broadcast(D)).then_inc(sh_in[par].h, 16)
                                if known_ge(t, 2):
                                    sp.wait_ge(arg_ok.h, arg_ok.at(t - 1))
                                sp.dma_start(rst[:, par, :], edges(reset_add, t).partition_broadcast(P)).then_inc(rst_in[par].h, 16)
                            if known_ge(t, 3):
                                u = t - 3
                                sp.wait_ge(o_ok.h, o_ok.at(u + 1))
                                sp.dma_start(rows0[bass.ds(u * SC, SC), :].rearrange("(c p) w -> p c w", p=P),
                                             o[:, 1 - par, :, :]).then_inc(stored[1 - par].h, 16)
                        run_steps(sp, body, T, after=3)
                        for j in range(2):
                            sp.wait_ge(stored[j].h, stored[j].at(16 * T2))

                    @block.gpsimd
                    def _(pool):
                        run_steps(pool, lambda t, par, i: gather_step(pool, t, par, i, gathers, T, idx_in, (xT, qT), gathered), T)

                    @block.tensor
                    def _(pe):
                        def heads_in(t, par, i):
                            pe.wait_ge(ef_in[par].h, ef_in[par].at((i + 1) * 16))
                            if known_ge(t, 1):
                                pe.wait_ge(hid_ok.h, hid_ok.at(t))
                            nc.tensor.matmul(bH[:], w1[:], ef[:, par, :], start=True, stop=True).then_inc(h_ps.h, 1)
                            pe.wait_ge(gathered[par].h, gathered[par].at((i + 1) * (16 * 2 * CH)))
                            if known_ge(t, 1):
                                pe.wait_ge(z_ok.h, z_ok.at(t))
                            for c in range(CH):
                                mm = nc.tensor.transpose(bX[:, c * P:(c + 1) * P], gx[:, par, c, :], ident[:])
                            mm.then_inc(xT.h, 1)

                        def queries_in(t, par, i):
                            if known_ge(t, 1):
                                pe.wait_ge(qk_ok.h, qk_ok.at(t))
                            for c in range(CH):
                                mm = nc.tensor.transpose(bQ[:, c * P:(c + 1) * P], gq[:, par, c, :], ident[:])
                            mm.then_inc(qT.h, 1)

                        def contract(bankx, coef, par, done):
                            for j in range(ZPAIRS):
                                n = P if j < ZPAIRS - 1 else D
                                mm = nc.tensor.matmul(bankx[:], coef[0:n, j, :], z[0:n, par, j, :],
                                                      start=(j == 0), stop=(j == ZPAIRS - 1))
                            mm.then_inc(done.h, 1)

                        def body(t, par, i):
                            nxt = (t + 1, 1 - par, i + par)
                            mid = known_ge(t, 0) and known_lt(t, T)
                            if mid:
                                pe.wait_ge(hid_ok.h, hid_ok.at(t + 1))
                                if isinstance(t, int) and t == 1:
                                    pe.wait_ge(wv_ok.h, wv_ok.at(1))
                                if known_ge(t, 2):
                                    pe.wait_ge(o_ok.h, o_ok.at(t - 1))
                                nc.tensor.matmul(bW[:], w2[0:D, :], hid[0:D, par, :], start=True, stop=True).then_inc(wk_ps.h, 1)
                            if known_lt(t, T - 1):
                                heads_in(*nxt)
                            if mid:
                                pe.wait_ge(wk_ok.h, wk_ok.at(t + 1))
                                nc.tensor.matmul(bW[:], w2[D:P, :], hid[D:P, par, :], start=True, stop=True).then_inc(wv_ps.h, 1)
                                pe.wait_ge(z_ok.h, z_ok.at(t + 1))
                                if known_ge(t, 1):
                                    pe.wait_ge(kw_ok.h, kw_ok.at(t))
                                contract(bK, ck, par, k_ps)
                                if known_ge(t, 1):
                                    pe.wait_ge(val_ok.h, val_ok.at(t))
                                contract(bV, cv, par, v_ps)
                                pe.wait_ge(qk_ok.h, qk_ok.at(t + 1))
                                if known_ge(t, 1):
                                    pe.wait_ge(arg_ok.h, arg_ok.at(t))
                                nc.tensor.matmul(bS[:], headsum[:], qk[:], start=True, stop=True).then_inc(s_ps.h, 1)
                            if known_ge(t, 1):
                                pe.wait_ge(scanned.h, scanned.at(2 * t))
                                if known_ge(t, 2):
                                    pe.wait_ge(o_ok.h, o_ok.at(t - 1))
                                if mid:
                                    pe.wait_ge(wv_ok.h, wv_ok.at(t + 1))
                                for c in range(CH):
                                    nc.tensor.transpose(bO[:, c * P:(c + 1) * P], num[:, 1 - par, c * P:(c + 1) * P], ident[:])
                                for c in range(CH):
                                    mm = nc.tensor.matmul(bW[:, c * HEADS0:(c + 1) * HEADS0], den[:, 1 - par, c * P:(c + 1) * P],
                                                          pick[:], start=True, stop=True)
                                mm.then_inc(o_ps.h, 1)
                            if known_lt(t, T - 1):
                                queries_in(*nxt)
                        run_steps(pe, body, T, before=1, after=1)

                    @block.scalar
                    def _(act):
                        def body(t, par, i):
                            mid = known_ge(t, 0) and known_lt(t, T)
                            if mid:
                                act.wait_ge(wk_ps.h, wk_ps.at(t + 1))
                                if known_ge(t, 1):
                                    act.wait_ge(kw_ok.h, kw_ok.at(t))
                                nc.scalar.activation(wk[:], bW[:], ACT.Identity, bias=b2[:, 0:1]).then_inc(wk_ok.h, 1)
                            if known_lt(t, T - 1):
                                act.wait_ge(h_ps.h, h_ps.at(t + 2))
                                if known_ge(t, 1):
                                    act.wait_ge(wv_ps.h, wv_ps.at(t))
                                nc.scalar.activation(hid[:, 1 - par, :], bH[:], ACT.Relu, bias=b1[:]).then_inc(hid_ok.h, 1)
                            if mid:
                                act.wait_ge(wv_ps.h, wv_ps.at(t + 1))
                                if known_ge(t, 1):
                                    act.wait_ge(val_ok.h, val_ok.at(t))
                                nc.scalar.activation(wv[:], bW[:], ACT.Identity, bias=b2[:, 1:2]).then_inc(wv_ok.h, 1)
                            if known_ge(t, 1):
                                act.wait_ge(o_ps.h, o_ps.at(t))
                                if known_ge(t, 3):
                                    act.wait_ge(stored[1 - par].h, stored[1 - par].at((i - 1 + par) * 16))
                                nc.scalar.activation(o[:, 1 - par, :, 0:P], bO[:].rearrange("p (c w) -> p c w", w=P), ACT.Copy)
                                nc.scalar.activation(o[:, 1 - par, :, P:W0], bW[:, 0:CH * HEADS0].rearrange("p (c w) -> p c w", w=HEADS0),
                                                     ACT.Copy).then_inc(o_ok.h, 1)
                            if mid:
                                act.wait_ge(arg_ok.h, arg_ok.at(t + 1))
                                if known_ge(t, 2):
                                    act.wait_ge(scanned.h, scanned.at(2 * (t - 1)))
                                nc.scalar.activation(pd[:, par, :], arg[:, par, :], ACT.Exp).then_inc(pd_ok.h, 1)
                        run_steps(act, body, T, before=1, after=1)

                    @block.vector
                    def _(dve):
                        nc.vector.memset(mx[:, 1, :], -BIG).then_inc(tmp_ok.h, 1)
                        nc.vector.memset(num[:, 1, :], 0.0).then_inc(tmp_ok.h, 1)
                        nc.vector.memset(den[:, 1, :], 0.0).then_inc(tmp_ok.h, 1)
                        dve.wait_ge(tmp_ok.h, tmp_ok.at(3))
                        tmp_ok.passed(3)

                        def body(t, par, i):
                            old = 1 - par
                            mid = known_ge(t, 0) and known_lt(t, T)
                            if known_lt(t, T - 1):
                                dve.wait_ge(xT.h, xT.at(t + 2))
                                dve.wait_ge(sh_in[old].h, sh_in[old].at((i + par + 1) * 32))
                                if known_ge(t, 1):
                                    dve.wait_ge(v_ps.h, v_ps.at(t))
                                nc.vector.tensor_tensor(z[:, old, 0:ZPAIRS - 1, :], bX[:].unsqueeze(1).to_broadcast([P, ZPAIRS - 1, SC]),
                                                        sh[:, old, 0:ZPAIRS - 1, :], ALU.mult)
                                nc.vector.tensor_tensor(z[0:D, old, ZPAIRS - 1, :], bX[0:D, :], sh[0:D, old, ZPAIRS - 1, :],
                                                        ALU.mult).then_inc(z_ok.h, 1)
                            if mid:
                                dve.wait_ge(k_ps.h, k_ps.at(t + 1))
                                dve.wait_ge(wk_ok.h, wk_ok.at(t + 1))
                                nc.vector.tensor_tensor(kw[:], wk[:], bK[:], ALU.mult).then_inc(kw_ok.h, 1)
                                dve.wait_ge(kw_ok.h, kw_ok.at(t + 1))
                                dve.wait_ge(qT.h, qT.at(t + 1))
                                if known_ge(t, 1):
                                    dve.wait_ge(s_ps.h, s_ps.at(t))
                                nc.vector.tensor_tensor(qk[:], kw[:], bQ[:], ALU.mult).then_inc(qk_ok.h, 1)
                            if known_ge(t, 1):
                                dve.wait_ge(pd_ok.h, pd_ok.at(t))
                                nc.vector.tensor_tensor(pv[:], pd[:, old, 0:SC], val[:, old, :], ALU.mult).then_inc(pv_ok.h, 1)
                                if known_ge(t, 3):
                                    dve.wait_ge(o_ps.h, o_ps.at(t - 2))
                                nc.vector.tensor_tensor_scan(den[:, old, :], pd[:, old, SC:2 * SC], pd[:, old, 0:SC],
                                                             den[:, par, SC - 1:SC], ALU.mult, ALU.add).then_inc(scanned.h, 1)
                                dve.wait_ge(pv_ok.h, pv_ok.at(t))
                                nc.vector.tensor_tensor_scan(num[:, old, :], pd[:, old, SC:2 * SC], pv[:],
                                                             num[:, par, SC - 1:SC], ALU.mult, ALU.add).then_inc(scanned.h, 1)
                            if mid:
                                dve.wait_ge(v_ps.h, v_ps.at(t + 1))
                                dve.wait_ge(wv_ok.h, wv_ok.at(t + 1))
                                nc.vector.tensor_tensor(val[:, par, :], wv[:], bV[:], ALU.mult).then_inc(val_ok.h, 1)
                                dve.wait_ge(s_ps.h, s_ps.at(t + 1))
                                dve.wait_ge(rst_in[par].h, rst_in[par].at((i + 1) * 16))
                                nc.vector.tensor_copy(mx[:, par, 0:1], mx[:, old, SC:SC + 1])
                                nc.vector.tensor_tensor_scan(mx[:, par, 1:SC + 1], rst[:, par, :], bS[:],
                                                             mx[:, old, SC:SC + 1], ALU.add, ALU.max).then_inc(mx_ok.h, 1)
                                dve.wait_ge(mx_ok.h, mx_ok.at(t + 1))
                                nc.vector.tensor_tensor(arg[:, par, SC:2 * SC], mx[:, par, 0:SC], rst[:, par, :], ALU.add).then_inc(sub_ok.h, 1)
                                nc.vector.tensor_tensor(arg[:, par, 0:SC], bS[:], mx[:, par, 1:SC + 1], ALU.subtract)
                                dve.wait_ge(sub_ok.h, sub_ok.at(t + 1))
                                nc.vector.tensor_tensor(arg[:, par, SC:2 * SC], arg[:, par, SC:2 * SC], mx[:, par, 1:SC + 1],
                                                        ALU.subtract).then_inc(arg_ok.h, 1)
                        run_steps(dve, body, T, before=1, after=1)
                for j in range(2):
                    for s, n in ((idx_in, 16), (ef_in, 16), (sh_in, 32), (rst_in, 16), (gathered, 32 * CH), (stored, 16)):
                        s[j].passed(n * T2)
                for s in (xT, qT, h_ps, hid_ok, wk_ps, wk_ok, wv_ps, wv_ok, z_ok, k_ps, v_ps, kw_ok, qk_ok, s_ps,
                          mx_ok, arg_ok, pd_ok, val_ok, pv_ok, o_ps, o_ok, sub_ok):
                    s.passed(T)
                scanned.passed(2 * T)

        def layer1_edges():
            with ExitStack() as ctx:
                aw = sb(ctx, "aw", [P, HEADS1])
                lw = sb(ctx, "lw", [P, 2, P])
                ab = sb(ctx, "ab", [P, 2])
                pick = sb(ctx, "pick1", [P, 2])
                idx = sb(ctx, "idx1", [P, 2, 2 * CH], I32)
                gx = sb(ctx, "gx1", [P, 2, CH, 3 * D])
                pair = sb(ctx, "pair1", [P, 2, SC])
                xs = sb(ctx, "xs1", [P, 2, SC])
                rst = sb(ctx, "rst1", [P, 2, SC])
                dec = sb(ctx, "dec1", [P, 2, SC])
                lr = sb(ctx, "lr1", [P, 2, SC])
                sc = sb(ctx, "sc1", [P, 2, SC])
                mx = sb(ctx, "mx1", [P, 2, 2, SC + 1])
                arg = sb(ctx, "arg1", [P, 2, 2, 2 * SC])
                pd = sb(ctx, "pd1", [P, 2, 2, 2 * SC])
                pv = sb(ctx, "pv1", [P, 2, SC])
                num = sb(ctx, "num1", [P, 2, 2, SC])
                den = sb(ctx, "den1", [P, 2, 2, SC])
                o = sb(ctx, "o1", [P, 2, CH, W1])
                load_all([(aw[0:D, :], a["attn_w"][D:2 * D, :]), (aw[D:P, :], a["attn_w"][0:D, :]), (pick[:], a["pick1"])]
                         + [(ab[D * k:D * (k + 1), g:g + 1], a["attn_b"][2 * g + k:2 * g + k + 1].partition_broadcast(D))
                            for g in range(2) for k in range(2)])
                bA, bX, bL0, bL1, bO0, bO1, bD, _ = bank
                idx_in, rst_in, dec_in, gathered, stored = ([S(f"{n}{j}") for j in range(2)] for n in (
                    "idx_in", "rst_in", "feat_in", "gathered", "stored"))
                aT, xT, pair_ok, xs_ok, l_ps, lr_ok, sc_ok, mx_ok, sub_ok, arg_ok = (S(n) for n in (
                    "qT", "xT", "hid_ok", "wk_ok", "s_ps", "wv_ok", "kw_ok", "mx_ok", "sub_ok", "arg_ok"))
                pd_ok, pv_ok, scanned, o_ps, o_ok, tmp_ok = (S(n) for n in ("pd_ok", "pv_ok", "scanned", "o_ps", "o_ok", "tmp_ok"))

                def gathers(par):
                    for j in range(CH):
                        yield gx[:, par, j, D:3 * D], tab_dup, idx[:, par, j:j + 1]
                    for j in range(CH):
                        yield gx[:, par, j, 0:D], tab_row, idx[:, par, CH + j:CH + j + 1]

                with nc.Block() as block:
                    @block.sync
                    def _(sp):
                        def body(t, par, i):
                            if known_lt(t, T):
                                if known_ge(t, 2):
                                    sp.wait_ge(gathered[par].h, gathered[par].at(i * (32 * CH)))
                                sp.dma_start(idx[:, par, :], a["idx"][bass.ds(t, 1)].rearrange("t p j -> p (t j)")).then_inc(idx_in[par].h, 16)
                                if known_ge(t, 2):
                                    sp.wait_ge(sc_ok.h, sc_ok.at(t - 1))
                                sp.dma_start(dec[:, par, :], edges(decay_row, t).partition_broadcast(P)).then_inc(dec_in[par].h, 16)
                                if known_ge(t, 2):
                                    sp.wait_ge(arg_ok.h, arg_ok.at(t - 1))
                                sp.dma_start(rst[:, par, :], edges(reset_add, t).partition_broadcast(P)).then_inc(rst_in[par].h, 16)
                            if known_ge(t, 3):
                                u = t - 3
                                sp.wait_ge(o_ok.h, o_ok.at(u + 1))
                                sp.dma_start(rows1[bass.ds(u * SC, SC), :].rearrange("(c p) w -> p c w", p=P),
                                             o[:, 1 - par, :, :]).then_inc(stored[1 - par].h, 16)
                        run_steps(sp, body, T, after=3)
                        for j in range(2):
                            sp.wait_ge(stored[j].h, stored[j].at(16 * T2))

                    @block.gpsimd
                    def _(pool):
                        run_steps(pool, lambda t, par, i: gather_step(pool, t, par, i, gathers, T, idx_in, (aT, xT), gathered), T)

                    @block.tensor
                    def _(pe):
                        pe.wait_ge(tmp_ok.h, tmp_ok.at(1))

                        def turn_in(t, par, i):
                            pe.wait_ge(gathered[par].h, gathered[par].at((i + 1) * (32 * CH)))
                            if known_ge(t, 1):
                                pe.wait_ge(pair_ok.h, pair_ok.at(t))
                            for c in range(CH):
                                mm = nc.tensor.transpose(bA[:, c * P:(c + 1) * P], gx[:, par, c, 0:2 * D], ident[:])
                            mm.then_inc(aT.h, 1)
                            if known_ge(t, 1):
                                pe.wait_ge(xs_ok.h, xs_ok.at(t))
                            for c in range(CH):
                                mm = nc.tensor.transpose(bX[:, c * P:(c + 1) * P], gx[:, par, c, D:3 * D], ident[:])
                            mm.then_inc(xT.h, 1)

                        def body(t, par, i):
                            if known_ge(t, 0) and known_lt(t, T):
                                pe.wait_ge(pair_ok.h, pair_ok.at(t + 1))
                                if known_ge(t, 1):
                                    pe.wait_ge(lr_ok.h, lr_ok.at(t))
                                nc.tensor.matmul(bL0[:], lw[:, 0, :], pair[:, par, :], start=True, stop=True)
                                nc.tensor.matmul(bL1[:], lw[:, 1, :], pair[:, par, :], start=True, stop=True).then_inc(l_ps.h, 1)
                            if known_lt(t, T - 1):
                                turn_in(t + 1, 1 - par, i + par)
                            if known_ge(t, 1):
                                pe.wait_ge(scanned.h, scanned.at(4 * t))
                                if known_ge(t, 2):
                                    pe.wait_ge(o_ok.h, o_ok.at(t - 1))
                                for g, b in ((0, bO0), (1, bO1)):
                                    for c in range(CH):
                                        nc.tensor.transpose(b[:, c * P:(c + 1) * P], num[:, 1 - par, g, c * P:(c + 1) * P], ident[:])
                                for c in range(CH):
                                    for g in range(2):
                                        k = c * HEADS1 + 2 * g
                                        mm = nc.tensor.matmul(bD[:, k:k + 2], den[:, 1 - par, g, c * P:(c + 1) * P], pick[:],
                                                              start=True, stop=True)
                                mm.then_inc(o_ps.h, 1)
                        run_steps(pe, body, T, before=1, after=1)

                    @block.scalar
                    def _(act):
                        def body(t, par, i):
                            mid = known_ge(t, 0) and known_lt(t, T)
                            if known_lt(t, T - 1):
                                act.wait_ge(aT.h, aT.at(t + 2))
                                if known_ge(t, 1):
                                    act.wait_ge(l_ps.h, l_ps.at(t))
                                nc.scalar.activation(pair[:, 1 - par, :], bA[:], ACT.Copy).then_inc(pair_ok.h, 1)
                                act.wait_ge(xT.h, xT.at(t + 2))
                                if known_ge(t, 1):
                                    act.wait_ge(pv_ok.h, pv_ok.at(t))
                                nc.scalar.activation(xs[:, 1 - par, :], bX[:], ACT.Copy).then_inc(xs_ok.h, 1)
                            if known_ge(t, 1):
                                act.wait_ge(o_ps.h, o_ps.at(t))
                                if known_ge(t, 3):
                                    act.wait_ge(stored[1 - par].h, stored[1 - par].at((i - 1 + par) * 16))
                                for g, b in ((0, bO0), (1, bO1)):
                                    nc.scalar.activation(o[:, 1 - par, :, g * P:(g + 1) * P], b[:].rearrange("p (c w) -> p c w", w=P), ACT.Copy)
                                nc.scalar.activation(o[:, 1 - par, :, 2 * P:W1], bD[:, 0:CH * HEADS1].rearrange("p (c w) -> p c w", w=HEADS1),
                                                     ACT.Copy).then_inc(o_ok.h, 1)
                            if mid:
                                act.wait_ge(arg_ok.h, arg_ok.at(t + 1))
                                if known_ge(t, 2):
                                    act.wait_ge(scanned.h, scanned.at(4 * (t - 1)))
                                for g in range(2):
                                    ins = nc.scalar.activation(pd[:, par, g, :], arg[:, par, g, :], ACT.Exp)
                                ins.then_inc(pd_ok.h, 1)
                        run_steps(act, body, T, before=1, after=1)

                    @block.vector
                    def _(dve):
                        for g in range(2):
                            for k in range(2):
                                ins = nc.vector.tensor_copy(lw[:, g, D * k:D * (k + 1)], aw[:, 2 * g + k:2 * g + k + 1].to_broadcast([P, D]))
                        ins.then_inc(tmp_ok.h, 1)
                        nc.vector.memset(mx[:, 1], -BIG).then_inc(tmp_ok.h, 1)
                        nc.vector.memset(num[:, 1], 0.0).then_inc(tmp_ok.h, 1)
                        nc.vector.memset(den[:, 1], 0.0).then_inc(tmp_ok.h, 1)
                        dve.wait_ge(tmp_ok.h, tmp_ok.at(4))

                        def both(x):
                            return x.unsqueeze(1).to_broadcast([P, 2, SC])

                        def body(t, par, i):
                            old = 1 - par
                            if known_ge(t, 1):
                                dve.wait_ge(pd_ok.h, pd_ok.at(t))
                                dve.wait_ge(xs_ok.h, xs_ok.at(t))
                                nc.vector.tensor_tensor(pv[:], pd[:, old, :, 0:SC], both(xs[:, old, :]), ALU.mult).then_inc(pv_ok.h, 1)
                                if known_ge(t, 3):
                                    dve.wait_ge(o_ps.h, o_ps.at(t - 2))
                                for g in range(2):
                                    nc.vector.tensor_tensor_scan(den[:, old, g, :], pd[:, old, g, SC:2 * SC], pd[:, old, g, 0:SC],
                                                                 den[:, par, g, SC - 1:SC], ALU.mult, ALU.add).then_inc(scanned.h, 1)
                                dve.wait_ge(pv_ok.h, pv_ok.at(t))
                                for g in range(2):
                                    nc.vector.tensor_tensor_scan(num[:, old, g, :], pd[:, old, g, SC:2 * SC], pv[:, g, :],
                                                                 num[:, par, g, SC - 1:SC], ALU.mult, ALU.add).then_inc(scanned.h, 1)
                            if known_ge(t, 0) and known_lt(t, T):
                                dve.wait_ge(l_ps.h, l_ps.at(t + 1))
                                dve.wait_ge(dec_in[par].h, dec_in[par].at((i + 1) * 16))
                                for g, b in ((0, bL0), (1, bL1)):
                                    ins = nc.vector.scalar_tensor_tensor(out=lr[:, g, :], in0=b[:], scalar=ab[:, g:g + 1], in1=dec[:, par, :],
                                                                         op0=ALU.add, op1=ALU.mult)
                                ins.then_inc(lr_ok.h, 1)
                                dve.wait_ge(lr_ok.h, lr_ok.at(t + 1))
                                nc.vector.scalar_tensor_tensor(out=sc[:], in0=lr[:], scalar=0.2, in1=lr[:],
                                                               op0=ALU.mult, op1=ALU.max).then_inc(sc_ok.h, 1)
                                dve.wait_ge(rst_in[par].h, rst_in[par].at((i + 1) * 16))
                                nc.vector.tensor_copy(mx[:, par, :, 0:1], mx[:, old, :, SC:SC + 1])
                                dve.wait_ge(sc_ok.h, sc_ok.at(t + 1))
                                for g in range(2):
                                    ins = nc.vector.tensor_tensor_scan(mx[:, par, g, 1:SC + 1], rst[:, par, :], sc[:, g, :],
                                                                       mx[:, old, g, SC:SC + 1], ALU.add, ALU.max)
                                ins.then_inc(mx_ok.h, 1)
                                dve.wait_ge(mx_ok.h, mx_ok.at(t + 1))
                                nc.vector.tensor_tensor(arg[:, par, :, SC:2 * SC], mx[:, par, :, 0:SC], both(rst[:, par, :]), ALU.add).then_inc(sub_ok.h, 1)
                                nc.vector.tensor_tensor(arg[:, par, :, 0:SC], sc[:], mx[:, par, :, 1:SC + 1], ALU.subtract)
                                dve.wait_ge(sub_ok.h, sub_ok.at(t + 1))
                                nc.vector.tensor_tensor(arg[:, par, :, SC:2 * SC], arg[:, par, :, SC:2 * SC], mx[:, par, :, 1:SC + 1],
                                                        ALU.subtract).then_inc(arg_ok.h, 1)
                        run_steps(dve, body, T, after=1)
                tmp_ok.passed(4)
                for j in range(2):
                    for s, n in ((idx_in, 16), (dec_in, 16), (rst_in, 16), (gathered, 32 * CH), (stored, 16)):
                        s[j].passed(n * T2)
                for s in (aT, xT, pair_ok, xs_ok, l_ps, lr_ok, sc_ok, mx_ok, sub_ok, arg_ok, pd_ok, pv_ok, o_ps, o_ok):
                    s.passed(T)
                scanned.passed(4 * T)

        def layer2_edges(layer):
            with ExitStack() as ctx:
                idx = sb(ctx, f"idx2_{layer}", [P, 2, 2 * CH], I32)
                gx = sb(ctx, f"gx2_{layer}", [P, 2, CH, 2 * D])
                keep = sb(ctx, f"keep2_{layer}", [P, 2, SC])
                sums = sb(ctx, f"sums2_{layer}", [P, 2, SC])
                o = sb(ctx, f"o2_{layer}", [P, 2, CH, 2 * D])
                idx_in, keep_in, gathered, stored = ([S(f"{n}{j}") for j in range(2)] for n in (
                    "idx_in", "rst_in", "gathered", "stored"))
                xT, scanned, o_ps, o_ok, tmp_ok = (S(n) for n in ("xT", "scanned", "o_ps", "o_ok", "tmp_ok"))

                def gathers(par):
                    for j in range(CH):
                        for half in range(2):
                            yield gx[:, par, j, half * D:(half + 1) * D], tab_row, idx[:, par, half * CH + j:half * CH + j + 1]

                with nc.Block() as block:
                    @block.sync
                    def _(sp):
                        def body(t, par, i):
                            if known_lt(t, T2):
                                if known_ge(t, 2):
                                    sp.wait_ge(gathered[par].h, gathered[par].at(i * (32 * CH)))
                                sp.dma_start(idx[:, par, :], a["idx_halves"][bass.ds(t, 1)].rearrange("t p j -> p (t j)")).then_inc(idx_in[par].h, 16)
                                if known_ge(t, 2):
                                    sp.wait_ge(scanned.h, scanned.at(t - 1))
                                sp.dma_start(keep[0:D, par, :], edges(keep_mul, t).partition_broadcast(D)).then_inc(keep_in[par].h, 16)
                                sp.dma_start(keep[D:P, par, :], edges(keep_mul, t + T2).partition_broadcast(D)).then_inc(keep_in[par].h, 16)
                            if known_ge(t, 3):
                                u = t - 3
                                sp.wait_ge(o_ok.h, o_ok.at(u + 1))
                                sp.dma_start(rows2[bass.ds(u * SC, SC), :].rearrange("(c p) w -> p c w", p=P),
                                             o[:, 1 - par, :, :]).then_inc(stored[1 - par].h, 16)
                        run_steps(sp, body, T2, after=3)
                        for j in range(2):
                            sp.wait_ge(stored[j].h, stored[j].at(8 * T2))

                    @block.gpsimd
                    def _(pool):
                        run_steps(pool, lambda t, par, i: gather_step(pool, t, par, i, gathers, T2, idx_in, (xT,), gathered), T2)

                    @block.tensor
                    def _(pe):
                        def body(t, par, i):
                            if known_lt(t, T2):
                                pe.wait_ge(gathered[par].h, gathered[par].at((i + 1) * (32 * CH)))
                                if known_ge(t, 2):
                                    pe.wait_ge(scanned.h, scanned.at(t - 1))
                                for c in range(CH):
                                    mm = nc.tensor.transpose(bank[par][:, c * P:(c + 1) * P], gx[:, par, c, :], ident[:])
                                mm.then_inc(xT.h, 1)
                            if known_ge(t, 1):
                                pe.wait_ge(scanned.h, scanned.at(t))
                                if known_ge(t, 3):
                                    pe.wait_ge(o_ok.h, o_ok.at(t - 2))
                                for c in range(CH):
                                    mm = nc.tensor.transpose(bank[3 - par][:, c * P:(c + 1) * P], sums[:, 1 - par, c * P:(c + 1) * P], ident[:])
                                mm.then_inc(o_ps.h, 1)
                        run_steps(pe, body, T2, after=1)

                    @block.vector
                    def _(dve):
                        nc.vector.memset(sums[:, 1, :], 0.0).then_inc(tmp_ok.h, 1)
                        dve.wait_ge(tmp_ok.h, tmp_ok.at(1))

                        def body(t, par, i):
                            dve.wait_ge(xT.h, xT.at(t + 1))
                            dve.wait_ge(keep_in[par].h, keep_in[par].at((i + 1) * 32))
                            if known_ge(t, 2):
                                dve.wait_ge(o_ps.h, o_ps.at(t - 1))
                            if known_ge(t, 1):
                                dve.wait_ge(scanned.h, scanned.at(t))
                            nc.vector.tensor_tensor_scan(sums[:, par, :], keep[:, par, :], bank[par][:],
                                                         sums[:, 1 - par, SC - 1:SC], ALU.mult, ALU.add).then_inc(scanned.h, 1)
                        run_steps(dve, body, T2)

                    @block.scalar
                    def _(act):
                        def body(t, par, i):
                            act.wait_ge(o_ps.h, o_ps.at(t + 1))
                            if known_ge(t, 2):
                                act.wait_ge(stored[par].h, stored[par].at(i * 16))
                            nc.scalar.activation(o[:, par, :, :], bank[2 + par][:].rearrange("p (c w) -> p c w", w=P),
                                                 ACT.Copy).then_inc(o_ok.h, 1)
                        run_steps(act, body, T2)
                tmp_ok.passed(1)
                for j in range(2):
                    for s, n in ((idx_in, 16), (keep_in, 32), (gathered, 32 * CH), (stored, 16)):
                        s[j].passed(n * T2 // 2)
                for s in (xT, scanned, o_ps, o_ok):
                    s.passed(T2)

        def layer3_edges():
            with ExitStack() as ctx:
                wab = sb(ctx, "wab3", [P, HID])
                wc = sb(ctx, "wc3", [32, HID])
                b_row = sb(ctx, "b_row3", [P, HID])
                b_c = sb(ctx, "b_c3", [P, 1])
                gb = sb(ctx, "gb3", [P, 5])
                mean_w = sb(ctx, "mean_w3", [P, HID])
                cut = sb(ctx, "cut3", [P, 4])
                idx = sb(ctx, "idx3", [P, 2, 2 * CH], I32)
                gx = sb(ctx, "gx3", [P, 2, CH, 2 * D])
                ea = sb(ctx, "ea3", [32, 2, SC])
                keep = sb(ctx, "keep3", [P, 2, SC])
                pair = sb(ctx, "pair3", [P, 2, SC])
                sq = sb(ctx, "sq3", [P, SC])
                lnv = sb(ctx, "lnv3", [P, SC])
                rstd = sb(ctx, "rstd3", [P, SC])
                nrm = sb(ctx, "nrm3", [P, SC])
                y = sb(ctx, "y3", [P, 2, SC])
                ex = sb(ctx, "ex3", [P, 2, SC])
                e1 = sb(ctx, "e13", [P, SC])
                rc = sb(ctx, "rc3", [P, SC])
                si = sb(ctx, "si3", [P, SC])
                sums = sb(ctx, "sums3", [P, 2, SC])
                o = sb(ctx, "o3", [P, 2, CH, HID])
                eps_t = sb(ctx, "eps3", [P, 1])
                load_all([(wab[:], a["W_msg1"][0:2 * D, :]), (wc[:], a["W_msg1"][2 * D:2 * D + 32, :]),
                          (gb[:, 0:1], a["b_msg1"]), (gb[:, 1:2], a["g_msg"]), (gb[:, 2:3], a["be_msg"]),
                          (mean_w[:], a["mean_w"])])
                with nc.Block() as block:
                    mm_ok = S("counted")

                    @block.tensor
                    def _(pe):
                        nc.tensor.matmul(bank[0][:, 0:1], mean_w[:], gb[:, 0:1], start=True, stop=True).then_inc(mm_ok.h, 1)

                    @block.vector
                    def _(dve):
                        for w, n, k in ((wab, P, 0), (wc, 32, 1)):
                            chain(dve, nc.vector.reduce_sum(cut[0:n, k:k + 1], w[:], AX_X))
                            chain(dve, nc.vector.tensor_scalar(cut[0:n, k:k + 1], cut[0:n, k:k + 1], 1.0 / HID, None, ALU.mult))
                            chain(dve, nc.vector.tensor_scalar(w[:], w[:], cut[0:n, k:k + 1], None, ALU.subtract))
                        chain(dve, nc.vector.memset(eps_t[:], EPS))
                        chain(dve, nc.vector.tensor_scalar(gb[:, 3:5], gb[:, 1:3], -1.0, None, ALU.mult))
                        dve.wait_ge(mm_ok.h, mm_ok.at(1))
                        chain(dve, nc.vector.tensor_tensor(b_c[:], gb[:, 0:1], bank[0][:, 0:1], ALU.subtract))
                mm_ok.passed(1)
                bA, bH, bV, bO = bank[0:4]
                idx_in, ea_in, keep_in, gathered, stored = ([S(f"{n}{j}") for j in range(2)] for n in (
                    "idx_in", "feat_in", "rst_in", "gathered", "stored"))
                aT, pair_ok, h_ps, sq_ok, v_ps, ln_ok, rstd_ok, nrm_ok, ex_ok = (S(n) for n in (
                    "xT", "hid_ok", "h_ps", "wk_ok", "v_ps", "wv_ok", "pd_ok", "kw_ok", "arg_ok"))
                e1_ok, rc_ok, si_ok, scanned, o_ps, o_ok, tmp_ok = (S(n) for n in (
                    "qk_ok", "val_ok", "pv_ok", "scanned", "o_ps", "o_ok", "tmp_ok"))

                def gathers(par):
                    for half in range(2):
                        for j in range(CH):
                            yield gx[:, par, j, half * D:(half + 1) * D], tab_row, idx[:, par, half * CH + j:half * CH + j + 1]

                with nc.Block() as block:
                    @block.sync
                    def _(sp):
                        def body(t, par, i):
                            if known_lt(t, T):
                                if known_ge(t, 2):
                                    sp.wait_ge(gathered[par].h, gathered[par].at(i * (32 * CH)))
                                sp.dma_start(idx[:, par, :], a["idx"][bass.ds(t, 1)].rearrange("t p j -> p (t j)")).then_inc(idx_in[par].h, 16)
                                if known_ge(t, 2):
                                    sp.wait_ge(h_ps.h, h_ps.at(t - 1))
                                sp.dma_start(ea[:, par, :], a["ea"][:, bass.ds(t * SC, SC)]).then_inc(ea_in[par].h, 16)
                                if known_ge(t, 2):
                                    sp.wait_ge(scanned.h, scanned.at(t - 1))
                                sp.dma_start(keep[:, par, :], edges(keep_mul, t).partition_broadcast(P)).then_inc(keep_in[par].h, 16)
                            if known_ge(t, 3):
                                u = t - 3
                                sp.wait_ge(o_ok.h, o_ok.at(u + 1))
                                sp.dma_start(rows3[bass.ds(u * SC, SC), :].rearrange("(c p) w -> p c w", p=P),
                                             o[:, 1 - par, :, :]).then_inc(stored[1 - par].h, 16)
                        run_steps(sp, body, T, after=3)
                        for j in range(2):
                            sp.wait_ge(stored[j].h, stored[j].at(16 * T2))

                    @block.gpsimd
                    def _(pool):
                        run_steps(pool, lambda t, par, i: gather_step(pool, t, par, i, gathers, T, idx_in, (aT,), gathered), T)

                    @block.tensor
                    def _(pe):
                        def turn_in(t, par, i):
                            pe.wait_ge(gathered[par].h, gathered[par].at((i + 1) * (32 * CH)))
                            if known_ge(t, 1):
                                pe.wait_ge(pair_ok.h, pair_ok.at(t))
                            for c in range(CH):
                                mm = nc.tensor.transpose(bA[:, c * P:(c + 1) * P], gx[:, par, c, :], ident[:])
                            mm.then_inc(aT.h, 1)

                        def body(t, par, i):
                            mid = known_ge(t, 0) and known_lt(t, T)
                            if mid:
                                pe.wait_ge(pair_ok.h, pair_ok.at(t + 1))
                                pe.wait_ge(ea_in[par].h, ea_in[par].at((i + 1) * 16))
                                if known_ge(t, 1):
                                    pe.wait_ge(nrm_ok.h, nrm_ok.at(t))
                                nc.tensor.matmul(bH[:], wab[:], pair[:, par, :], start=True, stop=False)
                                nc.tensor.matmul(bH[:], wc[:], ea[:, par, :], start=False, stop=True).then_inc(h_ps.h, 1)
                            if known_lt(t, T - 1):
                                turn_in(t + 1, 1 - par, i + par)
                            if mid:
                                pe.wait_ge(sq_ok.h, sq_ok.at(t + 1))
                                if known_ge(t, 1):
                                    pe.wait_ge(ln_ok.h, ln_ok.at(t))
                                nc.tensor.matmul(bV[:], mean_w[:], sq[:], start=True, stop=True).then_inc(v_ps.h, 1)
                            if known_ge(t, 1):
                                pe.wait_ge(scanned.h, scanned.at(t))
                                if known_ge(t, 2):
                                    pe.wait_ge(o_ok.h, o_ok.at(t - 1))
                                for c in range(CH):
                                    mm = nc.tensor.transpose(bO[:, c * P:(c + 1) * P], sums[:, 1 - par, c * P:(c + 1) * P], ident[:])
                                mm.then_inc(o_ps.h, 1)
                        run_steps(pe, body, T, before=1, after=1)

                    @block.scalar
                    def _(act):
                        def body(t, par, i):
                            mid = known_ge(t, 0) and known_lt(t, T)
                            if mid:
                                act.wait_ge(h_ps.h, h_ps.at(t + 1))
                                if known_ge(t, 1):
                                    act.wait_ge(v_ps.h, v_ps.at(t))
                                nc.scalar.activation(sq[:], bH[:], ACT.Square, bias=b_c[:]).then_inc(sq_ok.h, 1)
                            if known_lt(t, T - 1):
                                act.wait_ge(aT.h, aT.at(t + 2))
                                if known_ge(t, 1):
                                    act.wait_ge(h_ps.h, h_ps.at(t))
                                nc.scalar.activation(pair[:, 1 - par, :], bA[:], ACT.Copy).then_inc(pair_ok.h, 1)
                            if mid:
                                act.wait_ge(v_ps.h, v_ps.at(t + 1))
                                nc.scalar.activation(lnv[:], bV[:], ACT.Ln, bias=eps_t[:]).then_inc(ln_ok.h, 1)
                                act.wait_ge(ln_ok.h, ln_ok.at(t + 1))
                                if known_ge(t, 1):
                                    act.wait_ge(nrm_ok.h, nrm_ok.at(t))
                                nc.scalar.activation(rstd[:], lnv[:], ACT.Exp, scale=-0.5).then_inc(rstd_ok.h, 1)
                                act.wait_ge(nrm_ok.h, nrm_ok.at(t + 1))
                                if known_ge(t, 2):
                                    act.wait_ge(si_ok.h, si_ok.at(t - 1))
                                nc.scalar.activation(ex[:, par, :], nrm[:], ACT.Exp, scale=gb[:, 3:4], bias=gb[:, 4:5])
                                nc.scalar.activation(y[:, par, :], nrm[:], ACT.Identity, scale=gb[:, 1:2], bias=gb[:, 2:3]).then_inc(ex_ok.h, 1)
                            if known_ge(t, 1):
                                act.wait_ge(o_ps.h, o_ps.at(t))
                                if known_ge(t, 3):
                                    act.wait_ge(stored[1 - par].h, stored[1 - par].at((i - 1 + par) * 16))
                                nc.scalar.activation(o[:, 1 - par, :, :], bO[:].rearrange("p (c w) -> p c w", w=P), ACT.Copy).then_inc(o_ok.h, 1)
                        run_steps(act, body, T, before=1, after=1)

                    @block.vector
                    def _(dve):
                        nc.vector.memset(sums[:, 1, :], 0.0).then_inc(tmp_ok.h, 1)
                        dve.wait_ge(tmp_ok.h, tmp_ok.at(1))

                        def body(t, par, i):
                            old = 1 - par
                            if known_lt(t, T):
                                dve.wait_ge(rstd_ok.h, rstd_ok.at(t + 1))
                                if known_ge(t, 1):
                                    dve.wait_ge(ex_ok.h, ex_ok.at(t))
                                nc.vector.scalar_tensor_tensor(out=nrm[:], in0=bH[:], scalar=b_c[:], in1=rstd[:],
                                                               op0=ALU.add, op1=ALU.mult).then_inc(nrm_ok.h, 1)
                            if known_ge(t, 1):
                                dve.wait_ge(ex_ok.h, ex_ok.at(t))
                                nc.vector.tensor_scalar(e1[:], ex[:, old, :], 1.0, None, ALU.add).then_inc(e1_ok.h, 1)
                                dve.wait_ge(e1_ok.h, e1_ok.at(t))
                                nc.vector.reciprocal(rc[:], e1[:]).then_inc(rc_ok.h, 1)
                                dve.wait_ge(rc_ok.h, rc_ok.at(t))
                                nc.vector.tensor_tensor(si[:], y[:, old, :], rc[:], ALU.mult).then_inc(si_ok.h, 1)
                                dve.wait_ge(si_ok.h, si_ok.at(t))
                                dve.wait_ge(keep_in[old].h, keep_in[old].at((i + par) * 16))
                                if known_ge(t, 3):
                                    dve.wait_ge(o_ps.h, o_ps.at(t - 2))
                                nc.vector.tensor_tensor_scan(sums[:, old, :], keep[:, old, :], si[:],
                                                             sums[:, par, SC - 1:SC], ALU.mult, ALU.add).then_inc(scanned.h, 1)
                        run_steps(dve, body, T, after=1)
                tmp_ok.passed(1)
                for j in range(2):
                    for s, n in ((idx_in, 16), (ea_in, 16), (keep_in, 16), (gathered, 32 * CH), (stored, 16)):
                        s[j].passed(n * T2)
                for s in (aT, pair_ok, h_ps, sq_ok, v_ps, ln_ok, rstd_ok, nrm_ok, ex_ok, e1_ok, rc_ok, si_ok, scanned, o_ps, o_ok):
                    s.passed(T)

        def vector_step(*ops):
            with nc.Block() as block:
                @block.vector
                def _(dve):
                    for op in ops:
                        chain(dve, op())

        def add_back(bT):
            turn([(bT, tmp_n[:, :, 0:D], D, True)])
            vector_step(lambda: nc.vector.tensor_tensor(xn[:], xn[:], tmp_n[:, :, 0:D], ALU.add))

        prepare()

        pre_norm()
        turn([(hn[:], hT[:], D, False)])
        with ExitStack() as ctx:
            wq = sb(ctx, "wq", [D, P])
            load_all([(wq[:], a["Wq"])])
            product_rows([(hT[:], wq[:])], P, tmp_n[:])
            store_tables([(node_rows(tab_q, P), tmp_n[:]), (node_rows(tab_dup, 2 * D)[:, :, 0:D], hn[:]),
                          (node_rows(tab_dup, 2 * D)[:, :, D:2 * D], hn[:])])
        layer0_edges()
        with ExitStack() as ctx:
            g0 = sb(ctx, "g0", [P, NB, W0])
            rden = sb(ctx, "rden0", [P, NB, HEADS0])
            upd = sb(ctx, "upd0", [P, NB, P])
            updT = sb(ctx, "updT0", [P, NP])
            sumT = sb(ctx, "sumT0", [D, NP])
            bnT = sb(ctx, "bnT0", [D, NP])
            scT = sb(ctx, "scT0", [D, NP])
            w_out = sb(ctx, "w_out0", [P, D])
            w_self = sb(ctx, "w_self0", [D, D])
            gb = sb(ctx, "gb0", [D, 2])
            load_all([(w_out[:], a["W_out"]), (w_self[:], a["W_self"]), (gb[:, 0:1], a["gamma0"]), (gb[:, 1:2], a["beta0"])])
            read_rows([(rows0, last_row, g0)])
            vector_step(
                lambda: nc.vector.tensor_scalar(rden[:], g0[:, :, P:W0], 1e-16, None, ALU.add),
                lambda: nc.vector.reciprocal(rden[:], rden[:]),
                *[(lambda h=h: nc.vector.tensor_tensor(
                    upd[:, :, h * DH0:(h + 1) * DH0], g0[:, :, h * DH0:(h + 1) * DH0],
                    rden[:, :, h:h + 1].to_broadcast([P, NB, DH0]), ALU.mult)) for h in range(HEADS0)])
            turn([(upd[:], updT[:], P, False)])
            product_T([(w_out[:], updT[:]), (w_self[:], hT[:])], D, sumT[:])
            batch_norm(sumT[:], gb[:, 0:1], gb[:, 1:2], bnT[:], scT[:])
            add_back(bnT[:])

        pre_norm()
        turn([(hn[:], hT[:], D, False)])
        with ExitStack() as ctx:
            ww = sb(ctx, "ww", [D, D])
            wb = sb(ctx, "wb", [P, D])
            load_all([(ww[:], a["W_w"]), (wb[:], a["W_b"].partition_broadcast(P))])
            product_rows([(hT[:], ww[:])], D, tmp_n[:, :, 0:D], bias=wb[:])
            store_tables([(node_rows(tab_row, D), tmp_n[:, :, 0:D]), (node_rows(tab_dup, 2 * D)[:, :, 0:D], tmp_n[:, :, 0:D]),
                          (node_rows(tab_dup, 2 * D)[:, :, D:2 * D], tmp_n[:, :, 0:D])])
        layer1_edges()
        with ExitStack() as ctx:
            g1 = sb(ctx, "g1", [P, NB, W1])
            rden = sb(ctx, "rden1", [P, NB, HEADS1])
            aggT = [sb(ctx, f"aggT1{g}", [P, NP]) for g in range(2)]
            sumT = sb(ctx, "sumT1", [D, NP])
            pw = sb(ctx, "pw1", [P, 2, D])
            rows = sb(ctx, "brow1", [P, 3, D])
            zc = sb(ctx, "zc1", [P, NB, D])
            load_all([(pw[:, g, :], a["proj_w"][g * P:(g + 1) * P, :]) for g in range(2)]
                     + [(rows[:, k, :], a[n].partition_broadcast(P)) for k, n in enumerate(("proj_b", "ln_g", "ln_b"))])
            read_rows([(rows1, last_row, g1)])
            vector_step(
                lambda: nc.vector.tensor_scalar(rden[:], g1[:, :, 2 * P:W1], 1e-8, None, ALU.add),
                lambda: nc.vector.reciprocal(rden[:], rden[:]),
                *[(lambda h=h: nc.vector.tensor_tensor(
                    g1[:, :, h * D:(h + 1) * D], g1[:, :, h * D:(h + 1) * D],
                    rden[:, :, h:h + 1].to_broadcast([P, NB, D]), ALU.mult)) for h in range(HEADS1)])
            turn([(g1[:, :, g * P:(g + 1) * P], aggT[g][:], P, False) for g in range(2)])
            product_T([(pw[:, g, :], aggT[g][:]) for g in range(2)], D, sumT[:])
            turn([(sumT[:], tmp_n[:, :, 0:D], D, True)])
            row = lambda k: rows[:, k, :].unsqueeze(1).to_broadcast([P, NB, D])
            rs_sem, sd_sem = S("var_ready"), S("root_ready")
            with nc.Block() as block:
                @block.vector
                def _(dve):
                    z1 = tmp_n[:, :, 0:D]
                    chain(dve, nc.vector.tensor_tensor(z1, z1, row(0), ALU.add))
                    chain(dve, nc.vector.tensor_tensor(z1, z1, hn[:], ALU.add))
                    norm_rows(dve, z1, D, zc[:], tmp_n[:, :, D:2 * D], rs_sem, sd_sem)
                    chain(dve, nc.vector.tensor_tensor(zc[:], zc[:], row(1), ALU.mult))
                    chain(dve, nc.vector.tensor_tensor(zc[:], zc[:], row(2), ALU.add))
                    chain(dve, nc.vector.tensor_scalar(zc[:], zc[:], 0.0, None, ALU.max))
                    nc.vector.tensor_tensor(xn[:], xn[:], zc[:], ALU.add)

                @block.scalar
                def _(act):
                    root(act, rs_sem, sd_sem)
            rs_sem.passed(1)
            sd_sem.passed(1)

        pre_norm()
        with ExitStack() as ctx:
            w12 = sb(ctx, "w12", [D, 6, D])
            gb = sb(ctx, "gb2", [D, 6])
            scale = sb(ctx, "scale2", [P, 3])
            agg = sb(ctx, "agg2", [P, NB, D])
            more = sb(ctx, "more2", [P, NB, D])
            zT = sb(ctx, "zT2", [D, NP])
            uT = sb(ctx, "uT2", [D, NP])
            load_all([(w12[:, 0:3, :], a["W1T"].rearrange("l i o -> i l o")), (w12[:, 3:6, :], a["W2T"].rearrange("l i o -> i l o")),
                      (gb[:, 0:3], a["gamma2"]), (gb[:, 3:6], a["beta2"]), (scale[:], a["eps2"].partition_broadcast(P))])
            vector_step(lambda: nc.vector.tensor_scalar(scale[:], scale[:], 1.0, None, ALU.add))
            for layer in range(3):
                store_tables([(node_rows(tab_row, D), hn[:])])
                layer2_edges(layer)
                halves = rows2.rearrange("e (h w) -> (e h) w", h=2)
                read_rows([(halves, last_row2, agg), (halves, carry_row2, more)])
                vector_step(
                    lambda: nc.vector.tensor_tensor(agg[:], agg[:], more[:], ALU.add),
                    lambda: nc.vector.scalar_tensor_tensor(out=agg[:], in0=hn[:], scalar=scale[:, layer:layer + 1], in1=agg[:],
                                                           op0=ALU.mult, op1=ALU.add))
                turn([(agg[:], zT[:], D, False)])
                product_T([(w12[:, layer, :], zT[:])], D, uT[:], ACT.Relu)
                product_T([(w12[:, 3 + layer, :], uT[:])], D, zT[:], ACT.Relu)
                batch_norm(zT[:], gb[:, layer:layer + 1], gb[:, 3 + layer:4 + layer], uT[:], hT[:])
                turn([(uT[:], hn[:], D, True)])
            vector_step(lambda: nc.vector.tensor_tensor(xn[:], xn[:], hn[:], ALU.add))

        pre_norm()
        turn([(hn[:], hT[:], D, False)])
        store_tables([(node_rows(tab_row, D), hn[:])])
        layer3_edges()
        with ExitStack() as ctx:
            g3 = sb(ctx, "g3", [P, NB, HID])
            gT = sb(ctx, "gT3", [P, NP])
            agg = sb(ctx, "agg3", [P, NB, HID])
            wm2 = sb(ctx, "wm2", [HID, HID])
            wu1a = sb(ctx, "wu1a", [D, HID])
            wu1b = sb(ctx, "wu1b", [HID, HID])
            wu2 = sb(ctx, "wu2", [HID, D])
            rows = sb(ctx, "brow3", [P, 4, HID])
            b_u2 = sb(ctx, "b_u2", [P, D])
            load_all([(wm2[:], a["W_msg2"]), (wu1a[:], a["W_upd1"][0:D, :]), (wu1b[:], a["W_upd1"][D:D + HID, :]),
                      (wu2[:], a["W_upd2"]), (b_u2[:], a["b_upd2"].partition_broadcast(P))]
                     + [(rows[:, k, :], a[n].partition_broadcast(P)) for k, n in enumerate(("b_msg2", "b_upd1", "g_upd", "be_upd"))])
            read_rows([(rows3, last_row, g3)])
            turn([(g3[:], gT[:], P, False)])
            product_rows([(gT[:], wm2[:])], HID, agg[:])
            row = lambda k: rows[:, k, :].unsqueeze(1).to_broadcast([P, NB, HID])
            vector_step(
                lambda: nc.vector.tensor_tensor(g3[:], row(0), degree[:].unsqueeze(2).to_broadcast([P, NB, HID]), ALU.mult),
                lambda: nc.vector.tensor_tensor(agg[:], agg[:], g3[:], ALU.add))
            turn([(agg[:], gT[:], P, False)])
            product_rows([(hT[:], wu1a[:]), (gT[:], wu1b[:])], HID, agg[:], bias=rows[:, 1, :])
            rs_sem, sd_sem = S("var_ready"), S("root_ready")
            with nc.Block() as block:
                @block.vector
                def _(dve):
                    norm_rows(dve, agg[:], HID, g3[:], tmp_n[:], rs_sem, sd_sem)
                    chain(dve, nc.vector.tensor_tensor(g3[:], g3[:], row(2), ALU.mult))
                    nc.vector.tensor_tensor(g3[:], g3[:], row(3), ALU.add).then_inc(rs_sem.h, 1)
                    dve.wait_ge(sd_sem.h, sd_sem.at(2))
                    chain(dve, nc.vector.tensor_scalar(tmp_n[:], tmp_n[:], 1.0, None, ALU.add))
                    chain(dve, nc.vector.reciprocal(tmp_n[:], tmp_n[:]))
                    chain(dve, nc.vector.tensor_tensor(agg[:], g3[:], tmp_n[:], ALU.mult))

                @block.scalar
                def _(act):
                    root(act, rs_sem, sd_sem)
                    act.wait_ge(rs_sem.h, rs_sem.at(2))
                    nc.scalar.activation(tmp_n[:], g3[:], ACT.Exp, scale=-1.0).then_inc(sd_sem.h, 1)
            rs_sem.passed(2)
            sd_sem.passed(2)
            turn([(agg[:], gT[:], P, False)])
            product_rows([(gT[:], wu2[:])], D, tmp_n[:, :, 0:D], bias=b_u2[:])
            vector_step(
                lambda: nc.vector.tensor_tensor(hn[:], hn[:], tmp_n[:, :, 0:D], ALU.add),
                lambda: nc.vector.tensor_tensor(xn[:], xn[:], hn[:], ALU.add))
            store_tables([(out.rearrange("(p b) w -> p b w", b=NB), xn[0:PV])])


def constants():
    p = np.arange(P)
    headsum = (p[:, None] // DH0 == p[None, :] // DH0).astype(np.float32)
    pick0 = (p[:, None] == DH0 * np.arange(HEADS0)[None, :]).astype(np.float32)
    pick1 = (p[:, None] == D * np.arange(2)[None, :]).astype(np.float32)
    return {"ident": np.eye(P, dtype=np.float32), "headsum": headsum, "pick0": pick0, "pick1": pick1,
            "mean_w": np.full((P, HID), 1.0 / HID, np.float32)}


def lay_out(i):
    c = np.ascontiguousarray
    pad_e = EP - E
    src = np.pad(np.asarray(i["src"]), (0, pad_e))
    dst = np.pad(np.asarray(i["dst"]), (0, pad_e), constant_values=N)
    by_step = lambda v, steps: v.reshape(steps, CH, P).transpose(0, 2, 1)
    before = np.concatenate([np.full(1, -1, dst.dtype), dst[:-1]])
    col = lambda n: c(np.asarray(i[n]).reshape(-1, 1))
    wide = lambda n: c(np.pad(np.asarray(i[n]), ((0, pad_e), (0, 0))).T)
    return {
        "x": np.pad(np.asarray(i["x"]), ((0, NP - N), (0, 0))),
        "idx": c(np.concatenate([by_step(src, T), by_step(dst, T)], axis=2)),
        "idx_halves": c(np.concatenate([by_step(src[:HALF], T2), by_step(src[HALF:], T2)], axis=2)),
        "dst_rows": np.concatenate([dst, np.full(P, 2 * NP, dst.dtype)]).reshape(NC_ + 1, P),
        "chunk_last": c(dst[P - 1::P]),
        "dst_now": dst.reshape(P, NC_), "dst_before": before.reshape(P, NC_),
        "edge_weight": np.pad(np.asarray(i["edge_weight"]), (0, pad_e)).reshape(P, NC_),
        "ef": wide("edge_attr_64"), "sh": wide("edge_attr_9"), "ea": wide("edge_attr_32"),
        "Wq": c(i["L0_gnn_Wq"]), "Cqk": c(np.asarray(i["L0_gnn_Cqk"]).transpose(1, 0, 2)),
        "Cv": c(np.asarray(i["L0_gnn_Cv"]).transpose(1, 0, 2)),
        "k_w1": c(i["L0_gnn_k_w1"]), "v_w1": c(i["L0_gnn_v_w1"]), "k_w2": c(i["L0_gnn_k_w2"]), "v_w2": c(i["L0_gnn_v_w2"]),
        "k_b1": col("L0_gnn_k_b1"), "v_b1": col("L0_gnn_v_b1"), "k_b2": col("L0_gnn_k_b2"), "v_b2": col("L0_gnn_v_b2"),
        "W_out": c(i["L0_gnn_W_out"]), "W_self": c(i["L0_gnn_W_self"]),
        "gamma0": col("L0_gnn_gamma"), "beta0": col("L0_gnn_beta"),
        "W_w": c(i["L1_gnn_W_w"]), "W_b": c(i["L1_gnn_W_b"]), "attn_w": c(i["L1_gnn_attn_w"]), "attn_b": c(i["L1_gnn_attn_b"]),
        "decay_rate": c(i["L1_gnn_decay_rate"]),
        "proj_w": c(np.asarray(i["L1_gnn_proj_w"]).reshape(D, HEADS1, D).transpose(1, 0, 2)).reshape(HEADS1 * D, D),
        "proj_b": c(i["L1_gnn_proj_b"]), "ln_g": c(i["L1_gnn_ln_g"]), "ln_b": c(i["L1_gnn_ln_b"]),
        "W1T": c(np.asarray(i["L2_gnn_W1"]).transpose(0, 2, 1)), "W2T": c(np.asarray(i["L2_gnn_W2"]).transpose(0, 2, 1)),
        "gamma2": c(np.asarray(i["L2_gnn_gamma"]).T), "beta2": c(np.asarray(i["L2_gnn_beta"]).T), "eps2": c(i["L2_gnn_eps"]),
        "W_msg1": c(i["L3_gnn_W_msg1"]), "b_msg1": col("L3_gnn_b_msg1"), "g_msg": col("L3_gnn_g_msg"), "be_msg": col("L3_gnn_be_msg"),
        "W_msg2": c(i["L3_gnn_W_msg2"]), "b_msg2": c(i["L3_gnn_b_msg2"]),
        "W_upd1": c(i["L3_gnn_W_upd1"]), "b_upd1": c(i["L3_gnn_b_upd1"]), "g_upd": c(i["L3_gnn_g_upd"]),
        "be_upd": c(i["L3_gnn_be_upd"]), "W_upd2": c(i["L3_gnn_W_upd2"]), "b_upd2": c(i["L3_gnn_b_upd2"]),
    }


def kernel(**inputs):
    import concourse.bacc as bacc
    from concourse.bass_utils import run_bass_kernel_spmd as run

    nc = bacc.Bacc("TRN2", target_bir_lowering=False, num_devices=1)
    arrays, aps = {}, {}
    for name, value in {**lay_out(inputs), **constants()}.items():
        value = np.ascontiguousarray(value)
        arrays[f"in_{name}"] = value
        aps[name] = nc.dram_tensor(f"in_{name}", value.shape, mybir.dt.from_np(value.dtype), kind="ExternalInput").ap()
    out = nc.dram_tensor("out_0", (N, D), F32, kind="ExternalOutput").ap()
    build(nc, aps, out)
    return run(nc, [arrays], core_ids=[0]).results[0]["out_0"]
```

```python
from contextlib import ExitStack

import numpy as np

import concourse.bass as bass
from concourse import mybir

F32 = mybir.dt.float32
I32 = mybir.dt.int32
ALU = mybir.AluOpType
ACT = mybir.ActivationFunctionType
AX_X = mybir.AxisListType.X

P = 128
N, D, E = 3125, 64, 100000
NB = 25
NP = P * NB
PV = N // NB
SC = 512
CH = SC // P
T = 2 * -(-E // (2 * SC))
EP = T * SC
NC_ = EP // P
HALF = EP // 2
T2 = T // 2
HEADS0, DH0 = 8, 16
HEADS1 = 4
S9 = 9
ZPAIRS = (S9 + 1) // 2
W0 = P + HEADS0
W1 = HEADS1 * D + HEADS1
HID = 128
BIG = 1e30
EPS = 1e-5


class Sem:

    def __init__(self, nc, ctx, name):
        self.h = ctx.enter_context(nc.semaphore(name))
        self.base = 0

    def at(self, n):
        return n + self.base

    def passed(self, n):
        self.base += n


def known_ge(t, k):
    return t >= k if isinstance(t, int) else True


def known_lt(t, k):
    return t < k if isinstance(t, int) else True


def run_steps(eng, body, steps, before=0, after=0, first=4):
    for t in range(-before, first):
        body(t, t % 2, t // 2)
    with eng.Fori(first // 2, steps // 2 - 1) as i:
        body(i * 2, 0, i)
        body(i * 2 + 1, 1, i)
    for t in range(steps - 2, steps + after):
        body(t, t % 2, t // 2)


def build(nc, a, out):
    with ExitStack() as top:
        dram = lambda name, shape, dt=F32: nc.dram_tensor(name, shape, dt).ap()
        tab_dup = dram("tab_dup", (NP, 2 * D))
        tab_row = dram("tab_row", (NP, D))
        tab_q = dram("tab_q", (NP, P))
        rows0 = dram("rows0", (EP + 1, W0))
        rows1 = dram("rows1", (EP + 1, W1))
        rows2 = dram("rows2", (HALF + 1, 2 * D))
        rows3 = dram("rows3", (EP + 1, HID))
        dst_first = dram("dst_first", (EP + NP, D))
        reset_add = dram("reset_add", (EP,))
        keep_mul = dram("keep_mul", (EP,))
        decay_row = dram("decay_row", (EP,))

        def sb(ctx, name, shape, dt=F32):
            return ctx.enter_context(nc.sbuf_tensor(name, shape, dt))

        bank = [top.enter_context(nc.psum_tensor(f"bank{i}", [P, 512], F32)) for i in range(8)]

        names = {}

        def S(name):
            if name not in names:
                names[name] = Sem(nc, top, name)
            return names[name]

        ident = sb(top, "ident", [P, P])
        xn = sb(top, "xn", [P, NB, D])
        hn = sb(top, "hn", [P, NB, D])
        tmp_n = sb(top, "tmp_n", [P, NB, P])
        hT = sb(top, "hT", [D, NP])
        last_row = sb(top, "last_row", [P, NB], I32)
        last_row2 = sb(top, "last_row2", [P, NB], I32)
        crosses = sb(top, "crosses", [P, NB])
        first_row = sb(top, "first_row", [P, NB], I32)
        degree = sb(top, "degree", [P, NB])
        stat = [sb(top, f"stat{i}", [P, NB]) for i in range(4)]
        chain_sem = S("chain")

        def chain(eng, ins):
            ins.then_inc(chain_sem.h, 1)
            chain_sem.passed(1)
            eng.wait_ge(chain_sem.h, chain_sem.base)

        def load_all(pairs):
            sem = S("loaded")
            with nc.Block() as block:
                @block.sync
                def _(sp):
                    for dst, src in pairs:
                        sp.dma_start(dst, src).then_inc(sem.h, 16)
                    sp.wait_ge(sem.h, sem.at(16 * len(pairs)))
            sem.passed(16 * len(pairs))

        def node_rows(d, w):
            return d.rearrange("(p b) w -> p b w", b=NB)[:, :, 0:w] if w != d.shape[1] else d.rearrange("(p b) w -> p b w", b=NB)

        def norm_rows(dve, src, w, dst, scratch, rs_sem, sd_sem):
            s, m, v, r = (t[:] for t in stat)
            chain(dve, nc.vector.reduce_sum(s, src, AX_X))
            chain(dve, nc.vector.tensor_scalar(m, s, 1.0 / w, None, ALU.mult))
            chain(dve, nc.vector.tensor_tensor(dst, src, m.unsqueeze(2).to_broadcast([P, NB, w]), ALU.subtract))
            chain(dve, nc.vector.tensor_tensor(scratch, dst, dst, ALU.mult))
            chain(dve, nc.vector.reduce_sum(s, scratch, AX_X))
            nc.vector.tensor_scalar(v, s, 1.0 / w, EPS, ALU.mult, ALU.add).then_inc(rs_sem.h, 1)
            dve.wait_ge(sd_sem.h, sd_sem.at(1))
            chain(dve, nc.vector.reciprocal(m, r))
            chain(dve, nc.vector.tensor_tensor(dst, dst, m.unsqueeze(2).to_broadcast([P, NB, w]), ALU.mult))

        def root(act, rs_sem, sd_sem, n=P, tiles=(2, 3), w=NB):
            act.wait_ge(rs_sem.h, rs_sem.at(1))
            nc.scalar.activation(stat[tiles[1]][0:n, 0:w], stat[tiles[0]][0:n, 0:w], ACT.Sqrt).then_inc(sd_sem.h, 1)

        def pre_norm():
            rs_sem, sd_sem = S("var_ready"), S("root_ready")
            with nc.Block() as block:
                @block.vector
                def _(dve):
                    norm_rows(dve, xn[:], D, hn[:], tmp_n[:, :, 0:D], rs_sem, sd_sem)
                    nc.vector.tensor_scalar(hn[:], hn[:], 0.0, None, ALU.max)

                @block.scalar
                def _(act):
                    root(act, rs_sem, sd_sem)
            rs_sem.passed(1)
            sd_sem.passed(1)

        def turn(jobs):
            turned, emptied = S("turned"), S("emptied")
            work = []
            for src, dst, w, back in jobs:
                per = 512 // w if back else CH
                for g in range(0, NB, per):
                    work.append((src, dst, w, back, g, min(per, NB - g)))
            with nc.Block() as block:
                @block.tensor
                def _(pe):
                    for k, (src, dst, w, back, g, n) in enumerate(work):
                        if k >= 2:
                            pe.wait_ge(emptied.h, emptied.at(k - 1))
                        for j in range(n):
                            if back:
                                mm = nc.tensor.transpose(bank[k % 2][:, j * w:(j + 1) * w],
                                                         src[:, (g + j) * P:(g + j + 1) * P], ident[0:w, 0:w])
                            else:
                                mm = nc.tensor.transpose(bank[k % 2][0:w, j * P:(j + 1) * P],
                                                         src[:, g + j, :], ident[:])
                        mm.then_inc(turned.h, 1)

                @block.scalar
                def _(act):
                    for k, (src, dst, w, back, g, n) in enumerate(work):
                        act.wait_ge(turned.h, turned.at(k + 1))
                        if back:
                            o, i = dst[:, g:g + n, :], bank[k % 2][:, 0:n * w].rearrange("p (b w) -> p b w", w=w)
                        else:
                            o, i = dst[:, g * P:(g + n) * P], bank[k % 2][0:w, 0:n * P]
                        nc.scalar.activation(o, i, ACT.Copy).then_inc(emptied.h, 1)
            turned.passed(len(work))
            emptied.passed(len(work))

        def product_T(terms, m, dst, func=ACT.Copy):
            made, emptied = S("turned"), S("emptied")
            cuts = [(c, min(512, NP - c)) for c in range(0, NP, 512)]
            with nc.Block() as block:
                @block.tensor
                def _(pe):
                    for k, (c, n) in enumerate(cuts):
                        if k >= 2:
                            pe.wait_ge(emptied.h, emptied.at(k - 1))
                        for j, (lhsT, rhs) in enumerate(terms):
                            mm = nc.tensor.matmul(bank[k % 2][0:m, 0:n], lhsT, rhs[:, c:c + n],
                                                  start=(j == 0), stop=(j == len(terms) - 1))
                        mm.then_inc(made.h, 1)

                @block.scalar
                def _(act):
                    for k, (c, n) in enumerate(cuts):
                        act.wait_ge(made.h, made.at(k + 1))
                        nc.scalar.activation(dst[:, c:c + n], bank[k % 2][0:m, 0:n], func).then_inc(emptied.h, 1)
            made.passed(len(cuts))
            emptied.passed(len(cuts))

        def product_rows(terms, w, dst, bias=None):
            made, emptied = S("turned"), S("emptied")
            per = 512 // w
            cuts = [(g, min(per, NB - g)) for g in range(0, NB, per)]
            with nc.Block() as block:
                @block.tensor
                def _(pe):
                    for k, (g, n) in enumerate(cuts):
                        if k >= 2:
                            pe.wait_ge(emptied.h, emptied.at(k - 1))
                        for b in range(n):
                            for j, (tform, weights) in enumerate(terms):
                                mm = nc.tensor.matmul(bank[k % 2][:, b * w:(b + 1) * w],
                                                      tform[:, (g + b) * P:(g + b + 1) * P], weights,
                                                      start=(j == 0), stop=(j == len(terms) - 1))
                        mm.then_inc(made.h, 1)

                @block.vector
                def _(dve):
                    for k, (g, n) in enumerate(cuts):
                        dve.wait_ge(made.h, made.at(k + 1))
                        i = bank[k % 2][:, 0:n * w].rearrange("p (b w) -> p b w", w=w)
                        if bias is None:
                            nc.vector.tensor_copy(dst[:, g:g + n, :], i).then_inc(emptied.h, 1)
                        else:
                            nc.vector.tensor_tensor(dst[:, g:g + n, :], i,
                                                    bias.unsqueeze(1).to_broadcast([P, n, w]),
                                                    ALU.add).then_inc(emptied.h, 1)
            made.passed(len(cuts))
            emptied.passed(len(cuts))

        def store_tables(pairs):
            sem = S("loaded")
            with nc.Block() as block:
                @block.sync
                def _(sp):
                    for dst, src in pairs:
                        sp.dma_start(dst, src).then_inc(sem.h, 16)
                    sp.wait_ge(sem.h, sem.at(16 * len(pairs)))
            sem.passed(16 * len(pairs))

        def read_rows(jobs):
            sem = S("rows_read")
            with nc.Block() as block:
                @block.gpsimd
                def _(pool):
                    for table, index, dst in jobs:
                        for b in range(NB):
                            nc.gpsimd.indirect_dma_start(
                                out=dst[:, b, :], out_offset=None, in_=table,
                                in_offset=bass.IndirectOffsetOnAxis(ap=index[:, b:b + 1], axis=0),
                            ).then_inc(sem.h, 16)
                    pool.wait_ge(sem.h, sem.at(16 * NB * len(jobs)))
            sem.passed(16 * NB * len(jobs))

        def put_first_rows(src):
            sem = S("rows_read")
            with nc.Block() as block:
                @block.gpsimd
                def _(pool):
                    for b in range(NB):
                        nc.gpsimd.indirect_dma_start(
                            out=dst_first, out_offset=bass.IndirectOffsetOnAxis(ap=first_row[:, b:b + 1], axis=0),
                            in_=src[:, b, :], in_offset=None).then_inc(sem.h, 16)
                    pool.wait_ge(sem.h, sem.at(16 * NB))
            sem.passed(16 * NB)

        def batch_norm(vT, gamma, beta, dst, scratch):
            rs_sem, sd_sem = S("var_ready"), S("root_ready")
            real = lambda t: t.rearrange("d (b p) -> d b p", p=P)[:, :, 0:PV]
            s, m, v, r = (t[0:D, 0:1] for t in stat)
            part = stat[0][0:D, 0:NB]
            with nc.Block() as block:
                @block.vector
                def _(dve):
                    chain(dve, nc.vector.reduce_sum(part, real(vT), AX_X))
                    chain(dve, nc.vector.reduce_sum(m, part, AX_X))
                    chain(dve, nc.vector.tensor_scalar(m, m, 1.0 / N, None, ALU.mult))
                    chain(dve, nc.vector.tensor_scalar(dst, vT, m, None, ALU.subtract))
                    chain(dve, nc.vector.tensor_tensor(scratch, dst, dst, ALU.mult))
                    chain(dve, nc.vector.reduce_sum(part, real(scratch), AX_X))
                    chain(dve, nc.vector.reduce_sum(m, part, AX_X))
                    nc.vector.tensor_scalar(v, m, 1.0 / N, EPS, ALU.mult, ALU.add).then_inc(rs_sem.h, 1)
                    dve.wait_ge(sd_sem.h, sd_sem.at(1))
                    chain(dve, nc.vector.reciprocal(m, r))
                    chain(dve, nc.vector.tensor_tensor(m, m, gamma, ALU.mult))
                    nc.vector.tensor_scalar(dst, dst, m, beta, ALU.mult, ALU.add)

                @block.scalar
                def _(act):
                    root(act, rs_sem, sd_sem, n=D, w=1)
            rs_sem.passed(1)
            sd_sem.passed(1)

        def prepare():
            ZW = EP * D // P // 16
            with ExitStack() as ctx:
                dst_f = sb(ctx, "dst_f", [P, NC_])
                d_now = sb(ctx, "d_now", [P, NC_], I32)
                d_bef = sb(ctx, "d_bef", [P, NC_], I32)
                same = sb(ctx, "same", [P, NC_])
                reset = sb(ctx, "reset", [P, NC_])
                ew = sb(ctx, "ew", [P, NC_])
                chunk_last = sb(ctx, "chunk_last", [P, NC_], I32)
                rate = sb(ctx, "rate", [P, 1])
                zero = sb(ctx, "zero", [P, ZW])
                node_i = sb(ctx, "node_i", [P, NB], I32)
                bound = sb(ctx, "bound", [P, 2, NB])
                before = sb(ctx, "before", [P, 2, NB])
                before_i = sb(ctx, "before_i", [P, 2, NB], I32)
                rows = sb(ctx, "rows", [P, 2 * NB, P], I32)
                inside = sb(ctx, "inside", [P, 2, NB])
                edge = sb(ctx, "edge", [P, 2, NB])
                flag = sb(ctx, "flag", [P, NB])
                flag2 = sb(ctx, "flag2", [P, NB])
                k1 = sb(ctx, "k1", [P, NB])
                junk = sb(ctx, "junk", [P, NC_])
                load_all([(ident[:], a["ident"]), (xn[:], node_rows(a["x"], D)),
                          (d_now[:], a["dst_now"]), (d_bef[:], a["dst_before"]),
                          (ew[:], a["edge_weight"]), (chunk_last[:], a["chunk_last"].partition_broadcast(P)),
                          (rate[:], a["decay_rate"].partition_broadcast(P))])
                made, expd, rd = S("var_ready"), S("root_ready"), S("rows_read")
                sent, counted, iota, zeroed = S("loaded"), S("counted"), S("iota_ready"), S("tmp_ok")
                with nc.Block() as block:
                    @block.gpsimd
                    def _(pool):
                        nc.gpsimd.iota(node_i[:], pattern=[[1, NB]], base=0,
                                       channel_multiplier=NB).then_inc(iota.h, 1)
                        pool.wait_ge(counted.h, counted.at(1))
                        for j in range(2 * NB):
                            nc.gpsimd.indirect_dma_start(
                                out=rows[:, j, :], out_offset=None, in_=a["dst_rows"],
                                in_offset=bass.IndirectOffsetOnAxis(ap=before_i[:, j // NB, j % NB:j % NB + 1], axis=0),
                            ).then_inc(rd.h, 16)

                    @block.vector
                    def _(dve):
                        nc.vector.memset(zero[:], 0.0).then_inc(zeroed.h, 1)
                        chain(dve, nc.vector.tensor_copy(dst_f[:], d_now[:]))
                        chain(dve, nc.vector.tensor_copy(reset[:], d_bef[:]))
                        chain(dve, nc.vector.tensor_tensor(same[:], dst_f[:], reset[:], ALU.is_equal))
                        chain(dve, nc.vector.tensor_scalar(reset[:], same[:], -1.0, BIG, ALU.add, ALU.mult))
                        chain(dve, nc.vector.tensor_scalar(stat[0][:, 0:1], rate[:], -1.0, None, ALU.mult))
                        chain(dve, nc.vector.tensor_tensor(stat[0][:, 0:1], stat[0][:, 0:1], rate[:], ALU.max))
                        nc.vector.tensor_scalar(rate[:], rate[:], 0.0, None, ALU.max).then_inc(made.h, 1)
                        dve.wait_ge(iota.h, iota.at(1))
                        chain(dve, nc.vector.tensor_copy(bound[:, 0, :], node_i[:]))
                        chain(dve, nc.vector.tensor_scalar(bound[:, 1, :], bound[:, 0, :], 1.0, None, ALU.add))
                        chain(dve, nc.vector.tensor_copy(dst_f[:], chunk_last[:]))
                        for k in range(2):
                            for b in range(NB):
                                chain(dve, nc.vector.tensor_scalar(junk[:], dst_f[:], bound[:, k, b:b + 1], 0.0,
                                                                   ALU.is_lt, ALU.add,
                                                                   accum_out=before[:, k, b:b + 1]))
                        nc.vector.tensor_copy(before_i[:], before[:]).then_inc(counted.h, 1)
                        dve.wait_ge(expd.h, expd.at(2))
                        chain(dve, nc.vector.tensor_tensor(rate[:], rate[:], stat[1][:, 0:1], ALU.add))
                        nc.vector.tensor_scalar(ew[:], ew[:], -1.0, rate[:, 0:1], ALU.add, ALU.mult).then_inc(made.h, 1)
                        dve.wait_ge(rd.h, rd.at(32 * NB))
                        for k in range(2):
                            for b in range(NB):
                                chain(dve, nc.vector.tensor_copy(junk[:, 0:P], rows[:, k * NB + b, :]))
                                chain(dve, nc.vector.tensor_scalar(junk[:, P:2 * P], junk[:, 0:P], bound[:, k, b:b + 1], 0.0,
                                                                   ALU.is_lt, ALU.add,
                                                                   accum_out=inside[:, k, b:b + 1]))
                        chain(dve, nc.vector.tensor_scalar(edge[:], before[:], float(P), None, ALU.mult))
                        chain(dve, nc.vector.tensor_tensor(edge[:], edge[:], inside[:], ALU.add))
                        chain(dve, nc.vector.tensor_tensor(degree[:], edge[:, 1, :], edge[:, 0, :], ALU.subtract))
                        chain(dve, nc.vector.tensor_scalar(flag[:], degree[:], 1.0, None, ALU.min))
                        chain(dve, nc.vector.tensor_scalar(k1[:], edge[:, 1, :], float(-1 - EP), None, ALU.add))
                        chain(dve, nc.vector.tensor_tensor(k1[:], k1[:], flag[:], ALU.mult))
                        chain(dve, nc.vector.tensor_scalar(k1[:], k1[:], float(EP), None, ALU.add))
                        chain(dve, nc.vector.tensor_copy(last_row[:], k1[:]))
                        chain(dve, nc.vector.tensor_scalar(junk[:, 0:NB], bound[:, 0, :], float(EP), None, ALU.add))
                        chain(dve, nc.vector.tensor_tensor(flag2[:], edge[:, 0, :], junk[:, 0:NB], ALU.subtract))
                        chain(dve, nc.vector.tensor_tensor(flag2[:], flag2[:], flag[:], ALU.mult))
                        chain(dve, nc.vector.tensor_tensor(flag2[:], flag2[:], junk[:, 0:NB], ALU.add))
                        chain(dve, nc.vector.tensor_copy(first_row[:], flag2[:]))
                        chain(dve, nc.vector.tensor_scalar(flag2[:], k1[:], float(HALF), None, ALU.is_ge))
                        chain(dve, nc.vector.tensor_tensor(flag2[:], flag2[:], flag[:], ALU.mult))
                        chain(dve, nc.vector.tensor_scalar(k1[:], edge[:, 1, :], 2.0, float(-2 - EP), ALU.mult, ALU.add))
                        chain(dve, nc.vector.tensor_tensor(k1[:], k1[:], flag[:], ALU.mult))
                        chain(dve, nc.vector.tensor_scalar(junk[:, 0:NB], flag2[:], float(1 - 2 * HALF), float(EP), ALU.mult, ALU.add))
                        chain(dve, nc.vector.tensor_tensor(k1[:], k1[:], junk[:, 0:NB], ALU.add))
                        chain(dve, nc.vector.tensor_copy(last_row2[:], k1[:]))
                        chain(dve, nc.vector.tensor_scalar(flag[:], edge[:, 0, :], float(HALF), None, ALU.is_lt))
                        chain(dve, nc.vector.tensor_tensor(crosses[:], flag[:], flag2[:], ALU.mult))

                    @block.scalar
                    def _(act):
                        act.wait_ge(made.h, made.at(1))
                        nc.scalar.activation(stat[2][:, 0:1], stat[0][:, 0:1], ACT.Exp, scale=-1.0).then_inc(expd.h, 1)
                        act.wait_ge(expd.h, expd.at(1))
                        nc.scalar.activation(stat[1][:, 0:1], stat[2][:, 0:1], ACT.Ln, bias=1.0).then_inc(expd.h, 1)
                        act.wait_ge(made.h, made.at(2))
                        nc.scalar.activation(ew[:], ew[:], ACT.Exp).then_inc(expd.h, 1)

                    @block.sync
                    def _(sp):
                        sp.wait_ge(zeroed.h, zeroed.at(1))
                        for k in range(16):
                            sp.dma_start(dst_first[0:EP, :].rearrange("(k p c) d -> k p (c d)", k=16, p=P)[k],
                                         zero[:]).then_inc(sent.h, 16)
                        sp.wait_ge(made.h, made.at(1))
                        row = lambda d: d.rearrange("(p c) -> p c", c=NC_)
                        sp.dma_start(row(keep_mul), same[:]).then_inc(sent.h, 16)
                        sp.dma_start(row(reset_add), reset[:]).then_inc(sent.h, 16)
                        sp.dma_start(rows0[EP:EP + 1, :], zero[0:1, 0:W0]).then_inc(sent.h, 16)
                        sp.dma_start(rows1[EP:EP + 1, :], zero[0:1, 0:W1]).then_inc(sent.h, 16)
                        sp.dma_start(rows2[HALF:HALF + 1, :], zero[0:1, 0:2 * D]).then_inc(sent.h, 16)
                        sp.dma_start(rows3[EP:EP + 1, :], zero[0:1, 0:HID]).then_inc(sent.h, 16)
                        sp.wait_ge(expd.h, expd.at(3))
                        sp.dma_start(row(decay_row), ew[:]).then_inc(sent.h, 16)
                        sp.wait_ge(sent.h, sent.at(16 * 23))
                made.passed(2)
                expd.passed(3)
                rd.passed(32 * NB)
                sent.passed(16 * 23)
                zeroed.passed(1)
                counted.passed(1)
                iota.passed(1)

        def gather_step(pool, t, par, i, what, steps, idx_in, slots_free, gathered):
            if not (known_ge(t, 0) and known_lt(t, steps)):
                return
            pool.wait_ge(idx_in[par].h, idx_in[par].at((i + 1) * 16))
            if known_ge(t, 2):
                for sem in slots_free:
                    pool.wait_ge(sem.h, sem.at(t - 1))
            nc.gpsimd.sem_inc(S("pool_turn").h, 1)
            for dst, table, index in what(par):
                nc.gpsimd.indirect_dma_start(out=dst, out_offset=None, in_=table,
                                             in_offset=bass.IndirectOffsetOnAxis(ap=index, axis=0)
                                             ).then_inc(gathered[par].h, 16)

        def edges(d, t):
            return d[bass.ds(t * SC, SC)]

        def layer0_edges():
            with ExitStack() as ctx:
                ck = sb(ctx, "ck", [P, ZPAIRS, P])
                cv = sb(ctx, "cv", [P, ZPAIRS, P])
                w1 = sb(ctx, "w1", [D, 2 * D])
                b1 = sb(ctx, "b1", [P, 1])
                w2 = sb(ctx, "w2", [P, P])
                b2 = sb(ctx, "b2", [P, 2])
                headsum = sb(ctx, "headsum", [P, P])
                idx = sb(ctx, "idx", [P, 2, 2 * CH], I32)
                gx = sb(ctx, "gx", [P, 2, CH, 2 * D])
                gq = sb(ctx, "gq", [P, 2, CH, P])
                ef = sb(ctx, "ef", [D, 2, SC])
                sh = sb(ctx, "sh", [P, 2, ZPAIRS, SC])
                z = sb(ctx, "z", [P, 2, ZPAIRS, SC])
                rst = sb(ctx, "rst", [P, 2, SC])
                hid = sb(ctx, "hid", [P, 2, SC])
                wk = sb(ctx, "wk", [P, SC])
                wv = sb(ctx, "wv", [P, SC])
                kw = sb(ctx, "kw", [P, SC])
                qk = sb(ctx, "qk", [P, SC])
                val = sb(ctx, "val", [P, 2, SC])
                mx = sb(ctx, "mx", [P, 2, SC + 1])
                arg = sb(ctx, "arg", [P, 2, 2 * SC])
                pd = sb(ctx, "pd", [P, 2, 2 * SC])
                pv = sb(ctx, "pv", [P, SC])
                num = sb(ctx, "num", [P, 2, SC])
                den = sb(ctx, "den", [P, 2, SC])
                o = sb(ctx, "o", [P, 2, CH, W0])
                pairs = [(ck[0:D, j, :], a["Cqk"][2 * j]) for j in range(ZPAIRS)]
                pairs += [(ck[D:P, j, :], a["Cqk"][2 * j + 1]) for j in range(ZPAIRS - 1)]
                pairs += [(cv[0:D, j, :], a["Cv"][2 * j]) for j in range(ZPAIRS)]
                pairs += [(cv[D:P, j, :], a["Cv"][2 * j + 1]) for j in range(ZPAIRS - 1)]
                pairs += [(w1[:, 0:D], a["k_w1"]), (w1[:, D:2 * D], a["v_w1"]), (b1[0:D, :], a["k_b1"]),
                          (b1[D:P, :], a["v_b1"]), (w2[0:D, :], a["k_w2"]), (w2[D:P, :], a["v_w2"]),
                          (b2[:, 0:1], a["k_b2"]), (b2[:, 1:2], a["v_b2"]),
                          (headsum[:], a["headsum"])]
                load_all(pairs)
                bX, bQ, bH, bW, bK, bV, bS, bO = bank
                idx_in, ef_in, sh_in, rst_in = ([S(f"{n}{j}") for j in range(2)] for n in ("idx_in", "feat_in", "sh_in", "rst_in"))
                gathered, stored = ([S(f"{n}{j}") for j in range(2)] for n in ("gathered", "stored"))
                xT, qT, h_ps, hid_ok, wk_ps, wk_ok, wv_ps, wv_ok = (S(n) for n in (
                    "xT", "qT", "h_ps", "hid_ok", "wk_ps", "wk_ok", "wv_ps", "wv_ok"))
                z_ok, k_ps, v_ps, kw_ok, qk_ok, s_ps, mx_ok, arg_ok = (S(n) for n in (
                    "z_ok", "k_ps", "v_ps", "kw_ok", "qk_ok", "s_ps", "mx_ok", "arg_ok"))
                pd_ok, val_ok, pv_ok, scanned, o_ps, o_ok, tmp_ok, sub_ok = (S(n) for n in (
                    "pd_ok", "val_ok", "pv_ok", "scanned", "o_ps", "o_ok", "tmp_ok", "sub_ok"))

                def gathers(par):
                    for j in range(CH):
                        yield gx[:, par, j, :], tab_dup, idx[:, par, j:j + 1]
                    for j in range(CH):
                        yield gq[:, par, j, :], tab_q, idx[:, par, CH + j:CH + j + 1]

                with nc.Block() as block:
                    @block.sync
                    def _(sp):
                        def body(t, par, i):
                            if known_lt(t, T):
                                if known_ge(t, 2):
                                    sp.wait_ge(gathered[par].h, gathered[par].at(i * (16 * 2 * CH)))
                                sp.dma_start(idx[:, par, :], a["idx"][bass.ds(t, 1)].rearrange("t p j -> p (t j)")).then_inc(idx_in[par].h, 16)
                                if known_ge(t, 2):
                                    sp.wait_ge(h_ps.h, h_ps.at(t - 1))
                                sp.dma_start(ef[:, par, :], a["ef"][:, bass.ds(t * SC, SC)]).then_inc(ef_in[par].h, 16)
                                if known_ge(t, 2):
                                    sp.wait_ge(z_ok.h, z_ok.at(t - 1))
                                sp.dma_start(sh[0:D, par, :, :], a["sh"][0:S9:2, bass.ds(t * SC, SC)].partition_broadcast(D)).then_inc(sh_in[par].h, 16)
                                sp.dma_start(sh[D:P, par, 0:ZPAIRS - 1, :], a["sh"][1:S9:2, bass.ds(t * SC, SC)].partition_broadcast(D)).then_inc(sh_in[par].h, 16)
                                if known_ge(t, 2):
                                    sp.wait_ge(arg_ok.h, arg_ok.at(t - 1))
                                sp.dma_start(rst[:, par, :], edges(reset_add, t).partition_broadcast(P)).then_inc(rst_in[par].h, 16)
                            if known_ge(t, 3):
                                u = t - 3
                                sp.wait_ge(o_ok.h, o_ok.at(u + 1))
                                sp.dma_start(rows0[bass.ds(u * SC, SC), :].rearrange("(c p) w -> p c w", p=P),
                                             o[:, 1 - par, :, :]).then_inc(stored[1 - par].h, 16)
                        run_steps(sp, body, T, after=3)
                        for j in range(2):
                            sp.wait_ge(stored[j].h, stored[j].at(16 * T2))

                    @block.gpsimd
                    def _(pool):
                        run_steps(pool, lambda t, par, i: gather_step(pool, t, par, i, gathers, T, idx_in, (xT, qT), gathered), T)

                    @block.tensor
                    def _(pe):
                        def heads_in(t, par, i):
                            pe.wait_ge(ef_in[par].h, ef_in[par].at((i + 1) * 16))
                            if known_ge(t, 1):
                                pe.wait_ge(hid_ok.h, hid_ok.at(t))
                            nc.tensor.matmul(bH[:], w1[:], ef[:, par, :], start=True, stop=True).then_inc(h_ps.h, 1)
                            pe.wait_ge(gathered[par].h, gathered[par].at((i + 1) * (16 * 2 * CH)))
                            if known_ge(t, 1):
                                pe.wait_ge(z_ok.h, z_ok.at(t))
                            for c in range(CH):
                                mm = nc.tensor.transpose(bX[:, c * P:(c + 1) * P], gx[:, par, c, :], ident[:])
                            mm.then_inc(xT.h, 1)

                        def queries_in(t, par, i):
                            if known_ge(t, 1):
                                pe.wait_ge(qk_ok.h, qk_ok.at(t))
                            for c in range(CH):
                                mm = nc.tensor.transpose(bQ[:, c * P:(c + 1) * P], gq[:, par, c, :], ident[:])
                            mm.then_inc(qT.h, 1)

                        def contract(bankx, coef, par, pairs_of):
                            for j in pairs_of:
                                n = P if j < ZPAIRS - 1 else D
                                mm = nc.tensor.matmul(bankx[:], coef[0:n, j, :], z[0:n, par, j, :],
                                                      start=(j == 0), stop=(j == ZPAIRS - 1))
                            return mm

                        def body(t, par, i):
                            nxt = (t + 1, 1 - par, i + par)
                            mid = known_ge(t, 0) and known_lt(t, T)
                            if mid:
                                pe.wait_ge(hid_ok.h, hid_ok.at(t + 1))
                                if isinstance(t, int) and t == 1:
                                    pe.wait_ge(wv_ok.h, wv_ok.at(1))
                                if known_ge(t, 2):
                                    pe.wait_ge(o_ok.h, o_ok.at(t - 1))
                                nc.tensor.matmul(bW[:], w2[0:D, :], hid[0:D, par, :], start=True, stop=True).then_inc(wk_ps.h, 1)
                            if known_lt(t, T - 1):
                                heads_in(*nxt)
                            if mid:
                                pe.wait_ge(wk_ok.h, wk_ok.at(t + 1))
                                nc.tensor.matmul(bW[:], w2[D:P, :], hid[D:P, par, :], start=True, stop=True).then_inc(wv_ps.h, 1)
                                pe.wait_ge(z_ok.h, z_ok.at(t + 1))
                                if known_ge(t, 1):
                                    pe.wait_ge(kw_ok.h, kw_ok.at(t))
                                contract(bK, ck, par, range(ZPAIRS)).then_inc(k_ps.h, 1)
                            if known_ge(t, 1):
                                pe.wait_ge(scanned.h, scanned.at(2 * t))
                                if known_ge(t, 2):
                                    pe.wait_ge(o_ok.h, o_ok.at(t - 1))
                                if mid:
                                    pe.wait_ge(wv_ok.h, wv_ok.at(t + 1))
                                for c in range(CH):
                                    nc.tensor.transpose(bO[:, c * P:(c + 1) * P], num[:, 1 - par, c * P:(c + 1) * P], ident[:])
                                for c in range(CH):
                                    mm = nc.tensor.transpose(bW[:, c * P:(c + 1) * P], den[:, 1 - par, c * P:(c + 1) * P], ident[:])
                                mm.then_inc(o_ps.h, 1)
                            if mid:
                                if known_ge(t, 1):
                                    pe.wait_ge(val_ok.h, val_ok.at(t))
                                contract(bV, cv, par, range(2))
                                pe.wait_ge(qk_ok.h, qk_ok.at(t + 1))
                                if known_ge(t, 1):
                                    pe.wait_ge(arg_ok.h, arg_ok.at(t))
                                nc.tensor.matmul(bS[:], headsum[:], qk[:], start=True, stop=True).then_inc(s_ps.h, 1)
                                contract(bV, cv, par, range(2, ZPAIRS)).then_inc(v_ps.h, 1)
                            if known_lt(t, T - 1):
                                queries_in(*nxt)
                        run_steps(pe, body, T, before=1, after=1)

                    @block.scalar
                    def _(act):
                        def body(t, par, i):
                            mid = known_ge(t, 0) and known_lt(t, T)
                            if mid:
                                act.wait_ge(wk_ps.h, wk_ps.at(t + 1))
                                if known_ge(t, 1):
                                    act.wait_ge(kw_ok.h, kw_ok.at(t))
                                nc.scalar.activation(wk[:], bW[:], ACT.Identity, bias=b2[:, 0:1]).then_inc(wk_ok.h, 1)
                            if known_lt(t, T - 1):
                                act.wait_ge(h_ps.h, h_ps.at(t + 2))
                                if known_ge(t, 1):
                                    act.wait_ge(wv_ps.h, wv_ps.at(t))
                                nc.scalar.activation(hid[:, 1 - par, :], bH[:], ACT.Relu, bias=b1[:]).then_inc(hid_ok.h, 1)
                            if mid:
                                act.wait_ge(wv_ps.h, wv_ps.at(t + 1))
                                if known_ge(t, 1):
                                    act.wait_ge(val_ok.h, val_ok.at(t))
                                nc.scalar.activation(wv[:], bW[:], ACT.Identity, bias=b2[:, 1:2]).then_inc(wv_ok.h, 1)
                            if known_ge(t, 1):
                                act.wait_ge(o_ps.h, o_ps.at(t))
                                if known_ge(t, 3):
                                    act.wait_ge(stored[1 - par].h, stored[1 - par].at((i - 1 + par) * 16))
                                nc.scalar.activation(o[:, 1 - par, :, 0:P], bO[:].rearrange("p (c w) -> p c w", w=P), ACT.Copy)
                                nc.scalar.activation(o[:, 1 - par, :, P:W0], bW[:].rearrange("p (c h r) -> p c h r", c=CH, h=HEADS0)[:, :, :, 0],
                                                     ACT.Copy).then_inc(o_ok.h, 1)
                            if mid:
                                act.wait_ge(arg_ok.h, arg_ok.at(t + 1))
                                if known_ge(t, 2):
                                    act.wait_ge(scanned.h, scanned.at(2 * (t - 1)))
                                nc.scalar.activation(pd[:, par, :], arg[:, par, :], ACT.Exp).then_inc(pd_ok.h, 1)
                        run_steps(act, body, T, before=1, after=1)

                    @block.vector
                    def _(dve):
                        nc.vector.memset(mx[:, 1, :], -BIG).then_inc(tmp_ok.h, 1)
                        nc.vector.memset(num[:, 1, :], 0.0).then_inc(tmp_ok.h, 1)
                        nc.vector.memset(den[:, 1, :], 0.0).then_inc(tmp_ok.h, 1)
                        dve.wait_ge(tmp_ok.h, tmp_ok.at(3))
                        tmp_ok.passed(3)

                        def body(t, par, i):
                            old = 1 - par
                            mid = known_ge(t, 0) and known_lt(t, T)
                            if known_lt(t, T - 1):
                                dve.wait_ge(xT.h, xT.at(t + 2))
                                dve.wait_ge(sh_in[old].h, sh_in[old].at((i + par + 1) * 32))
                                if known_ge(t, 1):
                                    dve.wait_ge(v_ps.h, v_ps.at(t))
                                nc.vector.tensor_tensor(z[:, old, 0:ZPAIRS - 1, :], bX[:].unsqueeze(1).to_broadcast([P, ZPAIRS - 1, SC]),
                                                        sh[:, old, 0:ZPAIRS - 1, :], ALU.mult)
                                nc.vector.tensor_tensor(z[0:D, old, ZPAIRS - 1, :], bX[0:D, :], sh[0:D, old, ZPAIRS - 1, :],
                                                        ALU.mult).then_inc(z_ok.h, 1)
                            if known_ge(t, 1):
                                dve.wait_ge(pd_ok.h, pd_ok.at(t))
                                dve.wait_ge(val_ok.h, val_ok.at(t))
                                nc.vector.tensor_tensor(pv[:], pd[:, old, 0:SC], val[:, old, :], ALU.mult).then_inc(pv_ok.h, 1)
                                if known_ge(t, 3):
                                    dve.wait_ge(o_ps.h, o_ps.at(t - 2))
                                nc.vector.tensor_tensor_scan(den[:, old, :], pd[:, old, SC:2 * SC], pd[:, old, 0:SC],
                                                             den[:, par, SC - 1:SC], ALU.mult, ALU.add).then_inc(scanned.h, 1)
                                dve.wait_ge(pv_ok.h, pv_ok.at(t))
                                nc.vector.tensor_tensor_scan(num[:, old, :], pd[:, old, SC:2 * SC], pv[:],
                                                             num[:, par, SC - 1:SC], ALU.mult, ALU.add).then_inc(scanned.h, 1)
                            if mid:
                                dve.wait_ge(k_ps.h, k_ps.at(t + 1))
                                dve.wait_ge(wk_ok.h, wk_ok.at(t + 1))
                                nc.vector.tensor_tensor(kw[:], wk[:], bK[:], ALU.mult).then_inc(kw_ok.h, 1)
                                dve.wait_ge(kw_ok.h, kw_ok.at(t + 1))
                                dve.wait_ge(qT.h, qT.at(t + 1))
                                if known_ge(t, 1):
                                    dve.wait_ge(s_ps.h, s_ps.at(t))
                                nc.vector.tensor_tensor(qk[:], kw[:], bQ[:], ALU.mult).then_inc(qk_ok.h, 1)
                                dve.wait_ge(s_ps.h, s_ps.at(t + 1))
                                dve.wait_ge(rst_in[par].h, rst_in[par].at((i + 1) * 16))
                                nc.vector.tensor_copy(mx[:, par, 0:1], mx[:, old, SC:SC + 1])
                                nc.vector.tensor_tensor_scan(mx[:, par, 1:SC + 1], rst[:, par, :], bS[:],
                                                             mx[:, old, SC:SC + 1], ALU.add, ALU.max).then_inc(mx_ok.h, 1)
                                dve.wait_ge(mx_ok.h, mx_ok.at(t + 1))
                                nc.vector.tensor_tensor(arg[:, par, SC:2 * SC], mx[:, par, 0:SC], rst[:, par, :], ALU.add).then_inc(sub_ok.h, 1)
                                nc.vector.tensor_tensor(arg[:, par, 0:SC], bS[:], mx[:, par, 1:SC + 1], ALU.subtract)
                                dve.wait_ge(sub_ok.h, sub_ok.at(t + 1))
                                nc.vector.tensor_tensor(arg[:, par, SC:2 * SC], arg[:, par, SC:2 * SC], mx[:, par, 1:SC + 1],
                                                        ALU.subtract).then_inc(arg_ok.h, 1)
                                dve.wait_ge(v_ps.h, v_ps.at(t + 1))
                                dve.wait_ge(wv_ok.h, wv_ok.at(t + 1))
                                nc.vector.tensor_tensor(val[:, par, :], wv[:], bV[:], ALU.mult).then_inc(val_ok.h, 1)
                        run_steps(dve, body, T, before=1, after=1)
                for j in range(2):
                    for s, n in ((idx_in, 16), (ef_in, 16), (sh_in, 32), (rst_in, 16), (gathered, 32 * CH), (stored, 16)):
                        s[j].passed(n * T2)
                for s in (xT, qT, h_ps, hid_ok, wk_ps, wk_ok, wv_ps, wv_ok, z_ok, k_ps, v_ps, kw_ok, qk_ok, s_ps,
                          mx_ok, arg_ok, pd_ok, val_ok, pv_ok, o_ps, o_ok, sub_ok):
                    s.passed(T)
                scanned.passed(2 * T)

        def layer1_edges():
            with ExitStack() as ctx:
                aw = sb(ctx, "aw", [P, HEADS1])
                lw = sb(ctx, "lw", [P, P])
                ab = sb(ctx, "ab", [P, 1])
                pick = sb(ctx, "pick1", [P, HEADS1])
                spread = sb(ctx, "spread1", [P, 2, P])
                idx = sb(ctx, "idx1", [P, 2, 2 * CH], I32)
                gx = sb(ctx, "gx1", [P, 2, CH, 2 * D])
                pair = sb(ctx, "pair1", [P, 2, SC])
                xs = sb(ctx, "xs1", [P, 2, SC])
                rst = sb(ctx, "rst1", [P, 2, SC])
                dec = sb(ctx, "dec1", [P, 2, SC])
                lr = sb(ctx, "lr1", [P, SC])
                sc = sb(ctx, "sc1", [P, SC])
                mx = sb(ctx, "mx1", [P, 2, SC + 1])
                arg = sb(ctx, "arg1", [P, 2, 2 * SC])
                pd = sb(ctx, "pd1", [P, 2, 2 * SC])
                pv = sb(ctx, "pv1", [P, 2, SC])
                num = sb(ctx, "num1", [P, 2, 2, SC])
                den = sb(ctx, "den1", [P, 2, SC])
                o = sb(ctx, "o1", [P, 2, CH, W1])
                load_all([(aw[0:D, :], a["attn_w"][D:2 * D, :]), (aw[D:P, :], a["attn_w"][0:D, :]), (pick[:], a["pick1"]),
                          (spread[:], a["spread1"].rearrange("r (g m) -> r g m", g=2))]
                         + [(ab[32 * h:32 * (h + 1), :], a["attn_b"][h:h + 1].partition_broadcast(32)) for h in range(HEADS1)])
                bA, bL, bP0, bD0, bP1, bD1, bO0, bO1 = bank
                idx_in, rst_in, dec_in, gathered, stored = ([S(f"{n}{j}") for j in range(2)] for n in (
                    "idx_in", "rst_in", "feat_in", "gathered", "stored"))
                aT, pair_ok, xs_ok, l_ps, lr_ok, sc_ok, mx_ok, sub_ok, arg_ok = (S(n) for n in (
                    "xT", "hid_ok", "wk_ok", "s_ps", "wv_ok", "kw_ok", "mx_ok", "sub_ok", "arg_ok"))
                pd_ok, f_ps, pv_ok, den_ok, scanned, o_ps, o_ok, tmp_ok = (S(n) for n in (
                    "pd_ok", "k_ps", "pv_ok", "qk_ok", "scanned", "o_ps", "o_ok", "tmp_ok"))

                def gathers(par):
                    for j in range(CH):
                        yield gx[:, par, j, D:2 * D], tab_row, idx[:, par, j:j + 1]
                    for j in range(CH):
                        yield gx[:, par, j, 0:D], tab_row, idx[:, par, CH + j:CH + j + 1]

                with nc.Block() as block:
                    @block.sync
                    def _(sp):
                        def body(t, par, i):
                            if known_lt(t, T):
                                if known_ge(t, 2):
                                    sp.wait_ge(gathered[par].h, gathered[par].at(i * (32 * CH)))
                                sp.dma_start(idx[:, par, :], a["idx"][bass.ds(t, 1)].rearrange("t p j -> p (t j)")).then_inc(idx_in[par].h, 16)
                                if known_ge(t, 2):
                                    sp.wait_ge(lr_ok.h, lr_ok.at(t - 1))
                                sp.dma_start(dec[:, par, :], edges(decay_row, t).partition_broadcast(P)).then_inc(dec_in[par].h, 16)
                                if known_ge(t, 2):
                                    sp.wait_ge(sub_ok.h, sub_ok.at(t - 1))
                                sp.dma_start(rst[:, par, :], edges(reset_add, t).partition_broadcast(P)).then_inc(rst_in[par].h, 16)
                            if known_ge(t, 4):
                                u = t - 4
                                sp.wait_ge(o_ok.h, o_ok.at(u + 1))
                                sp.dma_start(rows1[bass.ds(u * SC, SC), :].rearrange("(c p) w -> p c w", p=P),
                                             o[:, par, :, :]).then_inc(stored[par].h, 16)
                        run_steps(sp, body, T, after=4)
                        for j in range(2):
                            sp.wait_ge(stored[j].h, stored[j].at(16 * T2))

                    @block.gpsimd
                    def _(pool):
                        run_steps(pool, lambda t, par, i: gather_step(pool, t, par, i, gathers, T, idx_in, (aT,), gathered), T)

                    @block.tensor
                    def _(pe):
                        pe.wait_ge(tmp_ok.h, tmp_ok.at(1))

                        def turn_in(t, par, i):
                            pe.wait_ge(gathered[par].h, gathered[par].at((i + 1) * (32 * CH)))
                            if known_ge(t, 1):
                                pe.wait_ge(pair_ok.h, pair_ok.at(t))
                            for c in range(CH):
                                mm = nc.tensor.transpose(bA[:, c * P:(c + 1) * P], gx[:, par, c, :], ident[:])
                            mm.then_inc(aT.h, 1)

                        def body(t, par, i):
                            old = 1 - par
                            if known_ge(t, 0) and known_lt(t, T):
                                pe.wait_ge(pair_ok.h, pair_ok.at(t + 1))
                                if isinstance(t, int) and t in (1, 2):
                                    pe.wait_ge(lr_ok.h, lr_ok.at(t))
                                if known_ge(t, 3):
                                    pe.wait_ge(o_ok.h, o_ok.at(t - 2))
                                nc.tensor.matmul(bL[:], lw[:], pair[:, par, :], start=True, stop=True).then_inc(l_ps.h, 1)
                            if known_ge(t, 1) and known_lt(t, T + 1):
                                pe.wait_ge(pd_ok.h, pd_ok.at(t))
                                if known_ge(t, 2):
                                    pe.wait_ge(scanned.h, scanned.at(2 * (t - 1)))
                                for g, bp, bd in ((0, bP0, bD0), (1, bP1, bD1)):
                                    nc.tensor.matmul(bp[:], spread[:, g, :], pd[:, old, 0:SC], start=True, stop=True)
                                    mm = nc.tensor.matmul(bd[:], spread[:, g, :], pd[:, old, SC:2 * SC], start=True, stop=True)
                                mm.then_inc(f_ps.h, 1)
                            if known_lt(t, T - 1):
                                turn_in(t + 1, old, i + par)
                            if known_ge(t, 2):
                                pe.wait_ge(scanned.h, scanned.at(2 * (t - 1)))
                                pe.wait_ge(den_ok.h, den_ok.at(t - 1))
                                if known_lt(t, T):
                                    pe.wait_ge(lr_ok.h, lr_ok.at(t + 1))
                                if known_ge(t, 3):
                                    pe.wait_ge(o_ok.h, o_ok.at(t - 2))
                                for c in range(CH):
                                    nc.tensor.matmul(bL[:, c * HEADS1:(c + 1) * HEADS1], den[:, par, c * P:(c + 1) * P], pick[:],
                                                     start=True, stop=True)
                                for g, b in ((0, bO0), (1, bO1)):
                                    for c in range(CH):
                                        mm = nc.tensor.transpose(b[:, c * P:(c + 1) * P], num[:, par, g, c * P:(c + 1) * P], ident[:])
                                mm.then_inc(o_ps.h, 1)
                        run_steps(pe, body, T, before=1, after=2)

                    @block.scalar
                    def _(act):
                        def body(t, par, i):
                            mid = known_ge(t, 0) and known_lt(t, T)
                            if mid:
                                act.wait_ge(pair_ok.h, pair_ok.at(t + 1))
                                if known_ge(t, 2):
                                    act.wait_ge(pv_ok.h, pv_ok.at(t - 1))
                                nc.scalar.activation(xs[0:D, par, :], pair[D:P, par, :], ACT.Copy)
                                nc.scalar.activation(xs[D:P, par, :], pair[D:P, par, :], ACT.Copy).then_inc(xs_ok.h, 1)
                            if known_lt(t, T - 1):
                                act.wait_ge(aT.h, aT.at(t + 2))
                                if known_ge(t, 1):
                                    act.wait_ge(l_ps.h, l_ps.at(t))
                                    act.wait_ge(xs_ok.h, xs_ok.at(t))
                                nc.scalar.activation(pair[:, 1 - par, :], bA[:], ACT.Copy).then_inc(pair_ok.h, 1)
                            if known_ge(t, 2):
                                act.wait_ge(o_ps.h, o_ps.at(t - 1))
                                if known_ge(t, 4):
                                    act.wait_ge(stored[par].h, stored[par].at((i - 1) * 16))
                                nc.scalar.activation(o[:, par, :, 2 * P:W1], bL[:, 0:CH * HEADS1].rearrange("p (c w) -> p c w", w=HEADS1), ACT.Copy)
                                for g, b in ((0, bO0), (1, bO1)):
                                    ins = nc.scalar.activation(o[:, par, :, g * P:(g + 1) * P], b[:].rearrange("p (c w) -> p c w", w=P), ACT.Copy)
                                ins.then_inc(o_ok.h, 1)
                            if mid:
                                act.wait_ge(arg_ok.h, arg_ok.at(t + 1))
                                if known_ge(t, 2):
                                    act.wait_ge(f_ps.h, f_ps.at(t - 1))
                                    act.wait_ge(den_ok.h, den_ok.at(t - 1))
                                nc.scalar.activation(pd[:, par, :], arg[:, par, :], ACT.Exp).then_inc(pd_ok.h, 1)
                        run_steps(act, body, T, before=1, after=2)

                    @block.vector
                    def _(dve):
                        for h in range(HEADS1):
                            ins = nc.vector.tensor_copy(lw[:, 32 * h:32 * (h + 1)], aw[:, h:h + 1].to_broadcast([P, 32]))
                        ins.then_inc(tmp_ok.h, 1)
                        nc.vector.memset(mx[:, 1], -BIG).then_inc(tmp_ok.h, 1)
                        nc.vector.memset(num[:, 1], 0.0).then_inc(tmp_ok.h, 1)
                        nc.vector.memset(den[:, 1], 0.0).then_inc(tmp_ok.h, 1)
                        dve.wait_ge(tmp_ok.h, tmp_ok.at(4))

                        def body(t, par, i):
                            old = 1 - par
                            if known_ge(t, 1):
                                dve.wait_ge(pd_ok.h, pd_ok.at(t))
                                if known_ge(t, 3):
                                    dve.wait_ge(o_ps.h, o_ps.at(t - 2))
                                nc.vector.tensor_tensor_scan(den[:, old, :], pd[:, old, SC:2 * SC], pd[:, old, 0:SC],
                                                             den[:, par, SC - 1:SC], ALU.mult, ALU.add).then_inc(den_ok.h, 1)
                            if known_ge(t, 0) and known_lt(t, T):
                                dve.wait_ge(l_ps.h, l_ps.at(t + 1))
                                dve.wait_ge(dec_in[par].h, dec_in[par].at((i + 1) * 16))
                                nc.vector.scalar_tensor_tensor(out=lr[:], in0=bL[:], scalar=ab[:], in1=dec[:, par, :],
                                                               op0=ALU.add, op1=ALU.mult).then_inc(lr_ok.h, 1)
                                nc.vector.tensor_copy(mx[:, par, 0:1], mx[:, old, SC:SC + 1])
                                dve.wait_ge(lr_ok.h, lr_ok.at(t + 1))
                                nc.vector.scalar_tensor_tensor(out=sc[:], in0=lr[:], scalar=0.2, in1=lr[:],
                                                               op0=ALU.mult, op1=ALU.max).then_inc(sc_ok.h, 1)
                                dve.wait_ge(rst_in[par].h, rst_in[par].at((i + 1) * 16))
                                dve.wait_ge(sc_ok.h, sc_ok.at(t + 1))
                                nc.vector.tensor_tensor_scan(mx[:, par, 1:SC + 1], rst[:, par, :], sc[:],
                                                             mx[:, old, SC:SC + 1], ALU.add, ALU.max).then_inc(mx_ok.h, 1)
                                dve.wait_ge(mx_ok.h, mx_ok.at(t + 1))
                                nc.vector.tensor_tensor(arg[:, par, SC:2 * SC], mx[:, par, 0:SC], rst[:, par, :], ALU.add).then_inc(sub_ok.h, 1)
                                nc.vector.tensor_tensor(arg[:, par, 0:SC], sc[:], mx[:, par, 1:SC + 1], ALU.subtract)
                                dve.wait_ge(sub_ok.h, sub_ok.at(t + 1))
                                nc.vector.tensor_tensor(arg[:, par, SC:2 * SC], arg[:, par, SC:2 * SC], mx[:, par, 1:SC + 1],
                                                        ALU.subtract).then_inc(arg_ok.h, 1)
                            if known_ge(t, 1):
                                dve.wait_ge(f_ps.h, f_ps.at(t))
                                dve.wait_ge(xs_ok.h, xs_ok.at(t))
                                for g, bp in ((0, bP0), (1, bP1)):
                                    ins = nc.vector.tensor_tensor(pv[:, g, :], bp[:], xs[:, old, :], ALU.mult)
                                ins.then_inc(pv_ok.h, 1)
                                dve.wait_ge(pv_ok.h, pv_ok.at(t))
                                for g, bd in ((0, bD0), (1, bD1)):
                                    nc.vector.tensor_tensor_scan(num[:, old, g, :], bd[:], pv[:, g, :],
                                                                 num[:, par, g, SC - 1:SC], ALU.mult, ALU.add).then_inc(scanned.h, 1)
                        run_steps(dve, body, T, after=1)
                tmp_ok.passed(4)
                for j in range(2):
                    for s, n in ((idx_in, 16), (dec_in, 16), (rst_in, 16), (gathered, 32 * CH), (stored, 16)):
                        s[j].passed(n * T2)
                for s in (aT, pair_ok, xs_ok, l_ps, lr_ok, sc_ok, mx_ok, sub_ok, arg_ok, pd_ok, f_ps, pv_ok, den_ok, o_ps, o_ok):
                    s.passed(T)
                scanned.passed(2 * T)

        def layer2_edges(layer):
            with ExitStack() as ctx:
                idx = sb(ctx, f"idx2_{layer}", [P, 2, 2 * CH], I32)
                gx = sb(ctx, f"gx2_{layer}", [P, 2, CH, 2 * D])
                keep = sb(ctx, f"keep2_{layer}", [P, 2, SC])
                sums = sb(ctx, f"sums2_{layer}", [P, 2, SC])
                o = sb(ctx, f"o2_{layer}", [P, 2, CH, 2 * D])
                idx_in, keep_in, gathered, stored = ([S(f"{n}{j}") for j in range(2)] for n in (
                    "idx_in", "rst_in", "gathered", "stored"))
                xT, scanned, o_ps, o_ok, tmp_ok = (S(n) for n in ("xT", "scanned", "o_ps", "o_ok", "tmp_ok"))

                def gathers(par):
                    for j in range(CH):
                        for half in range(2):
                            yield gx[:, par, j, half * D:(half + 1) * D], tab_row, idx[:, par, half * CH + j:half * CH + j + 1]

                with nc.Block() as block:
                    @block.sync
                    def _(sp):
                        def body(t, par, i):
                            if known_lt(t, T2):
                                if known_ge(t, 2):
                                    sp.wait_ge(gathered[par].h, gathered[par].at(i * (32 * CH)))
                                sp.dma_start(idx[:, par, :], a["idx_halves"][bass.ds(t, 1)].rearrange("t p j -> p (t j)")).then_inc(idx_in[par].h, 16)
                                if known_ge(t, 2):
                                    sp.wait_ge(scanned.h, scanned.at(t - 1))
                                sp.dma_start(keep[0:D, par, :], edges(keep_mul, t).partition_broadcast(D)).then_inc(keep_in[par].h, 16)
                                sp.dma_start(keep[D:P, par, :], edges(keep_mul, t + T2).partition_broadcast(D)).then_inc(keep_in[par].h, 16)
                            if known_ge(t, 3):
                                u = t - 3
                                sp.wait_ge(o_ok.h, o_ok.at(u + 1))
                                sp.dma_start(rows2[bass.ds(u * SC, SC), :].rearrange("(c p) w -> p c w", p=P),
                                             o[:, 1 - par, :, :]).then_inc(stored[1 - par].h, 16)
                        run_steps(sp, body, T2, after=3)
                        for j in range(2):
                            sp.wait_ge(stored[j].h, stored[j].at(8 * T2))

                    @block.gpsimd
                    def _(pool):
                        run_steps(pool, lambda t, par, i: gather_step(pool, t, par, i, gathers, T2, idx_in, (xT,), gathered), T2)

                    @block.tensor
                    def _(pe):
                        def body(t, par, i):
                            if known_lt(t, T2):
                                pe.wait_ge(gathered[par].h, gathered[par].at((i + 1) * (32 * CH)))
                                if known_ge(t, 2):
                                    pe.wait_ge(scanned.h, scanned.at(t - 1))
                                for c in range(CH):
                                    mm = nc.tensor.transpose(bank[par][:, c * P:(c + 1) * P], gx[:, par, c, :], ident[:])
                                mm.then_inc(xT.h, 1)
                            if known_ge(t, 1):
                                pe.wait_ge(scanned.h, scanned.at(t))
                                if known_ge(t, 3):
                                    pe.wait_ge(o_ok.h, o_ok.at(t - 2))
                                for c in range(CH):
                                    mm = nc.tensor.transpose(bank[3 - par][:, c * P:(c + 1) * P], sums[:, 1 - par, c * P:(c + 1) * P], ident[:])
                                mm.then_inc(o_ps.h, 1)
                        run_steps(pe, body, T2, after=1)

                    @block.vector
                    def _(dve):
                        nc.vector.memset(sums[:, 1, :], 0.0).then_inc(tmp_ok.h, 1)
                        dve.wait_ge(tmp_ok.h, tmp_ok.at(1))

                        def body(t, par, i):
                            dve.wait_ge(xT.h, xT.at(t + 1))
                            dve.wait_ge(keep_in[par].h, keep_in[par].at((i + 1) * 32))
                            if known_ge(t, 2):
                                dve.wait_ge(o_ps.h, o_ps.at(t - 1))
                            if known_ge(t, 1):
                                dve.wait_ge(scanned.h, scanned.at(t))
                            nc.vector.tensor_tensor_scan(sums[:, par, :], keep[:, par, :], bank[par][:],
                                                         sums[:, 1 - par, SC - 1:SC], ALU.mult, ALU.add).then_inc(scanned.h, 1)
                        run_steps(dve, body, T2)

                    @block.scalar
                    def _(act):
                        def body(t, par, i):
                            act.wait_ge(o_ps.h, o_ps.at(t + 1))
                            if known_ge(t, 2):
                                act.wait_ge(stored[par].h, stored[par].at(i * 16))
                            nc.scalar.activation(o[:, par, :, :], bank[2 + par][:].rearrange("p (c w) -> p c w", w=P),
                                                 ACT.Copy).then_inc(o_ok.h, 1)
                        run_steps(act, body, T2)
                tmp_ok.passed(1)
                for j in range(2):
                    for s, n in ((idx_in, 16), (keep_in, 32), (gathered, 32 * CH), (stored, 16)):
                        s[j].passed(n * T2 // 2)
                for s in (xT, scanned, o_ps, o_ok):
                    s.passed(T2)

        def layer3_edges():
            EF = 32
            with ExitStack() as ctx:
                wab = sb(ctx, "wab3", [P, HID])
                wc = sb(ctx, "wc3", [EF + 1, HID])
                gb = sb(ctx, "gb3", [P, 2])
                cut = sb(ctx, "cut3", [P, 2])
                half_neg = sb(ctx, "half_neg3", [P, CH])
                idx = sb(ctx, "idx3", [P, 2, 2 * CH], I32)
                gx = sb(ctx, "gx3", [P, 2, CH, 2 * D])
                ea = sb(ctx, "ea3", [EF + 1, 2, SC])
                hold = sb(ctx, "hold3", [P, 2, SC])
                keep = sb(ctx, "keep3", [P, 2, SC])
                pair = sb(ctx, "pair3", [P, 2, SC])
                sq = sb(ctx, "sq3", [P, 2, SC])
                ssum = sb(ctx, "ssum3", [P, 2, CH])
                var = sb(ctx, "var3", [P, 2, CH])
                rstd = sb(ctx, "rstd3", [P, 2, CH])
                nrm = sb(ctx, "nrm3", [P, 2, SC])
                si = sb(ctx, "si3", [P, 2, SC])
                sums = sb(ctx, "sums3", [P, 2, SC])
                o = sb(ctx, "o3", [P, 2, CH, HID])
                load_all([(wab[:], a["W_msg1"][0:2 * D, :]), (wc[0:EF, :], a["W_msg1"][2 * D:2 * D + EF, :]),
                          (wc[EF:EF + 1, :], a["b_msg1"]), (gb[:, 0:1], a["g_msg"]), (gb[:, 1:2], a["be_msg"])])
                with nc.Block() as block:
                    @block.vector
                    def _(dve):
                        for w, n, k in ((wab, P, 0), (wc, EF + 1, 1)):
                            chain(dve, nc.vector.reduce_sum(cut[0:n, k:k + 1], w[:], AX_X))
                            chain(dve, nc.vector.tensor_scalar(cut[0:n, k:k + 1], cut[0:n, k:k + 1], 1.0 / HID, None, ALU.mult))
                            chain(dve, nc.vector.tensor_scalar(w[:], w[:], cut[0:n, k:k + 1], None, ALU.subtract))
                        chain(dve, nc.vector.memset(half_neg[:], -0.5))
                        chain(dve, nc.vector.memset(ea[EF:EF + 1, :, :], 1.0))
                        chain(dve, nc.vector.memset(sums[:, 1, :], 0.0))
                        chain(dve, nc.vector.memset(pair[D:P, 1, :], 0.0))
                bA, bH, bT, bO = (bank[2 * k:2 * k + 2] for k in range(4))
                idx_in, ea_in, hold_in, keep_in, dst_in, gathered, stored = ([S(f"{n}{j}") for j in range(2)] for n in (
                    "idx_in", "feat_in", "hold_in", "rst_in", "sh_in", "gathered", "stored"))
                aT, src_ok, dst_ok, h_ps, sq_ok, ssum_ok, var_ok, rstd_ok, nrm_ok = (S(n) for n in (
                    "xT", "hid_ok", "z_ok", "h_ps", "wk_ok", "v_ps", "wv_ok", "pd_ok", "kw_ok"))
                t_ps, si_ok, scanned, o_ps, o_ok = (S(n) for n in ("k_ps", "pv_ok", "scanned", "o_ps", "o_ok"))

                def gathers(par):
                    for j in range(CH):
                        yield gx[:, par, j, 0:D], tab_row, idx[:, par, j:j + 1]

                with nc.Block() as block:
                    @block.sync
                    def _(sp):
                        def body(t, par, i):
                            old = 1 - par
                            if known_lt(t, T - 1):
                                if known_ge(t, 1):
                                    sp.wait_ge(gathered[old].h, gathered[old].at((i + par) * (16 * CH)))
                                sp.dma_start(idx[:, old, :], a["idx"][bass.ds(t + 1, 1)].rearrange("t p j -> p (t j)")).then_inc(idx_in[old].h, 16)
                                if known_ge(t, 1):
                                    sp.wait_ge(aT.h, aT.at(t))
                                    nc.sync.sem_inc(S("sp_turn").h, 1)
                                sp.dma_start(gx[:, old, :, D:2 * D], dst_first[bass.ds(t * SC + SC, SC), :].rearrange("(c p) w -> p c w", p=P)
                                             ).then_inc(dst_in[old].h, 16)
                                if known_ge(t, 1):
                                    sp.wait_ge(dst_ok.h, dst_ok.at(t))
                                    nc.sync.sem_inc(S("sp_turn").h, 1)
                                sp.dma_start(hold[D:P, old, :], edges(keep_mul, t + 1).partition_broadcast(D)).then_inc(hold_in[old].h, 16)
                            if known_ge(t, 0) and known_lt(t, T):
                                if known_ge(t, 2):
                                    sp.wait_ge(h_ps.h, h_ps.at(t - 1))
                                    nc.sync.sem_inc(S("sp_turn").h, 1)
                                sp.dma_start(ea[0:EF, par, :], a["ea"][:, bass.ds(t * SC, SC)]).then_inc(ea_in[par].h, 16)
                            if known_ge(t, 3):
                                u = t - 3
                                if known_ge(t, 5):
                                    sp.wait_ge(scanned.h, scanned.at(t - 4))
                                sp.dma_start(keep[:, old, :], edges(keep_mul, u).partition_broadcast(P)).then_inc(keep_in[old].h, 16)
                            if known_ge(t, 5):
                                u = t - 5
                                sp.wait_ge(o_ok.h, o_ok.at(u + 1))
                                sp.dma_start(rows3[bass.ds(u * SC, SC), :].rearrange("(c p) w -> p c w", p=P),
                                             o[:, old, :, :]).then_inc(stored[old].h, 16)
                        run_steps(sp, body, T, before=1, after=3, first=6)
                        for u in (T - 2, T - 1):
                            sp.wait_ge(o_ok.h, o_ok.at(u + 1))
                            sp.dma_start(rows3[u * SC:(u + 1) * SC, :].rearrange("(c p) w -> p c w", p=P),
                                         o[:, u % 2, :, :]).then_inc(stored[u % 2].h, 16)
                        for j in range(2):
                            sp.wait_ge(stored[j].h, stored[j].at(16 * T2))

                    @block.gpsimd
                    def _(pool):
                        def body(t, par, i):
                            old = 1 - par
                            gather_step(pool, t, par, i, gathers, T, idx_in, (aT,), gathered)
                            if known_ge(t, 3):
                                pool.wait_ge(var_ok.h, var_ok.at(t - 2))
                                if known_ge(t, 5):
                                    pool.wait_ge(nrm_ok.h, nrm_ok.at(t - 4))
                                nc.gpsimd.tensor_tensor(rstd[:, old, :], var[:, old, :], half_neg[:], ALU.pow).then_inc(rstd_ok.h, 1)
                        run_steps(pool, body, T, after=3, first=6)

                    @block.tensor
                    def _(pe):
                        def body(t, par, i):
                            old = 1 - par
                            if known_lt(t, T - 1):
                                pe.wait_ge(gathered[old].h, gathered[old].at((i + par + 1) * (16 * CH)))
                                pe.wait_ge(dst_in[old].h, dst_in[old].at((i + par + 1) * 16))
                                if known_ge(t, 1):
                                    pe.wait_ge(src_ok.h, src_ok.at(t))
                                    pe.wait_ge(dst_ok.h, dst_ok.at(t))
                                for c in range(CH):
                                    mm = nc.tensor.transpose(bA[old][:, c * P:(c + 1) * P], gx[:, old, c, :], ident[:])
                                mm.then_inc(aT.h, 1)
                            if known_ge(t, 2) and known_lt(t, T + 2):
                                pe.wait_ge(nrm_ok.h, nrm_ok.at(t - 1))
                                if known_ge(t, 4):
                                    pe.wait_ge(si_ok.h, si_ok.at(t - 3))
                                for c in range(CH):
                                    mm = nc.tensor.transpose(bT[par][:, c * P:(c + 1) * P], nrm[:, par, c * P:(c + 1) * P], ident[:])
                                mm.then_inc(t_ps.h, 1)
                            if known_ge(t, 0) and known_lt(t, T):
                                pe.wait_ge(src_ok.h, src_ok.at(t + 1))
                                pe.wait_ge(dst_ok.h, dst_ok.at(t + 1))
                                pe.wait_ge(ea_in[par].h, ea_in[par].at((i + 1) * 16))
                                if known_ge(t, 2):
                                    pe.wait_ge(nrm_ok.h, nrm_ok.at(t - 1))
                                for c in range(CH):
                                    cut_c = slice(c * P, (c + 1) * P)
                                    nc.tensor.matmul(bH[par][:, cut_c], pair[:, par, cut_c], wab[:], start=True, stop=False)
                                    mm = nc.tensor.matmul(bH[par][:, cut_c], ea[:, par, cut_c], wc[:], start=False, stop=True)
                                mm.then_inc(h_ps.h, 1)
                            if known_ge(t, 3):
                                pe.wait_ge(scanned.h, scanned.at(t - 2))
                                if known_ge(t, 5):
                                    pe.wait_ge(o_ok.h, o_ok.at(t - 4))
                                for c in range(CH):
                                    mm = nc.tensor.transpose(bO[old][:, c * P:(c + 1) * P], sums[:, old, c * P:(c + 1) * P], ident[:])
                                mm.then_inc(o_ps.h, 1)
                        run_steps(pe, body, T, before=1, after=3, first=6)

                    @block.scalar
                    def _(act):
                        def body(t, par, i):
                            old = 1 - par
                            if known_ge(t, 1) and known_lt(t, T + 1):
                                act.wait_ge(h_ps.h, h_ps.at(t))
                                if known_ge(t, 3):
                                    act.wait_ge(ssum_ok.h, ssum_ok.at(t - 2))
                                nc.scalar.activation(sq[:, old, :], bH[old][:], ACT.Square).then_inc(sq_ok.h, 1)
                            if known_ge(t, 4):
                                act.wait_ge(o_ps.h, o_ps.at(t - 3))
                                if known_ge(t, 6):
                                    act.wait_ge(stored[par].h, stored[par].at((i - 2) * 16))
                                nc.scalar.activation(o[:, par, :, :], bO[par][:].rearrange("p (c w) -> p c w", w=P), ACT.Copy).then_inc(o_ok.h, 1)
                            if known_lt(t, T - 1):
                                act.wait_ge(aT.h, aT.at(t + 2))
                                if known_ge(t, 1):
                                    act.wait_ge(h_ps.h, h_ps.at(t))
                                nc.scalar.activation(pair[0:D, old, :], bA[old][0:D, :], ACT.Copy).then_inc(src_ok.h, 1)
                            if known_ge(t, 2) and known_lt(t, T + 2):
                                act.wait_ge(t_ps.h, t_ps.at(t - 1))
                                if known_ge(t, 4):
                                    act.wait_ge(scanned.h, scanned.at(t - 3))
                                nc.scalar.activation(si[:, par, :], bT[par][:], ACT.Silu, scale=gb[:, 0:1], bias=gb[:, 1:2]).then_inc(si_ok.h, 1)
                        run_steps(act, body, T, before=1, after=4, first=6)

                    @block.vector
                    def _(dve):
                        def body(t, par, i):
                            old = 1 - par
                            if known_ge(t, 2) and known_lt(t, T + 2):
                                dve.wait_ge(rstd_ok.h, rstd_ok.at(t - 1))
                                if known_ge(t, 4):
                                    dve.wait_ge(t_ps.h, t_ps.at(t - 3))
                                nc.vector.tensor_tensor(nrm[:, par, :].rearrange("p (c w) -> p c w", w=P),
                                                        bH[par][:].rearrange("p (c w) -> p c w", w=P),
                                                        rstd[:, par, :].unsqueeze(2).to_broadcast([P, CH, P]), ALU.mult).then_inc(nrm_ok.h, 1)
                            if known_ge(t, 1) and known_lt(t, T + 1):
                                dve.wait_ge(sq_ok.h, sq_ok.at(t))
                                nc.vector.reduce_sum(ssum[:, old, :], sq[:, old, :].rearrange("p (c w) -> p c w", w=P), AX_X).then_inc(ssum_ok.h, 1)
                                dve.wait_ge(ssum_ok.h, ssum_ok.at(t))
                                if known_ge(t, 3):
                                    dve.wait_ge(rstd_ok.h, rstd_ok.at(t - 2))
                                nc.vector.tensor_scalar(var[:, old, :], ssum[:, old, :], 1.0 / HID, EPS, ALU.mult, ALU.add).then_inc(var_ok.h, 1)
                            if known_lt(t, T - 1):
                                dve.wait_ge(aT.h, aT.at(t + 2))
                                dve.wait_ge(hold_in[old].h, hold_in[old].at((i + par + 1) * 16))
                                if known_ge(t, 1):
                                    dve.wait_ge(h_ps.h, h_ps.at(t))
                                if known_ge(t, 0):
                                    dve.wait_ge(dst_ok.h, dst_ok.at(t + 1))
                                nc.vector.tensor_tensor_scan(pair[D:P, old, :], hold[D:P, old, :], bA[old][D:P, :],
                                                             pair[D:P, par, SC - 1:SC], ALU.mult, ALU.add).then_inc(dst_ok.h, 1)
                            if known_ge(t, 3):
                                dve.wait_ge(si_ok.h, si_ok.at(t - 2))
                                dve.wait_ge(keep_in[old].h, keep_in[old].at((i + par - 1) * 16))
                                if known_ge(t, 5):
                                    dve.wait_ge(o_ps.h, o_ps.at(t - 4))
                                if known_ge(t, 4):
                                    dve.wait_ge(scanned.h, scanned.at(t - 3))
                                nc.vector.tensor_tensor_scan(sums[:, old, :], keep[:, old, :], si[:, old, :],
                                                             sums[:, par, SC - 1:SC], ALU.mult, ALU.add).then_inc(scanned.h, 1)
                        run_steps(dve, body, T, before=1, after=3, first=6)
                for j in range(2):
                    for s, n in ((idx_in, 16), (ea_in, 16), (hold_in, 16), (keep_in, 16), (dst_in, 16), (gathered, 16 * CH), (stored, 16)):
                        s[j].passed(n * T2)
                for s in (aT, src_ok, dst_ok, h_ps, sq_ok, ssum_ok, var_ok, rstd_ok, nrm_ok, t_ps, si_ok, scanned, o_ps, o_ok):
                    s.passed(T)

        def vector_step(*ops):
            with nc.Block() as block:
                @block.vector
                def _(dve):
                    for op in ops:
                        chain(dve, op())

        def add_back(bT):
            turn([(bT, tmp_n[:, :, 0:D], D, True)])
            vector_step(lambda: nc.vector.tensor_tensor(xn[:], xn[:], tmp_n[:, :, 0:D], ALU.add))

        prepare()

        pre_norm()
        turn([(hn[:], hT[:], D, False)])
        with ExitStack() as ctx:
            wq = sb(ctx, "wq", [D, P])
            load_all([(wq[:], a["Wq"])])
            product_rows([(hT[:], wq[:])], P, tmp_n[:])
            store_tables([(node_rows(tab_q, P), tmp_n[:]), (node_rows(tab_dup, 2 * D)[:, :, 0:D], hn[:]),
                          (node_rows(tab_dup, 2 * D)[:, :, D:2 * D], hn[:])])
        layer0_edges()
        with ExitStack() as ctx:
            g0 = sb(ctx, "g0", [P, NB, W0])
            rden = sb(ctx, "rden0", [P, NB, HEADS0])
            upd = sb(ctx, "upd0", [P, NB, P])
            updT = sb(ctx, "updT0", [P, NP])
            sumT = sb(ctx, "sumT0", [D, NP])
            bnT = sb(ctx, "bnT0", [D, NP])
            scT = sb(ctx, "scT0", [D, NP])
            w_out = sb(ctx, "w_out0", [P, D])
            w_self = sb(ctx, "w_self0", [D, D])
            gb = sb(ctx, "gb0", [D, 2])
            load_all([(w_out[:], a["W_out"]), (w_self[:], a["W_self"]), (gb[:, 0:1], a["gamma0"]), (gb[:, 1:2], a["beta0"])])
            read_rows([(rows0, last_row, g0)])
            vector_step(
                lambda: nc.vector.tensor_scalar(rden[:], g0[:, :, P:W0], 1e-16, None, ALU.add),
                lambda: nc.vector.reciprocal(rden[:], rden[:]),
                *[(lambda h=h: nc.vector.tensor_tensor(
                    upd[:, :, h * DH0:(h + 1) * DH0], g0[:, :, h * DH0:(h + 1) * DH0],
                    rden[:, :, h:h + 1].to_broadcast([P, NB, DH0]), ALU.mult)) for h in range(HEADS0)])
            turn([(upd[:], updT[:], P, False)])
            product_T([(w_out[:], updT[:]), (w_self[:], hT[:])], D, sumT[:])
            batch_norm(sumT[:], gb[:, 0:1], gb[:, 1:2], bnT[:], scT[:])
            add_back(bnT[:])

        pre_norm()
        turn([(hn[:], hT[:], D, False)])
        with ExitStack() as ctx:
            ww = sb(ctx, "ww", [D, D])
            wb = sb(ctx, "wb", [P, D])
            load_all([(ww[:], a["W_w"]), (wb[:], a["W_b"].partition_broadcast(P))])
            product_rows([(hT[:], ww[:])], D, tmp_n[:, :, 0:D], bias=wb[:])
            store_tables([(node_rows(tab_row, D), tmp_n[:, :, 0:D])])
        layer1_edges()
        with ExitStack() as ctx:
            g1 = sb(ctx, "g1", [P, NB, W1])
            rden = sb(ctx, "rden1", [P, NB, HEADS1])
            aggT = [sb(ctx, f"aggT1{g}", [P, NP]) for g in range(2)]
            sumT = sb(ctx, "sumT1", [D, NP])
            pw = sb(ctx, "pw1", [P, 2, D])
            rows = sb(ctx, "brow1", [P, 3, D])
            zc = sb(ctx, "zc1", [P, NB, D])
            load_all([(pw[:, g, :], a["proj_w"][g * P:(g + 1) * P, :]) for g in range(2)]
                     + [(rows[:, k, :], a[n].partition_broadcast(P)) for k, n in enumerate(("proj_b", "ln_g", "ln_b"))])
            read_rows([(rows1, last_row, g1)])
            vector_step(
                lambda: nc.vector.tensor_scalar(rden[:], g1[:, :, 2 * P:W1], 1e-8, None, ALU.add),
                lambda: nc.vector.reciprocal(rden[:], rden[:]),
                *[(lambda h=h: nc.vector.tensor_tensor(
                    g1[:, :, h * D:(h + 1) * D], g1[:, :, h * D:(h + 1) * D],
                    rden[:, :, h:h + 1].to_broadcast([P, NB, D]), ALU.mult)) for h in range(HEADS1)])
            turn([(g1[:, :, g * P:(g + 1) * P], aggT[g][:], P, False) for g in range(2)])
            product_T([(pw[:, g, :], aggT[g][:]) for g in range(2)], D, sumT[:])
            turn([(sumT[:], tmp_n[:, :, 0:D], D, True)])
            row = lambda k: rows[:, k, :].unsqueeze(1).to_broadcast([P, NB, D])
            rs_sem, sd_sem = S("var_ready"), S("root_ready")
            with nc.Block() as block:
                @block.vector
                def _(dve):
                    z1 = tmp_n[:, :, 0:D]
                    chain(dve, nc.vector.tensor_tensor(z1, z1, row(0), ALU.add))
                    chain(dve, nc.vector.tensor_tensor(z1, z1, hn[:], ALU.add))
                    norm_rows(dve, z1, D, zc[:], tmp_n[:, :, D:2 * D], rs_sem, sd_sem)
                    chain(dve, nc.vector.tensor_tensor(zc[:], zc[:], row(1), ALU.mult))
                    chain(dve, nc.vector.tensor_tensor(zc[:], zc[:], row(2), ALU.add))
                    chain(dve, nc.vector.tensor_scalar(zc[:], zc[:], 0.0, None, ALU.max))
                    nc.vector.tensor_tensor(xn[:], xn[:], zc[:], ALU.add)

                @block.scalar
                def _(act):
                    root(act, rs_sem, sd_sem)
            rs_sem.passed(1)
            sd_sem.passed(1)

        pre_norm()
        with ExitStack() as ctx:
            w12 = sb(ctx, "w12", [D, 6, D])
            gb = sb(ctx, "gb2", [D, 6])
            scale = sb(ctx, "scale2", [P, 3])
            agg = sb(ctx, "agg2", [P, NB, D])
            more = sb(ctx, "more2", [P, NB, D])
            carry = sb(ctx, "carry2", [P, D])
            zT = sb(ctx, "zT2", [D, NP])
            uT = sb(ctx, "uT2", [D, NP])
            load_all([(w12[:, 0:3, :], a["W1T"].rearrange("l i o -> i l o")), (w12[:, 3:6, :], a["W2T"].rearrange("l i o -> i l o")),
                      (gb[:, 0:3], a["gamma2"]), (gb[:, 3:6], a["beta2"]), (scale[:], a["eps2"].partition_broadcast(P))])
            vector_step(lambda: nc.vector.tensor_scalar(scale[:], scale[:], 1.0, None, ALU.add))
            for layer in range(3):
                store_tables([(node_rows(tab_row, D), hn[:])])
                layer2_edges(layer)
                halves = rows2.rearrange("e (h w) -> (e h) w", h=2)
                read_rows([(halves, last_row2, agg)])
                load_all([(carry[:], halves[EP - 2:EP - 1, :].rearrange("r w -> (r w)").partition_broadcast(P))])
                vector_step(
                    lambda: nc.vector.tensor_tensor(more[:], carry[:].unsqueeze(1).to_broadcast([P, NB, D]),
                                                    crosses[:].unsqueeze(2).to_broadcast([P, NB, D]), ALU.mult),
                    lambda: nc.vector.tensor_tensor(agg[:], agg[:], more[:], ALU.add),
                    lambda: nc.vector.scalar_tensor_tensor(out=agg[:], in0=hn[:], scalar=scale[:, layer:layer + 1], in1=agg[:],
                                                           op0=ALU.mult, op1=ALU.add))
                turn([(agg[:], zT[:], D, False)])
                product_T([(w12[:, layer, :], zT[:])], D, uT[:], ACT.Relu)
                product_T([(w12[:, 3 + layer, :], uT[:])], D, zT[:], ACT.Relu)
                batch_norm(zT[:], gb[:, layer:layer + 1], gb[:, 3 + layer:4 + layer], uT[:], hT[:])
                turn([(uT[:], hn[:], D, True)])
            vector_step(lambda: nc.vector.tensor_tensor(xn[:], xn[:], hn[:], ALU.add))

        pre_norm()
        turn([(hn[:], hT[:], D, False)])
        store_tables([(node_rows(tab_row, D), hn[:])])
        put_first_rows(hn)
        layer3_edges()
        with ExitStack() as ctx:
            g3 = sb(ctx, "g3", [P, NB, HID])
            gT = sb(ctx, "gT3", [P, NP])
            agg = sb(ctx, "agg3", [P, NB, HID])
            wm2 = sb(ctx, "wm2", [HID, HID])
            wu1a = sb(ctx, "wu1a", [D, HID])
            wu1b = sb(ctx, "wu1b", [HID, HID])
            wu2 = sb(ctx, "wu2", [HID, D])
            rows = sb(ctx, "brow3", [P, 4, HID])
            b_u2 = sb(ctx, "b_u2", [P, D])
            load_all([(wm2[:], a["W_msg2"]), (wu1a[:], a["W_upd1"][0:D, :]), (wu1b[:], a["W_upd1"][D:D + HID, :]),
                      (wu2[:], a["W_upd2"]), (b_u2[:], a["b_upd2"].partition_broadcast(P))]
                     + [(rows[:, k, :], a[n].partition_broadcast(P)) for k, n in enumerate(("b_msg2", "b_upd1", "g_upd", "be_upd"))])
            read_rows([(rows3, last_row, g3)])
            turn([(g3[:], gT[:], P, False)])
            product_rows([(gT[:], wm2[:])], HID, agg[:])
            row = lambda k: rows[:, k, :].unsqueeze(1).to_broadcast([P, NB, HID])
            vector_step(
                lambda: nc.vector.tensor_tensor(g3[:], row(0), degree[:].unsqueeze(2).to_broadcast([P, NB, HID]), ALU.mult),
                lambda: nc.vector.tensor_tensor(agg[:], agg[:], g3[:], ALU.add))
            turn([(agg[:], gT[:], P, False)])
            product_rows([(hT[:], wu1a[:]), (gT[:], wu1b[:])], HID, agg[:], bias=rows[:, 1, :])
            rs_sem, sd_sem = S("var_ready"), S("root_ready")
            with nc.Block() as block:
                @block.vector
                def _(dve):
                    norm_rows(dve, agg[:], HID, g3[:], tmp_n[:], rs_sem, sd_sem)
                    chain(dve, nc.vector.tensor_tensor(g3[:], g3[:], row(2), ALU.mult))
                    nc.vector.tensor_tensor(g3[:], g3[:], row(3), ALU.add).then_inc(rs_sem.h, 1)
                    dve.wait_ge(sd_sem.h, sd_sem.at(2))
                    chain(dve, nc.vector.tensor_scalar(tmp_n[:], tmp_n[:], 1.0, None, ALU.add))
                    chain(dve, nc.vector.reciprocal(tmp_n[:], tmp_n[:]))
                    chain(dve, nc.vector.tensor_tensor(agg[:], g3[:], tmp_n[:], ALU.mult))

                @block.scalar
                def _(act):
                    root(act, rs_sem, sd_sem)
                    act.wait_ge(rs_sem.h, rs_sem.at(2))
                    nc.scalar.activation(tmp_n[:], g3[:], ACT.Exp, scale=-1.0).then_inc(sd_sem.h, 1)
            rs_sem.passed(2)
            sd_sem.passed(2)
            turn([(agg[:], gT[:], P, False)])
            product_rows([(gT[:], wu2[:])], D, tmp_n[:, :, 0:D], bias=b_u2[:])
            vector_step(
                lambda: nc.vector.tensor_tensor(hn[:], hn[:], tmp_n[:, :, 0:D], ALU.add),
                lambda: nc.vector.tensor_tensor(xn[:], xn[:], hn[:], ALU.add))
            store_tables([(out.rearrange("(p b) w -> p b w", b=NB), xn[0:PV])])


def constants():
    p = np.arange(P)
    headsum = (p[:, None] // DH0 == p[None, :] // DH0).astype(np.float32)
    pick1 = (p[:, None] == 32 * np.arange(HEADS1)[None, :]).astype(np.float32)
    spread1 = (p[:, None] == 32 * (np.arange(2 * P)[None, :] // D)).astype(np.float32)
    return {"ident": np.eye(P, dtype=np.float32), "headsum": headsum, "pick1": pick1, "spread1": spread1,
            "mean_w": np.full((P, HID), 1.0 / HID, np.float32)}


def lay_out(i):
    c = np.ascontiguousarray
    pad_e = EP - E
    src = np.pad(np.asarray(i["src"]), (0, pad_e))
    dst = np.pad(np.asarray(i["dst"]), (0, pad_e), constant_values=N)
    by_step = lambda v, steps: v.reshape(steps, CH, P).transpose(0, 2, 1)
    before = np.concatenate([np.full(1, -1, dst.dtype), dst[:-1]])
    col = lambda n: c(np.asarray(i[n]).reshape(-1, 1))
    wide = lambda n: c(np.pad(np.asarray(i[n]), ((0, pad_e), (0, 0))).T)
    return {
        "x": np.pad(np.asarray(i["x"]), ((0, NP - N), (0, 0))),
        "idx": c(np.concatenate([by_step(src, T), by_step(dst, T)], axis=2)),
        "idx_halves": c(np.concatenate([by_step(src[:HALF], T2), by_step(src[HALF:], T2)], axis=2)),
        "dst_rows": np.concatenate([dst, np.full(P, 2 * NP, dst.dtype)]).reshape(NC_ + 1, P),
        "chunk_last": c(dst[P - 1::P]),
        "dst_now": dst.reshape(P, NC_), "dst_before": before.reshape(P, NC_),
        "edge_weight": np.pad(np.asarray(i["edge_weight"]), (0, pad_e)).reshape(P, NC_),
        "ef": wide("edge_attr_64"), "sh": wide("edge_attr_9"), "ea": wide("edge_attr_32"),
        "Wq": c(i["L0_gnn_Wq"]), "Cqk": c(np.asarray(i["L0_gnn_Cqk"]).transpose(1, 0, 2)),
        "Cv": c(np.asarray(i["L0_gnn_Cv"]).transpose(1, 0, 2)),
        "k_w1": c(i["L0_gnn_k_w1"]), "v_w1": c(i["L0_gnn_v_w1"]), "k_w2": c(i["L0_gnn_k_w2"]), "v_w2": c(i["L0_gnn_v_w2"]),
        "k_b1": col("L0_gnn_k_b1"), "v_b1": col("L0_gnn_v_b1"), "k_b2": col("L0_gnn_k_b2"), "v_b2": col("L0_gnn_v_b2"),
        "W_out": c(i["L0_gnn_W_out"]), "W_self": c(i["L0_gnn_W_self"]),
        "gamma0": col("L0_gnn_gamma"), "beta0": col("L0_gnn_beta"),
        "W_w": c(i["L1_gnn_W_w"]), "W_b": c(i["L1_gnn_W_b"]), "attn_w": c(i["L1_gnn_attn_w"]), "attn_b": c(i["L1_gnn_attn_b"]),
        "decay_rate": c(i["L1_gnn_decay_rate"]),
        "proj_w": c(np.asarray(i["L1_gnn_proj_w"]).reshape(D, HEADS1, D).transpose(1, 0, 2)).reshape(HEADS1 * D, D),
        "proj_b": c(i["L1_gnn_proj_b"]), "ln_g": c(i["L1_gnn_ln_g"]), "ln_b": c(i["L1_gnn_ln_b"]),
        "W1T": c(np.asarray(i["L2_gnn_W1"]).transpose(0, 2, 1)), "W2T": c(np.asarray(i["L2_gnn_W2"]).transpose(0, 2, 1)),
        "gamma2": c(np.asarray(i["L2_gnn_gamma"]).T), "beta2": c(np.asarray(i["L2_gnn_beta"]).T), "eps2": c(i["L2_gnn_eps"]),
        "W_msg1": c(i["L3_gnn_W_msg1"]), "b_msg1": np.asarray(i["L3_gnn_b_msg1"]).reshape(1, HID), "g_msg": col("L3_gnn_g_msg"), "be_msg": col("L3_gnn_be_msg"),
        "W_msg2": c(i["L3_gnn_W_msg2"]), "b_msg2": c(i["L3_gnn_b_msg2"]),
        "W_upd1": c(i["L3_gnn_W_upd1"]), "b_upd1": c(i["L3_gnn_b_upd1"]), "g_upd": c(i["L3_gnn_g_upd"]),
        "be_upd": c(i["L3_gnn_be_upd"]), "W_upd2": c(i["L3_gnn_W_upd2"]), "b_upd2": c(i["L3_gnn_b_upd2"]),
    }


def kernel(**inputs):
    import concourse.bacc as bacc
    from concourse.bass_utils import run_bass_kernel_spmd as run

    nc = bacc.Bacc("TRN2", target_bir_lowering=False, num_devices=1)
    arrays, aps = {}, {}
    for name, value in {**lay_out(inputs), **constants()}.items():
        value = np.ascontiguousarray(value)
        arrays[f"in_{name}"] = value
        aps[name] = nc.dram_tensor(f"in_{name}", value.shape, mybir.dt.from_np(value.dtype), kind="ExternalInput").ap()
    out = nc.dram_tensor("out_0", (N, D), F32, kind="ExternalOutput").ap()
    build(nc, aps, out)
    return run(nc, [arrays], core_ids=[0]).results[0]["out_0"]
```

```python
from contextlib import ExitStack

import numpy as np

import concourse.bass as bass
from concourse import mybir

F32 = mybir.dt.float32
I32 = mybir.dt.int32
ALU = mybir.AluOpType
ACT = mybir.ActivationFunctionType
AX_X = mybir.AxisListType.X

P = 128
N, D, E = 3125, 64, 100000
NB = 25
NP = P * NB
PV = N // NB
SC = 512
CH = SC // P
T = 2 * -(-E // (2 * SC))
EP = T * SC
NC_ = EP // P
HALF = EP // 2
T2 = T // 2
HEADS0, DH0 = 8, 16
HEADS1 = 4
S9 = 9
ZPAIRS = (S9 + 1) // 2
W0 = P + HEADS0
W1 = HEADS1 * D + HEADS1
HID = 128
BIG = 1e30
EPS = 1e-5


class Sem:

    def __init__(self, nc, ctx, name):
        self.h = ctx.enter_context(nc.semaphore(name))
        self.base = 0

    def at(self, n):
        return n + self.base

    def passed(self, n):
        self.base += n


def known_ge(t, k):
    return t >= k if isinstance(t, int) else True


def known_lt(t, k):
    return t < k if isinstance(t, int) else True


def run_steps(eng, body, steps, before=0, after=0, first=4):
    for t in range(-before, first):
        body(t, t % 2, t // 2)
    with eng.Fori(first // 2, steps // 2 - 1) as i:
        body(i * 2, 0, i)
        body(i * 2 + 1, 1, i)
    for t in range(steps - 2, steps + after):
        body(t, t % 2, t // 2)


def build(nc, a, out):
    with ExitStack() as top:
        dram = lambda name, shape, dt=F32: nc.dram_tensor(name, shape, dt).ap()
        tab_dup = dram("tab_dup", (NP, 2 * D))
        tab_row = dram("tab_row", (NP, D))
        tab_q = dram("tab_q", (NP, P))
        rows0 = dram("rows0", (EP + 1, W0))
        rows1 = dram("rows1", (EP + 1, W1))
        rows2 = dram("rows2", (HALF + 1, 2 * D))
        rows3 = dram("rows3", (EP + 1, HID))
        dst_first = dram("dst_first", (EP + NP, D))
        reset_add = dram("reset_add", (EP,))
        keep_mul = dram("keep_mul", (EP,))
        decay_row = dram("decay_row", (EP,))

        def sb(ctx, name, shape, dt=F32):
            return ctx.enter_context(nc.sbuf_tensor(name, shape, dt))

        bank = [top.enter_context(nc.psum_tensor(f"bank{i}", [P, 512], F32)) for i in range(8)]

        names = {}

        def S(name):
            if name not in names:
                names[name] = Sem(nc, top, name)
            return names[name]

        ident = sb(top, "ident", [P, P])
        xn = sb(top, "xn", [P, NB, D])
        hn = sb(top, "hn", [P, NB, D])
        tmp_n = sb(top, "tmp_n", [P, NB, P])
        hT = sb(top, "hT", [D, NP])
        last_row = sb(top, "last_row", [P, NB], I32)
        last_row2 = sb(top, "last_row2", [P, NB], I32)
        crosses = sb(top, "crosses", [P, NB])
        first_row = sb(top, "first_row", [P, NB], I32)
        degree = sb(top, "degree", [P, NB])
        zero = sb(top, "zero", [P, max(CH * D, W0, W1)])
        stat = [sb(top, f"stat{i}", [P, NB]) for i in range(4)]
        chain_sem = S("chain")

        def chain(eng, ins):
            ins.then_inc(chain_sem.h, 1)
            chain_sem.passed(1)
            eng.wait_ge(chain_sem.h, chain_sem.base)

        def load_all(pairs):
            sem = S("loaded")
            with nc.Block() as block:
                @block.sync
                def _(sp):
                    for dst, src in pairs:
                        sp.dma_start(dst, src).then_inc(sem.h, 16)
                    sp.wait_ge(sem.h, sem.at(16 * len(pairs)))
            sem.passed(16 * len(pairs))

        cleared = S("cleared")

        def node_rows(d, w):
            return d.rearrange("(p b) w -> p b w", b=NB)[:, :, 0:w] if w != d.shape[1] else d.rearrange("(p b) w -> p b w", b=NB)

        def norm_rows(dve, src, w, dst, scratch, rs_sem, sd_sem):
            s, m, v, r = (t[:] for t in stat)
            chain(dve, nc.vector.reduce_sum(s, src, AX_X))
            chain(dve, nc.vector.tensor_scalar(m, s, 1.0 / w, None, ALU.mult))
            chain(dve, nc.vector.tensor_tensor(dst, src, m.unsqueeze(2).to_broadcast([P, NB, w]), ALU.subtract))
            chain(dve, nc.vector.tensor_tensor(scratch, dst, dst, ALU.mult))
            chain(dve, nc.vector.reduce_sum(s, scratch, AX_X))
            nc.vector.tensor_scalar(v, s, 1.0 / w, EPS, ALU.mult, ALU.add).then_inc(rs_sem.h, 1)
            dve.wait_ge(sd_sem.h, sd_sem.at(1))
            chain(dve, nc.vector.reciprocal(m, r))
            chain(dve, nc.vector.tensor_tensor(dst, dst, m.unsqueeze(2).to_broadcast([P, NB, w]), ALU.mult))

        def root(act, rs_sem, sd_sem, n=P, tiles=(2, 3), w=NB):
            act.wait_ge(rs_sem.h, rs_sem.at(1))
            nc.scalar.activation(stat[tiles[1]][0:n, 0:w], stat[tiles[0]][0:n, 0:w], ACT.Sqrt).then_inc(sd_sem.h, 1)

        def pre_norm():
            rs_sem, sd_sem = S("var_ready"), S("root_ready")
            with nc.Block() as block:
                @block.vector
                def _(dve):
                    norm_rows(dve, xn[:], D, hn[:], tmp_n[:, :, 0:D], rs_sem, sd_sem)
                    nc.vector.tensor_scalar(hn[:], hn[:], 0.0, None, ALU.max)

                @block.scalar
                def _(act):
                    root(act, rs_sem, sd_sem)
            rs_sem.passed(1)
            sd_sem.passed(1)

        def turn(jobs, func=ACT.Copy, **affine):
            turned, emptied = S("turned"), S("emptied")
            work = []
            for src, dst, w, back in jobs:
                per = 512 // w if back else CH
                for g in range(0, NB, per):
                    work.append((src, dst, w, back, g, min(per, NB - g)))
            with nc.Block() as block:
                @block.tensor
                def _(pe):
                    for k, (src, dst, w, back, g, n) in enumerate(work):
                        if k >= 2:
                            pe.wait_ge(emptied.h, emptied.at(k - 1))
                        for j in range(n):
                            if back:
                                mm = nc.tensor.transpose(bank[k % 2][:, j * w:(j + 1) * w],
                                                         src[:, (g + j) * P:(g + j + 1) * P], ident[0:w, 0:w])
                            else:
                                mm = nc.tensor.transpose(bank[k % 2][0:w, j * P:(j + 1) * P],
                                                         src[:, g + j, :], ident[:])
                        mm.then_inc(turned.h, 1)

                @block.scalar
                def _(act):
                    for k, (src, dst, w, back, g, n) in enumerate(work):
                        act.wait_ge(turned.h, turned.at(k + 1))
                        if back:
                            o, i = dst[:, g:g + n, :], bank[k % 2][:, 0:n * w].rearrange("p (b w) -> p b w", w=w)
                        else:
                            o, i = dst[:, g * P:(g + n) * P], bank[k % 2][0:w, 0:n * P]
                        nc.scalar.activation(o, i, func, **affine).then_inc(emptied.h, 1)
            turned.passed(len(work))
            emptied.passed(len(work))

        def product_T(terms, m, dst, func=ACT.Copy):
            made, emptied = S("turned"), S("emptied")
            cuts = [(c, min(512, NP - c)) for c in range(0, NP, 512)]
            with nc.Block() as block:
                @block.tensor
                def _(pe):
                    for k, (c, n) in enumerate(cuts):
                        if k >= 2:
                            pe.wait_ge(emptied.h, emptied.at(k - 1))
                        for j, (lhsT, rhs) in enumerate(terms):
                            mm = nc.tensor.matmul(bank[k % 2][0:m, 0:n], lhsT, rhs[:, c:c + n],
                                                  start=(j == 0), stop=(j == len(terms) - 1))
                        mm.then_inc(made.h, 1)

                @block.scalar
                def _(act):
                    for k, (c, n) in enumerate(cuts):
                        act.wait_ge(made.h, made.at(k + 1))
                        nc.scalar.activation(dst[:, c:c + n], bank[k % 2][0:m, 0:n], func).then_inc(emptied.h, 1)
            made.passed(len(cuts))
            emptied.passed(len(cuts))

        def product_rows(terms, w, dst, bias=None):
            made, emptied = S("turned"), S("emptied")
            per = 512 // w
            cuts = [(g, min(per, NB - g)) for g in range(0, NB, per)]
            with nc.Block() as block:
                @block.tensor
                def _(pe):
                    for k, (g, n) in enumerate(cuts):
                        if k >= 2:
                            pe.wait_ge(emptied.h, emptied.at(k - 1))
                        for b in range(n):
                            for j, (tform, weights) in enumerate(terms):
                                mm = nc.tensor.matmul(bank[k % 2][:, b * w:(b + 1) * w],
                                                      tform[:, (g + b) * P:(g + b + 1) * P], weights,
                                                      start=(j == 0), stop=(j == len(terms) - 1))
                        mm.then_inc(made.h, 1)

                @block.vector
                def _(dve):
                    for k, (g, n) in enumerate(cuts):
                        dve.wait_ge(made.h, made.at(k + 1))
                        i = bank[k % 2][:, 0:n * w].rearrange("p (b w) -> p b w", w=w)
                        if bias is None:
                            nc.vector.tensor_copy(dst[:, g:g + n, :], i).then_inc(emptied.h, 1)
                        else:
                            nc.vector.tensor_tensor(dst[:, g:g + n, :], i,
                                                    bias.unsqueeze(1).to_broadcast([P, n, w]),
                                                    ALU.add).then_inc(emptied.h, 1)
            made.passed(len(cuts))
            emptied.passed(len(cuts))

        def store_tables(pairs):
            sem = S("loaded")
            with nc.Block() as block:
                @block.sync
                def _(sp):
                    for dst, src in pairs:
                        sp.dma_start(dst, src).then_inc(sem.h, 16)
                    sp.wait_ge(sem.h, sem.at(16 * len(pairs)))
            sem.passed(16 * len(pairs))

        def read_rows(jobs, loads=()):
            sem, loaded = S("rows_read"), S("loaded")
            with nc.Block() as block:
                if loads:
                    @block.sync
                    def _(sp):
                        for dst, src in loads:
                            sp.dma_start(dst, src).then_inc(loaded.h, 16)
                        sp.wait_ge(loaded.h, loaded.at(16 * len(loads)))

                @block.gpsimd
                def _(pool):
                    for table, index, dst in jobs:
                        for b in range(NB):
                            nc.gpsimd.indirect_dma_start(
                                out=dst[:, b, :], out_offset=None, in_=table,
                                in_offset=bass.IndirectOffsetOnAxis(ap=index[:, b:b + 1], axis=0),
                            ).then_inc(sem.h, 16)
                    pool.wait_ge(sem.h, sem.at(16 * NB * len(jobs)))
            sem.passed(16 * NB * len(jobs))
            loaded.passed(16 * len(loads))

        def put_first_rows(src):
            sem = S("rows_read")
            with nc.Block() as block:
                @block.gpsimd
                def _(pool):
                    pool.wait_ge(cleared.h, cleared.at(16 * T))
                    for b in range(NB):
                        nc.gpsimd.indirect_dma_start(
                            out=dst_first, out_offset=bass.IndirectOffsetOnAxis(ap=first_row[:, b:b + 1], axis=0),
                            in_=src[:, b, :], in_offset=None).then_inc(sem.h, 16)
                    pool.wait_ge(sem.h, sem.at(16 * NB))
            sem.passed(16 * NB)

        def batch_norm(vT, gamma, beta, dst, scratch):
            rs_sem, sd_sem = S("var_ready"), S("root_ready")
            real = lambda t: t.rearrange("d (b p) -> d b p", p=P)[:, :, 0:PV]
            s, m, v, r = (t[0:D, 0:1] for t in stat)
            part = stat[0][0:D, 0:NB]
            with nc.Block() as block:
                @block.vector
                def _(dve):
                    chain(dve, nc.vector.reduce_sum(part, real(vT), AX_X))
                    chain(dve, nc.vector.reduce_sum(m, part, AX_X))
                    chain(dve, nc.vector.tensor_scalar(m, m, 1.0 / N, None, ALU.mult))
                    chain(dve, nc.vector.tensor_scalar(dst, vT, m, None, ALU.subtract))
                    chain(dve, nc.vector.tensor_tensor(scratch, dst, dst, ALU.mult))
                    chain(dve, nc.vector.reduce_sum(part, real(scratch), AX_X))
                    chain(dve, nc.vector.reduce_sum(m, part, AX_X))
                    nc.vector.tensor_scalar(v, m, 1.0 / N, EPS, ALU.mult, ALU.add).then_inc(rs_sem.h, 1)
                    dve.wait_ge(sd_sem.h, sd_sem.at(1))
                    chain(dve, nc.vector.reciprocal(m, r))
                    chain(dve, nc.vector.tensor_tensor(m, m, gamma, ALU.mult))
                    nc.vector.tensor_scalar(dst, dst, m, beta, ALU.mult, ALU.add)

                @block.scalar
                def _(act):
                    root(act, rs_sem, sd_sem, n=D, w=1)
            rs_sem.passed(1)
            sd_sem.passed(1)

        def prepare():
            with ExitStack() as ctx:
                dst_f = sb(ctx, "dst_f", [P, NC_])
                d_now = sb(ctx, "d_now", [P, NC_], I32)
                d_bef = sb(ctx, "d_bef", [P, NC_], I32)
                same = sb(ctx, "same", [P, NC_])
                reset = sb(ctx, "reset", [P, NC_])
                ew = sb(ctx, "ew", [P, NC_])
                chunk_last = sb(ctx, "chunk_last", [P, NC_], I32)
                rate = sb(ctx, "rate", [P, 1])
                NE = NB + 1
                node_i = sb(ctx, "node_i", [P, NE], I32)
                bound = sb(ctx, "bound", [P, NE])
                before = sb(ctx, "before", [P, NE])
                before_i = sb(ctx, "before_i", [P, NE], I32)
                rows = sb(ctx, "rows", [P, NE, P], I32)
                inside = sb(ctx, "inside", [P, NE])
                edge = sb(ctx, "edge", [P, NE])
                flag = sb(ctx, "flag", [P, NB])
                flag2 = sb(ctx, "flag2", [P, NB])
                k1 = sb(ctx, "k1", [P, NB])
                junk = sb(ctx, "junk", [P, 2, NC_])
                rows_f = sb(ctx, "rows_f", [P, NE, P])
                load_all([(ident[:], a["ident"]), (xn[:], node_rows(a["x"], D)),
                          (d_now[:], a["dst_now"]), (d_bef[:], a["dst_before"]),
                          (ew[:], a["edge_weight"]), (chunk_last[:], a["chunk_last"].partition_broadcast(P)),
                          (rate[:], a["decay_rate"].partition_broadcast(P))])
                made, expd, rd = S("var_ready"), S("root_ready"), [S("rows_read"), S("gathered0")]
                sent, counted, iota, zeroed = S("loaded"), S("counted"), S("iota_ready"), S("tmp_ok")
                parts = [range(0, NE // 2), range(NE // 2, NE)]
                conv = S("turned")
                with nc.Block() as block:
                    @block.gpsimd
                    def _(pool):
                        nc.gpsimd.iota(node_i[:], pattern=[[1, NE]], base=0,
                                       channel_multiplier=NB).then_inc(iota.h, 1)
                        for part, sem in zip(parts, rd):
                            for b in part:
                                pool.wait_ge(counted.h, counted.at(b + 1))
                                nc.gpsimd.indirect_dma_start(
                                    out=rows[:, b, :], out_offset=None, in_=a["dst_rows"],
                                    in_offset=bass.IndirectOffsetOnAxis(ap=before_i[:, b:b + 1], axis=0),
                                ).then_inc(sem.h, 16)

                    @block.vector
                    def _(dve):
                        nc.vector.memset(zero[:], 0.0).then_inc(zeroed.h, 1)
                        chain(dve, nc.vector.tensor_copy(dst_f[:], d_now[:]))
                        chain(dve, nc.vector.tensor_copy(reset[:], d_bef[:]))
                        chain(dve, nc.vector.tensor_tensor(same[:], dst_f[:], reset[:], ALU.is_equal))
                        chain(dve, nc.vector.tensor_scalar(reset[:], same[:], -1.0, BIG, ALU.add, ALU.mult))
                        chain(dve, nc.vector.tensor_scalar(stat[0][:, 0:1], rate[:], -1.0, None, ALU.mult))
                        chain(dve, nc.vector.tensor_tensor(stat[0][:, 0:1], stat[0][:, 0:1], rate[:], ALU.max))
                        nc.vector.tensor_scalar(rate[:], rate[:], 0.0, None, ALU.max).then_inc(made.h, 1)
                        dve.wait_ge(iota.h, iota.at(1))
                        chain(dve, nc.vector.tensor_copy(bound[:], node_i[:]))
                        chain(dve, nc.vector.tensor_copy(dst_f[:], chunk_last[:]))
                        for b in range(NE):
                            nc.vector.tensor_scalar(junk[:, b % 2, :], dst_f[:], bound[:, b:b + 1], 0.0, ALU.is_lt, ALU.add,
                                                    accum_out=before[:, b:b + 1]).then_inc(conv.h, 1)
                            if b >= 1:
                                dve.wait_ge(conv.h, conv.at(b))
                                nc.vector.tensor_copy(before_i[:, b - 1:b], before[:, b - 1:b]).then_inc(counted.h, 1)
                        dve.wait_ge(conv.h, conv.at(NE))
                        nc.vector.tensor_copy(before_i[:, NB:NE], before[:, NB:NE]).then_inc(counted.h, 1)
                        dve.wait_ge(expd.h, expd.at(2))
                        chain(dve, nc.vector.tensor_tensor(rate[:], rate[:], stat[1][:, 0:1], ALU.add))
                        nc.vector.tensor_scalar(ew[:], ew[:], -1.0, rate[:, 0:1], ALU.add, ALU.mult).then_inc(made.h, 1)
                        for part, sem in zip(parts, rd):
                            dve.wait_ge(sem.h, sem.at(16 * len(part)))
                            lo, hi = part[0], part[-1] + 1
                            chain(dve, nc.vector.tensor_copy(rows_f[:, lo:hi, :], rows[:, lo:hi, :]))
                            for b in part:
                                ins = nc.vector.tensor_scalar(rows_f[:, b, :], rows_f[:, b, :], bound[:, b:b + 1], 0.0,
                                                              ALU.is_lt, ALU.add, accum_out=inside[:, b:b + 1])
                            chain(dve, ins)
                        chain(dve, nc.vector.tensor_scalar(edge[:], before[:], float(P), None, ALU.mult))
                        chain(dve, nc.vector.tensor_tensor(edge[:], edge[:], inside[:], ALU.add))
                        chain(dve, nc.vector.tensor_tensor(degree[:], edge[:, 1:NE], edge[:, 0:NB], ALU.subtract))
                        chain(dve, nc.vector.tensor_scalar(flag[:], degree[:], 1.0, None, ALU.min))
                        chain(dve, nc.vector.tensor_scalar(k1[:], edge[:, 1:NE], float(-1 - EP), None, ALU.add))
                        chain(dve, nc.vector.tensor_tensor(k1[:], k1[:], flag[:], ALU.mult))
                        chain(dve, nc.vector.tensor_scalar(k1[:], k1[:], float(EP), None, ALU.add))
                        chain(dve, nc.vector.tensor_copy(last_row[:], k1[:]))
                        chain(dve, nc.vector.tensor_scalar(junk[:, 0, 0:NB], bound[:, 0:NB], float(EP), None, ALU.add))
                        chain(dve, nc.vector.tensor_tensor(flag2[:], edge[:, 0:NB], junk[:, 0, 0:NB], ALU.subtract))
                        chain(dve, nc.vector.tensor_tensor(flag2[:], flag2[:], flag[:], ALU.mult))
                        chain(dve, nc.vector.tensor_tensor(flag2[:], flag2[:], junk[:, 0, 0:NB], ALU.add))
                        chain(dve, nc.vector.tensor_copy(first_row[:], flag2[:]))
                        chain(dve, nc.vector.tensor_scalar(flag2[:], k1[:], float(HALF), None, ALU.is_ge))
                        chain(dve, nc.vector.tensor_tensor(flag2[:], flag2[:], flag[:], ALU.mult))
                        chain(dve, nc.vector.tensor_scalar(k1[:], edge[:, 1:NE], 2.0, float(-2 - EP), ALU.mult, ALU.add))
                        chain(dve, nc.vector.tensor_tensor(k1[:], k1[:], flag[:], ALU.mult))
                        chain(dve, nc.vector.tensor_scalar(junk[:, 0, 0:NB], flag2[:], float(1 - 2 * HALF), float(EP), ALU.mult, ALU.add))
                        chain(dve, nc.vector.tensor_tensor(k1[:], k1[:], junk[:, 0, 0:NB], ALU.add))
                        chain(dve, nc.vector.tensor_copy(last_row2[:], k1[:]))
                        chain(dve, nc.vector.tensor_scalar(flag[:], edge[:, 0:NB], float(HALF), None, ALU.is_lt))
                        chain(dve, nc.vector.tensor_tensor(crosses[:], flag[:], flag2[:], ALU.mult))

                    @block.scalar
                    def _(act):
                        act.wait_ge(made.h, made.at(1))
                        nc.scalar.activation(stat[2][:, 0:1], stat[0][:, 0:1], ACT.Exp, scale=-1.0).then_inc(expd.h, 1)
                        act.wait_ge(expd.h, expd.at(1))
                        nc.scalar.activation(stat[1][:, 0:1], stat[2][:, 0:1], ACT.Ln, bias=1.0).then_inc(expd.h, 1)
                        act.wait_ge(made.h, made.at(2))
                        nc.scalar.activation(ew[:], ew[:], ACT.Exp).then_inc(expd.h, 1)

                    @block.sync
                    def _(sp):
                        sp.wait_ge(zeroed.h, zeroed.at(1))
                        sp.wait_ge(made.h, made.at(1))
                        row = lambda d: d.rearrange("(p c) -> p c", c=NC_)
                        sp.dma_start(row(keep_mul), same[:]).then_inc(sent.h, 16)
                        sp.dma_start(row(reset_add), reset[:]).then_inc(sent.h, 16)
                        sp.dma_start(rows0[EP:EP + 1, :], zero[0:1, 0:W0]).then_inc(sent.h, 16)
                        sp.dma_start(rows1[EP:EP + 1, :], zero[0:1, 0:W1]).then_inc(sent.h, 16)
                        sp.dma_start(rows2[HALF:HALF + 1, :], zero[0:1, 0:2 * D]).then_inc(sent.h, 16)
                        sp.dma_start(rows3[EP:EP + 1, :], zero[0:1, 0:HID]).then_inc(sent.h, 16)
                        sp.wait_ge(expd.h, expd.at(3))
                        sp.dma_start(row(decay_row), ew[:]).then_inc(sent.h, 16)
                        sp.wait_ge(sent.h, sent.at(16 * 7))
                made.passed(2)
                expd.passed(3)
                for part, sem in zip(parts, rd):
                    sem.passed(16 * len(part))
                conv.passed(NE)
                sent.passed(16 * 7)
                zeroed.passed(1)
                counted.passed(NE)
                iota.passed(1)

        def gather_step(pool, t, par, i, what, steps, idx_in, slots_free, gathered):
            if not (known_ge(t, 0) and known_lt(t, steps)):
                return
            pool.wait_ge(idx_in[par].h, idx_in[par].at((i + 1) * 16))
            if known_ge(t, 2):
                for sem in slots_free:
                    pool.wait_ge(sem.h, sem.at(t - 1))
            nc.gpsimd.sem_inc(S("pool_turn").h, 1)
            for dst, table, index in what(par):
                nc.gpsimd.indirect_dma_start(out=dst, out_offset=None, in_=table,
                                             in_offset=bass.IndirectOffsetOnAxis(ap=index, axis=0)
                                             ).then_inc(gathered[par].h, 16)

        def edges(d, t):
            return d[bass.ds(t * SC, SC)]

        def layer0_edges():
            with ExitStack() as ctx:
                ck = sb(ctx, "ck", [P, ZPAIRS, P])
                cv = sb(ctx, "cv", [P, ZPAIRS, P])
                w1 = sb(ctx, "w1", [D, 2 * D])
                b1 = sb(ctx, "b1", [P, 1])
                w2 = sb(ctx, "w2", [P, P])
                b2 = sb(ctx, "b2", [P, 2])
                headsum = sb(ctx, "headsum", [P, P])
                idx = sb(ctx, "idx", [P, 2, 2 * CH], I32)
                gx = sb(ctx, "gx", [P, 2, CH, 2 * D])
                gq = sb(ctx, "gq", [P, 2, CH, P])
                ef = sb(ctx, "ef", [D, 2, SC])
                sh = sb(ctx, "sh", [P, 2, ZPAIRS, SC])
                z = sb(ctx, "z", [P, 2, ZPAIRS, SC])
                rst = sb(ctx, "rst", [P, 2, SC])
                hid = sb(ctx, "hid", [P, 2, SC])
                wk = sb(ctx, "wk", [P, SC])
                wv = sb(ctx, "wv", [P, SC])
                kw = sb(ctx, "kw", [P, SC])
                qk = sb(ctx, "qk", [P, SC])
                val = sb(ctx, "val", [P, 2, SC])
                mx = sb(ctx, "mx", [P, 2, SC + 1])
                arg = sb(ctx, "arg", [P, 2, 2 * SC])
                pd = sb(ctx, "pd", [P, 2, 2 * SC])
                pv = sb(ctx, "pv", [P, SC])
                num = sb(ctx, "num", [P, 2, SC])
                den = sb(ctx, "den", [P, 2, SC])
                o = sb(ctx, "o", [P, 2, CH, W0])
                pairs = [(ck[0:D, j, :], a["Cqk"][2 * j]) for j in range(ZPAIRS)]
                pairs += [(ck[D:P, j, :], a["Cqk"][2 * j + 1]) for j in range(ZPAIRS - 1)]
                pairs += [(cv[0:D, j, :], a["Cv"][2 * j]) for j in range(ZPAIRS - 1)]
                pairs += [(cv[D:P, j, :], a["Cv"][min(2 * j + 1, S9 - 1)]) for j in range(ZPAIRS)]
                pairs += [(w1[:, 0:D], a["k_w1"]), (w1[:, D:2 * D], a["v_w1"]), (b1[0:D, :], a["k_b1"]),
                          (b1[D:P, :], a["v_b1"]), (w2[0:D, :], a["k_w2"]), (w2[D:P, :], a["v_w2"]),
                          (b2[:, 0:1], a["k_b2"]), (b2[:, 1:2], a["v_b2"]),
                          (headsum[:], a["headsum"])]
                load_all(pairs)
                bX, bQ, bH, bW, bK, bV, bS, bO = bank
                idx_in, ef_in, sh_in, rst_in = ([S(f"{n}{j}") for j in range(2)] for n in ("idx_in", "feat_in", "sh_in", "rst_in"))
                gathered, stored = ([S(f"{n}{j}") for j in range(2)] for n in ("gathered", "stored"))
                xT, qT, h_ps, hid_ok, wk_ps, wk_ok, wv_ps, wv_ok = (S(n) for n in (
                    "xT", "qT", "h_ps", "hid_ok", "wk_ps", "wk_ok", "wv_ps", "wv_ok"))
                z_ok, k_ps, v_ps, kw_ok, qk_ok, s_ps, mx_ok, arg_ok = (S(n) for n in (
                    "z_ok", "k_ps", "v_ps", "kw_ok", "qk_ok", "s_ps", "mx_ok", "arg_ok"))
                pd_ok, val_ok, pv_ok, scanned, o_ps, o_ok, tmp_ok, sub_ok = (S(n) for n in (
                    "pd_ok", "val_ok", "pv_ok", "scanned", "o_ps", "o_ok", "tmp_ok", "sub_ok"))

                def gathers(par):
                    for j in range(CH):
                        yield gx[:, par, j, :], tab_dup, idx[:, par, j:j + 1]
                    for j in range(CH):
                        yield gq[:, par, j, :], tab_q, idx[:, par, CH + j:CH + j + 1]

                with nc.Block() as block:
                    @block.sync
                    def _(sp):
                        def body(t, par, i):
                            if known_lt(t, T):
                                if known_ge(t, 2):
                                    sp.wait_ge(gathered[par].h, gathered[par].at(i * (16 * 2 * CH)))
                                sp.dma_start(idx[:, par, :], a["idx"][bass.ds(t, 1)].rearrange("t p j -> p (t j)")).then_inc(idx_in[par].h, 16)
                                if known_ge(t, 2):
                                    sp.wait_ge(h_ps.h, h_ps.at(t - 1))
                                sp.dma_start(ef[:, par, :], a["ef"][:, bass.ds(t * SC, SC)]).then_inc(ef_in[par].h, 16)
                                if known_ge(t, 2):
                                    sp.wait_ge(z_ok.h, z_ok.at(t - 1))
                                sp.dma_start(sh[0:D, par, :, :], a["sh"][0:S9:2, bass.ds(t * SC, SC)].partition_broadcast(D)).then_inc(sh_in[par].h, 16)
                                sp.dma_start(sh[D:P, par, 0:ZPAIRS - 1, :], a["sh"][1:S9:2, bass.ds(t * SC, SC)].partition_broadcast(D)).then_inc(sh_in[par].h, 16)
                                sp.dma_start(sh[D:P, par, ZPAIRS - 1:ZPAIRS, :], a["sh"][S9 - 1:S9, bass.ds(t * SC, SC)].partition_broadcast(D)).then_inc(sh_in[par].h, 16)
                                if known_ge(t, 2):
                                    sp.wait_ge(arg_ok.h, arg_ok.at(t - 1))
                                sp.dma_start(rst[:, par, :], edges(reset_add, t).partition_broadcast(P)).then_inc(rst_in[par].h, 16)
                                sp.dma_start(dst_first[bass.ds(t * SC, SC), :].rearrange("(p c) w -> p (c w)", p=P),
                                             zero[:, 0:CH * D]).then_inc(cleared.h, 16)
                            if known_ge(t, 3):
                                u = t - 3
                                sp.wait_ge(o_ok.h, o_ok.at(u + 1))
                                sp.dma_start(rows0[bass.ds(u * SC, SC), :].rearrange("(c p) w -> p c w", p=P),
                                             o[:, 1 - par, :, :]).then_inc(stored[1 - par].h, 16)
                        run_steps(sp, body, T, after=3)
                        for j in range(2):
                            sp.wait_ge(stored[j].h, stored[j].at(16 * T2))

                    @block.gpsimd
                    def _(pool):
                        run_steps(pool, lambda t, par, i: gather_step(pool, t, par, i, gathers, T, idx_in, (xT, qT), gathered), T)

                    @block.tensor
                    def _(pe):
                        def heads_in(t, par, i):
                            pe.wait_ge(ef_in[par].h, ef_in[par].at((i + 1) * 16))
                            if known_ge(t, 1):
                                pe.wait_ge(hid_ok.h, hid_ok.at(t))
                            nc.tensor.matmul(bH[:], w1[:], ef[:, par, :], start=True, stop=True).then_inc(h_ps.h, 1)
                            pe.wait_ge(gathered[par].h, gathered[par].at((i + 1) * (16 * 2 * CH)))
                            if known_ge(t, 1):
                                pe.wait_ge(z_ok.h, z_ok.at(t))
                            for c in range(CH):
                                mm = nc.tensor.transpose(bX[:, c * P:(c + 1) * P], gx[:, par, c, :], ident[:])
                            mm.then_inc(xT.h, 1)

                        def queries_in(t, par, i):
                            if known_ge(t, 1):
                                pe.wait_ge(qk_ok.h, qk_ok.at(t))
                            for c in range(CH):
                                mm = nc.tensor.transpose(bQ[:, c * P:(c + 1) * P], gq[:, par, c, :], ident[:])
                            mm.then_inc(qT.h, 1)

                        def contract(bankx, coef, par, pairs_of):
                            first, last = (0, ZPAIRS - 1) if bankx is bK else (ZPAIRS - 1, ZPAIRS - 2)
                            for j in pairs_of:
                                r = slice(0, P) if j < ZPAIRS - 1 else slice(0, D) if bankx is bK else slice(D, P)
                                mm = nc.tensor.matmul(bankx[:], coef[r, j, :], z[r, par, j, :],
                                                      start=(j == first), stop=(j == last))
                            return mm

                        def body(t, par, i):
                            nxt = (t + 1, 1 - par, i + par)
                            mid = known_ge(t, 0) and known_lt(t, T)
                            if mid:
                                pe.wait_ge(hid_ok.h, hid_ok.at(t + 1))
                                if isinstance(t, int) and t == 1:
                                    pe.wait_ge(wv_ok.h, wv_ok.at(1))
                                if known_ge(t, 2):
                                    pe.wait_ge(o_ok.h, o_ok.at(t - 1))
                                nc.tensor.matmul(bW[:], w2[0:D, :], hid[0:D, par, :], start=True, stop=True).then_inc(wk_ps.h, 1)
                            if known_lt(t, T - 1):
                                heads_in(*nxt)
                            if mid:
                                pe.wait_ge(wk_ok.h, wk_ok.at(t + 1))
                                nc.tensor.matmul(bW[:], w2[D:P, :], hid[D:P, par, :], start=True, stop=True).then_inc(wv_ps.h, 1)
                                pe.wait_ge(z_ok.h, z_ok.at(t + 1))
                                if known_ge(t, 1):
                                    pe.wait_ge(kw_ok.h, kw_ok.at(t))
                                contract(bK, ck, par, range(ZPAIRS)).then_inc(k_ps.h, 1)
                                if known_ge(t, 1):
                                    pe.wait_ge(val_ok.h, val_ok.at(t))
                                contract(bV, cv, par, (ZPAIRS - 1,))
                            if known_ge(t, 1):
                                pe.wait_ge(scanned.h, scanned.at(2 * t))
                                if known_ge(t, 2):
                                    pe.wait_ge(o_ok.h, o_ok.at(t - 1))
                                if mid:
                                    pe.wait_ge(wv_ok.h, wv_ok.at(t + 1))
                                for c in range(CH):
                                    nc.tensor.transpose(bO[:, c * P:(c + 1) * P], num[:, 1 - par, c * P:(c + 1) * P], ident[:])
                                for c in range(CH):
                                    mm = nc.tensor.transpose(bW[:, c * P:(c + 1) * P], den[:, 1 - par, c * P:(c + 1) * P], ident[:])
                                mm.then_inc(o_ps.h, 1)
                            if mid:
                                contract(bV, cv, par, range(1))
                                pe.wait_ge(qk_ok.h, qk_ok.at(t + 1))
                                if known_ge(t, 1):
                                    pe.wait_ge(arg_ok.h, arg_ok.at(t))
                                nc.tensor.matmul(bS[:], headsum[:], qk[:], start=True, stop=True).then_inc(s_ps.h, 1)
                                contract(bV, cv, par, range(1, ZPAIRS - 1)).then_inc(v_ps.h, 1)
                            if known_lt(t, T - 1):
                                queries_in(*nxt)
                        run_steps(pe, body, T, before=1, after=1)

                    @block.scalar
                    def _(act):
                        def body(t, par, i):
                            mid = known_ge(t, 0) and known_lt(t, T)
                            if mid:
                                act.wait_ge(wk_ps.h, wk_ps.at(t + 1))
                                if known_ge(t, 1):
                                    act.wait_ge(kw_ok.h, kw_ok.at(t))
                                nc.scalar.activation(wk[:], bW[:], ACT.Identity, bias=b2[:, 0:1]).then_inc(wk_ok.h, 1)
                            if known_lt(t, T - 1):
                                act.wait_ge(h_ps.h, h_ps.at(t + 2))
                                if known_ge(t, 1):
                                    act.wait_ge(wv_ps.h, wv_ps.at(t))
                                nc.scalar.activation(hid[:, 1 - par, :], bH[:], ACT.Relu, bias=b1[:]).then_inc(hid_ok.h, 1)
                            if mid:
                                act.wait_ge(wv_ps.h, wv_ps.at(t + 1))
                                if known_ge(t, 1):
                                    act.wait_ge(val_ok.h, val_ok.at(t))
                                nc.scalar.activation(wv[:], bW[:], ACT.Identity, bias=b2[:, 1:2]).then_inc(wv_ok.h, 1)
                            if known_ge(t, 1):
                                act.wait_ge(o_ps.h, o_ps.at(t))
                                if known_ge(t, 3):
                                    act.wait_ge(stored[1 - par].h, stored[1 - par].at((i - 1 + par) * 16))
                                nc.scalar.activation(o[:, 1 - par, :, 0:P], bO[:].rearrange("p (c w) -> p c w", w=P), ACT.Copy)
                                nc.scalar.activation(o[:, 1 - par, :, P:W0], bW[:].rearrange("p (c h r) -> p c h r", c=CH, h=HEADS0)[:, :, :, 0],
                                                     ACT.Copy).then_inc(o_ok.h, 1)
                            if mid:
                                act.wait_ge(arg_ok.h, arg_ok.at(t + 1))
                                if known_ge(t, 2):
                                    act.wait_ge(scanned.h, scanned.at(2 * (t - 1)))
                                nc.scalar.activation(pd[:, par, :], arg[:, par, :], ACT.Exp).then_inc(pd_ok.h, 1)
                        run_steps(act, body, T, before=1, after=1)

                    @block.vector
                    def _(dve):
                        nc.vector.memset(mx[:, 1, :], -BIG).then_inc(tmp_ok.h, 1)
                        nc.vector.memset(num[:, 1, :], 0.0).then_inc(tmp_ok.h, 1)
                        nc.vector.memset(den[:, 1, :], 0.0).then_inc(tmp_ok.h, 1)
                        dve.wait_ge(tmp_ok.h, tmp_ok.at(3))
                        tmp_ok.passed(3)

                        def body(t, par, i):
                            old = 1 - par
                            mid = known_ge(t, 0) and known_lt(t, T)
                            if known_lt(t, T - 1):
                                dve.wait_ge(xT.h, xT.at(t + 2))
                                dve.wait_ge(sh_in[old].h, sh_in[old].at((i + par + 1) * 48))
                                if known_ge(t, 1):
                                    dve.wait_ge(v_ps.h, v_ps.at(t))
                                nc.vector.tensor_tensor(z[:, old, :, :], bX[:].unsqueeze(1).to_broadcast([P, ZPAIRS, SC]),
                                                        sh[:, old, :, :], ALU.mult).then_inc(z_ok.h, 1)
                            if known_ge(t, 1):
                                dve.wait_ge(pd_ok.h, pd_ok.at(t))
                                dve.wait_ge(val_ok.h, val_ok.at(t))
                                nc.vector.tensor_tensor(pv[:], pd[:, old, 0:SC], val[:, old, :], ALU.mult).then_inc(pv_ok.h, 1)
                                if known_ge(t, 3):
                                    dve.wait_ge(o_ps.h, o_ps.at(t - 2))
                                nc.vector.tensor_tensor_scan(den[:, old, :], pd[:, old, SC:2 * SC], pd[:, old, 0:SC],
                                                             den[:, par, SC - 1:SC], ALU.mult, ALU.add).then_inc(scanned.h, 1)
                                dve.wait_ge(pv_ok.h, pv_ok.at(t))
                                nc.vector.tensor_tensor_scan(num[:, old, :], pd[:, old, SC:2 * SC], pv[:],
                                                             num[:, par, SC - 1:SC], ALU.mult, ALU.add).then_inc(scanned.h, 1)
                            if mid:
                                dve.wait_ge(k_ps.h, k_ps.at(t + 1))
                                dve.wait_ge(wk_ok.h, wk_ok.at(t + 1))
                                nc.vector.tensor_tensor(kw[:], wk[:], bK[:], ALU.mult).then_inc(kw_ok.h, 1)
                                dve.wait_ge(kw_ok.h, kw_ok.at(t + 1))
                                dve.wait_ge(qT.h, qT.at(t + 1))
                                if known_ge(t, 1):
                                    dve.wait_ge(s_ps.h, s_ps.at(t))
                                nc.vector.tensor_tensor(qk[:], kw[:], bQ[:], ALU.mult).then_inc(qk_ok.h, 1)
                                dve.wait_ge(s_ps.h, s_ps.at(t + 1))
                                dve.wait_ge(rst_in[par].h, rst_in[par].at((i + 1) * 16))
                                nc.vector.tensor_copy(mx[:, par, 0:1], mx[:, old, SC:SC + 1])
                                nc.vector.tensor_tensor_scan(mx[:, par, 1:SC + 1], rst[:, par, :], bS[:],
                                                             mx[:, old, SC:SC + 1], ALU.add, ALU.max).then_inc(mx_ok.h, 1)
                                dve.wait_ge(mx_ok.h, mx_ok.at(t + 1))
                                nc.vector.tensor_tensor(arg[:, par, SC:2 * SC], mx[:, par, 0:SC], rst[:, par, :], ALU.add).then_inc(sub_ok.h, 1)
                                nc.vector.tensor_tensor(arg[:, par, 0:SC], bS[:], mx[:, par, 1:SC + 1], ALU.subtract)
                                dve.wait_ge(sub_ok.h, sub_ok.at(t + 1))
                                nc.vector.tensor_tensor(arg[:, par, SC:2 * SC], arg[:, par, SC:2 * SC], mx[:, par, 1:SC + 1],
                                                        ALU.subtract).then_inc(arg_ok.h, 1)
                                dve.wait_ge(v_ps.h, v_ps.at(t + 1))
                                dve.wait_ge(wv_ok.h, wv_ok.at(t + 1))
                                nc.vector.tensor_tensor(val[:, par, :], wv[:], bV[:], ALU.mult).then_inc(val_ok.h, 1)
                        run_steps(dve, body, T, before=1, after=1)
                for j in range(2):
                    for s, n in ((idx_in, 16), (ef_in, 16), (sh_in, 48), (rst_in, 16), (gathered, 32 * CH), (stored, 16)):
                        s[j].passed(n * T2)
                for s in (xT, qT, h_ps, hid_ok, wk_ps, wk_ok, wv_ps, wv_ok, z_ok, k_ps, v_ps, kw_ok, qk_ok, s_ps,
                          mx_ok, arg_ok, pd_ok, val_ok, pv_ok, o_ps, o_ok, sub_ok):
                    s.passed(T)
                scanned.passed(2 * T)

        def layer1_edges():
            with ExitStack() as ctx:
                aw = sb(ctx, "aw", [P, HEADS1])
                lw = sb(ctx, "lw", [P, P])
                ab = sb(ctx, "ab", [P, 1])
                pick = sb(ctx, "pick1", [P, HEADS1])
                spread = sb(ctx, "spread1", [P, 2, P])
                idx = sb(ctx, "idx1", [P, 2, 2 * CH], I32)
                gx = sb(ctx, "gx1", [P, 2, CH, 2 * D])
                pair = sb(ctx, "pair1", [P, 2, SC])
                xs = sb(ctx, "xs1", [P, 2, SC])
                rst = sb(ctx, "rst1", [P, 2, SC])
                dec = sb(ctx, "dec1", [P, 2, SC])
                lr = sb(ctx, "lr1", [P, SC])
                sc = sb(ctx, "sc1", [P, SC])
                mx = sb(ctx, "mx1", [P, 2, SC + 1])
                run = sb(ctx, "run1", [P, SC])
                gap = sb(ctx, "gap1", [P, 2, SC])
                arg = sb(ctx, "arg1", [P, 2 * SC])
                pd = sb(ctx, "pd1", [P, 2, 2 * SC])
                pv = sb(ctx, "pv1", [P, 2, SC])
                num = sb(ctx, "num1", [P, 2, 2, SC])
                den = sb(ctx, "den1", [P, 2, SC])
                o = sb(ctx, "o1", [P, 2, CH, W1])
                load_all([(aw[0:D, :], a["attn_w"][D:2 * D, :]), (aw[D:P, :], a["attn_w"][0:D, :]), (pick[:], a["pick1"]),
                          (spread[:], a["spread1"].rearrange("r (g m) -> r g m", g=2))]
                         + [(ab[32 * h:32 * (h + 1), :], a["attn_b"][h:h + 1].partition_broadcast(32)) for h in range(HEADS1)])
                bA, bL, bP0, bD0, bP1, bD1, bO0, bO1 = bank
                idx_in, rst_in, dec_in, gathered, stored = ([S(f"{n}{j}") for j in range(2)] for n in (
                    "idx_in", "rst_in", "feat_in", "gathered", "stored"))
                aT, pair_ok, xs_ok, l_ps, lr_ok, sc_ok, mx_ok, sub_ok, arg_ok, gap_ok = (S(n) for n in (
                    "xT", "hid_ok", "wk_ok", "s_ps", "wv_ok", "kw_ok", "mx_ok", "sub_ok", "arg_ok", "val_ok"))
                pd_ok, p_ps, d_ps, pv_ok, den_ok, scanned, den_ps, dn_ok, o_ps, o_ok, tmp_ok = (S(n) for n in (
                    "pd_ok", "k_ps", "v_ps", "pv_ok", "qk_ok", "scanned", "wk_ps", "wv_ps", "o_ps", "o_ok", "tmp_ok"))

                def gathers(par):
                    for j in range(CH):
                        yield gx[:, par, j, D:2 * D], tab_row, idx[:, par, j:j + 1]
                    for j in range(CH):
                        yield gx[:, par, j, 0:D], tab_row, idx[:, par, CH + j:CH + j + 1]

                with nc.Block() as block:
                    @block.sync
                    def _(sp):
                        def body(t, par, i):
                            old = 1 - par
                            if known_lt(t, T - 1):
                                if known_ge(t, 1):
                                    sp.wait_ge(gathered[old].h, gathered[old].at((i + par) * (32 * CH)))
                                sp.dma_start(idx[:, old, :], a["idx"][bass.ds(t + 1, 1)].rearrange("t p j -> p (t j)")).then_inc(idx_in[old].h, 16)
                            if known_ge(t, 0) and known_lt(t, T):
                                if known_ge(t, 2):
                                    sp.wait_ge(lr_ok.h, lr_ok.at(t - 1))
                                sp.dma_start(dec[:, par, :], edges(decay_row, t).partition_broadcast(P)).then_inc(dec_in[par].h, 16)
                                if known_ge(t, 2):
                                    sp.wait_ge(sub_ok.h, sub_ok.at(t - 1))
                                sp.dma_start(rst[:, par, :], edges(reset_add, t).partition_broadcast(P)).then_inc(rst_in[par].h, 16)
                            if known_ge(t, 4):
                                u = t - 4
                                sp.wait_ge(o_ok.h, o_ok.at(u + 1))
                                sp.dma_start(rows1[bass.ds(u * SC, SC), :].rearrange("(c p) w -> p c w", p=P),
                                             o[:, par, :, :]).then_inc(stored[par].h, 16)
                        run_steps(sp, body, T, before=1, after=4)
                        for j in range(2):
                            sp.wait_ge(stored[j].h, stored[j].at(16 * T2))

                    @block.gpsimd
                    def _(pool):
                        run_steps(pool, lambda t, par, i: gather_step(pool, t, par, i, gathers, T, idx_in, (aT,), gathered), T)

                    @block.tensor
                    def _(pe):
                        pe.wait_ge(tmp_ok.h, tmp_ok.at(1))

                        def body(t, par, i):
                            old = 1 - par
                            if known_lt(t, T - 1):
                                pe.wait_ge(gathered[old].h, gathered[old].at((i + par + 1) * (32 * CH)))
                                if known_ge(t, 0):
                                    pe.wait_ge(pair_ok.h, pair_ok.at(t + 1))
                                for c in range(CH):
                                    mm = nc.tensor.transpose(bA[:, c * P:(c + 1) * P], gx[:, old, c, :], ident[:])
                                mm.then_inc(aT.h, 1)
                            if known_ge(t, 2):
                                pe.wait_ge(den_ok.h, den_ok.at(t - 1))
                                if known_lt(t, T):
                                    pe.wait_ge(lr_ok.h, lr_ok.at(t + 1))
                                else:
                                    pe.wait_ge(dn_ok.h, dn_ok.at(t - 2))
                                for c in range(CH):
                                    mm = nc.tensor.matmul(bL[:, c * HEADS1:(c + 1) * HEADS1], den[:, par, c * P:(c + 1) * P], pick[:],
                                                          start=True, stop=True)
                                mm.then_inc(den_ps.h, 1)
                                pe.wait_ge(scanned.h, scanned.at(2 * (t - 1)))
                                if known_ge(t, 3):
                                    pe.wait_ge(o_ok.h, o_ok.at(t - 2))
                                for g, b in ((0, bO0), (1, bO1)):
                                    for c in range(CH):
                                        mm = nc.tensor.transpose(b[:, c * P:(c + 1) * P], num[:, par, g, c * P:(c + 1) * P], ident[:])
                                mm.then_inc(o_ps.h, 1)
                            if known_lt(t, T - 1):
                                pe.wait_ge(pair_ok.h, pair_ok.at(t + 2))
                                if known_ge(t, 0):
                                    pe.wait_ge(lr_ok.h, lr_ok.at(t + 1))
                                if known_ge(t, 2):
                                    pe.wait_ge(dn_ok.h, dn_ok.at(t - 1))
                                nc.tensor.matmul(bL[:], lw[:], pair[:, old, :], start=True, stop=True).then_inc(l_ps.h, 1)
                            if known_ge(t, 0) and known_lt(t, T):
                                pe.wait_ge(pd_ok.h, pd_ok.at(t + 1))
                                if known_ge(t, 1):
                                    pe.wait_ge(pv_ok.h, pv_ok.at(t))
                                for g, bp in ((0, bP0), (1, bP1)):
                                    mm = nc.tensor.matmul(bp[:], spread[:, g, :], pd[:, par, 0:SC], start=True, stop=True)
                                mm.then_inc(p_ps.h, 1)
                                for g, bd in ((0, bD0), (1, bD1)):
                                    if known_ge(t, 1):
                                        pe.wait_ge(scanned.h, scanned.at(2 * t - 1 + g))
                                    mm = nc.tensor.matmul(bd[:], spread[:, g, :], pd[:, par, SC:2 * SC], start=True, stop=True)
                                mm.then_inc(d_ps.h, 1)
                        run_steps(pe, body, T, before=1, after=2)

                    @block.scalar
                    def _(act):
                        def body(t, par, i):
                            old = 1 - par
                            mid = known_ge(t, 0) and known_lt(t, T)
                            if mid:
                                act.wait_ge(pair_ok.h, pair_ok.at(t + 1))
                                if known_ge(t, 2):
                                    act.wait_ge(pv_ok.h, pv_ok.at(t - 1))
                                nc.scalar.activation(xs[0:D, par, :], pair[D:P, par, :], ACT.Copy)
                                nc.scalar.activation(xs[D:P, par, :], pair[D:P, par, :], ACT.Copy).then_inc(xs_ok.h, 1)
                            if known_lt(t, T - 1):
                                act.wait_ge(aT.h, aT.at(t + 2))
                                if known_ge(t, 1):
                                    act.wait_ge(l_ps.h, l_ps.at(t))
                                    act.wait_ge(xs_ok.h, xs_ok.at(t))
                                nc.scalar.activation(pair[:, old, :], bA[:], ACT.Copy).then_inc(pair_ok.h, 1)
                            if known_ge(t, 2):
                                act.wait_ge(den_ps.h, den_ps.at(t - 1))
                                if known_ge(t, 4):
                                    act.wait_ge(stored[par].h, stored[par].at((i - 1) * 16))
                                nc.scalar.activation(o[:, par, :, 2 * P:W1], bL[:, 0:CH * HEADS1].rearrange("p (c w) -> p c w", w=HEADS1),
                                                     ACT.Copy).then_inc(dn_ok.h, 1)
                            if mid:
                                act.wait_ge(gap_ok.h, gap_ok.at(t + 1))
                                if known_ge(t, 1):
                                    act.wait_ge(pd_ok.h, pd_ok.at(t))
                                nc.scalar.activation(arg[:, 0:SC], gap[:, par, :], ACT.Relu, scale=-1.0).then_inc(arg_ok.h, 1)
                                nc.scalar.activation(arg[:, SC:2 * SC], gap[:, par, :], ACT.Relu).then_inc(arg_ok.h, 1)
                                act.wait_ge(arg_ok.h, arg_ok.at(2 * t + 2))
                                if known_ge(t, 2):
                                    act.wait_ge(d_ps.h, d_ps.at(t - 1))
                                    act.wait_ge(den_ok.h, den_ok.at(t - 1))
                                nc.scalar.activation(pd[:, par, :], arg[:], ACT.Exp, scale=-1.0).then_inc(pd_ok.h, 1)
                            if known_ge(t, 2):
                                act.wait_ge(o_ps.h, o_ps.at(t - 1))
                                for g, b in ((0, bO0), (1, bO1)):
                                    ins = nc.scalar.activation(o[:, par, :, g * P:(g + 1) * P], b[:].rearrange("p (c w) -> p c w", w=P), ACT.Copy)
                                ins.then_inc(o_ok.h, 1)
                        run_steps(act, body, T, before=1, after=2)

                    @block.vector
                    def _(dve):
                        for h in range(HEADS1):
                            ins = nc.vector.tensor_copy(lw[:, 32 * h:32 * (h + 1)], aw[:, h:h + 1].to_broadcast([P, 32]))
                        ins.then_inc(tmp_ok.h, 1)
                        nc.vector.memset(mx[:, 1], -BIG).then_inc(tmp_ok.h, 1)
                        nc.vector.memset(num[:, 1], 0.0).then_inc(tmp_ok.h, 1)
                        nc.vector.memset(den[:, 1], 0.0).then_inc(tmp_ok.h, 1)
                        dve.wait_ge(tmp_ok.h, tmp_ok.at(4))

                        def body(t, par, i):
                            old = 1 - par
                            if known_ge(t, 0) and known_lt(t, T):
                                dve.wait_ge(l_ps.h, l_ps.at(t + 1))
                                dve.wait_ge(dec_in[par].h, dec_in[par].at((i + 1) * 16))
                                nc.vector.scalar_tensor_tensor(out=lr[:], in0=bL[:], scalar=ab[:], in1=dec[:, par, :],
                                                               op0=ALU.add, op1=ALU.mult).then_inc(lr_ok.h, 1)
                                nc.vector.tensor_copy(mx[:, par, 0:1], mx[:, old, SC:SC + 1])
                                dve.wait_ge(lr_ok.h, lr_ok.at(t + 1))
                                nc.vector.scalar_tensor_tensor(out=sc[:], in0=lr[:], scalar=0.2, in1=lr[:],
                                                               op0=ALU.mult, op1=ALU.max).then_inc(sc_ok.h, 1)
                                dve.wait_ge(rst_in[par].h, rst_in[par].at((i + 1) * 16))
                                dve.wait_ge(sc_ok.h, sc_ok.at(t + 1))
                                nc.vector.tensor_tensor_scan(mx[:, par, 1:SC + 1], rst[:, par, :], sc[:],
                                                             mx[:, old, SC:SC + 1], ALU.add, ALU.max).then_inc(mx_ok.h, 1)
                                dve.wait_ge(mx_ok.h, mx_ok.at(t + 1))
                                nc.vector.tensor_tensor(run[:], mx[:, par, 0:SC], rst[:, par, :], ALU.add).then_inc(sub_ok.h, 1)
                                dve.wait_ge(sub_ok.h, sub_ok.at(t + 1))
                                if known_ge(t, 2):
                                    dve.wait_ge(arg_ok.h, arg_ok.at(2 * (t - 1)))
                                nc.vector.tensor_tensor(gap[:, par, :], sc[:], run[:], ALU.subtract).then_inc(gap_ok.h, 1)
                            if known_ge(t, 1):
                                dve.wait_ge(pd_ok.h, pd_ok.at(t))
                                if known_ge(t, 3):
                                    dve.wait_ge(o_ps.h, o_ps.at(t - 2))
                                nc.vector.tensor_tensor_scan(den[:, old, :], pd[:, old, SC:2 * SC], pd[:, old, 0:SC],
                                                             den[:, par, SC - 1:SC], ALU.mult, ALU.add).then_inc(den_ok.h, 1)
                                dve.wait_ge(p_ps.h, p_ps.at(t))
                                dve.wait_ge(xs_ok.h, xs_ok.at(t))
                                if known_ge(t, 2):
                                    dve.wait_ge(scanned.h, scanned.at(2 * (t - 1)))
                                for g, bp in ((0, bP0), (1, bP1)):
                                    ins = nc.vector.tensor_tensor(pv[:, g, :], bp[:], xs[:, old, :], ALU.mult)
                                ins.then_inc(pv_ok.h, 1)
                                dve.wait_ge(pv_ok.h, pv_ok.at(t))
                                dve.wait_ge(d_ps.h, d_ps.at(t))
                                for g, bd in ((0, bD0), (1, bD1)):
                                    nc.vector.tensor_tensor_scan(num[:, old, g, :], bd[:], pv[:, g, :],
                                                                 num[:, par, g, SC - 1:SC], ALU.mult, ALU.add).then_inc(scanned.h, 1)
                        run_steps(dve, body, T, after=1)
                tmp_ok.passed(4)
                for j in range(2):
                    for s, n in ((idx_in, 16), (dec_in, 16), (rst_in, 16), (gathered, 32 * CH), (stored, 16)):
                        s[j].passed(n * T2)
                for s in (aT, pair_ok, xs_ok, l_ps, lr_ok, sc_ok, mx_ok, sub_ok, gap_ok, pd_ok, p_ps, d_ps, pv_ok, den_ok, den_ps, dn_ok, o_ps, o_ok):
                    s.passed(T)
                scanned.passed(2 * T)
                arg_ok.passed(2 * T)

        def layer2_edges(layer):
            with ExitStack() as ctx:
                idx = sb(ctx, f"idx2_{layer}", [P, 2, 2 * CH], I32)
                gx = sb(ctx, f"gx2_{layer}", [P, 2, CH, 2 * D])
                keep = sb(ctx, f"keep2_{layer}", [P, 2, SC])
                sums = sb(ctx, f"sums2_{layer}", [P, 2, SC])
                o = sb(ctx, f"o2_{layer}", [P, 2, CH, 2 * D])
                idx_in, keep_in, gathered, stored = ([S(f"{n}{j}") for j in range(2)] for n in (
                    "idx_in", "rst_in", "gathered", "stored"))
                xT, scanned, o_ps, o_ok, tmp_ok = (S(n) for n in ("xT", "scanned", "o_ps", "o_ok", "tmp_ok"))

                def gathers(par):
                    for j in range(CH):
                        for half in range(2):
                            yield gx[:, par, j, half * D:(half + 1) * D], tab_row, idx[:, par, half * CH + j:half * CH + j + 1]

                with nc.Block() as block:
                    @block.sync
                    def _(sp):
                        def body(t, par, i):
                            if known_lt(t, T2):
                                if known_ge(t, 2):
                                    sp.wait_ge(gathered[par].h, gathered[par].at(i * (32 * CH)))
                                sp.dma_start(idx[:, par, :], a["idx_halves"][bass.ds(t, 1)].rearrange("t p j -> p (t j)")).then_inc(idx_in[par].h, 16)
                                if known_ge(t, 2):
                                    sp.wait_ge(scanned.h, scanned.at(t - 1))
                                sp.dma_start(keep[0:D, par, :], edges(keep_mul, t).partition_broadcast(D)).then_inc(keep_in[par].h, 16)
                                sp.dma_start(keep[D:P, par, :], edges(keep_mul, t + T2).partition_broadcast(D)).then_inc(keep_in[par].h, 16)
                            if known_ge(t, 3):
                                u = t - 3
                                sp.wait_ge(o_ok.h, o_ok.at(u + 1))
                                sp.dma_start(rows2[bass.ds(u * SC, SC), :].rearrange("(c p) w -> p c w", p=P),
                                             o[:, 1 - par, :, :]).then_inc(stored[1 - par].h, 16)
                        run_steps(sp, body, T2, after=3)
                        for j in range(2):
                            sp.wait_ge(stored[j].h, stored[j].at(8 * T2))

                    @block.gpsimd
                    def _(pool):
                        run_steps(pool, lambda t, par, i: gather_step(pool, t, par, i, gathers, T2, idx_in, (xT,), gathered), T2)

                    @block.tensor
                    def _(pe):
                        def body(t, par, i):
                            if known_lt(t, T2):
                                pe.wait_ge(gathered[par].h, gathered[par].at((i + 1) * (32 * CH)))
                                if known_ge(t, 2):
                                    pe.wait_ge(scanned.h, scanned.at(t - 1))
                                for c in range(CH):
                                    mm = nc.tensor.transpose(bank[par][:, c * P:(c + 1) * P], gx[:, par, c, :], ident[:])
                                mm.then_inc(xT.h, 1)
                            if known_ge(t, 1):
                                pe.wait_ge(scanned.h, scanned.at(t))
                                if known_ge(t, 3):
                                    pe.wait_ge(o_ok.h, o_ok.at(t - 2))
                                for c in range(CH):
                                    mm = nc.tensor.transpose(bank[3 - par][:, c * P:(c + 1) * P], sums[:, 1 - par, c * P:(c + 1) * P], ident[:])
                                mm.then_inc(o_ps.h, 1)
                        run_steps(pe, body, T2, after=1)

                    @block.vector
                    def _(dve):
                        nc.vector.memset(sums[:, 1, :], 0.0).then_inc(tmp_ok.h, 1)
                        dve.wait_ge(tmp_ok.h, tmp_ok.at(1))

                        def body(t, par, i):
                            dve.wait_ge(xT.h, xT.at(t + 1))
                            dve.wait_ge(keep_in[par].h, keep_in[par].at((i + 1) * 32))
                            if known_ge(t, 2):
                                dve.wait_ge(o_ps.h, o_ps.at(t - 1))
                            if known_ge(t, 1):
                                dve.wait_ge(scanned.h, scanned.at(t))
                            nc.vector.tensor_tensor_scan(sums[:, par, :], keep[:, par, :], bank[par][:],
                                                         sums[:, 1 - par, SC - 1:SC], ALU.mult, ALU.add).then_inc(scanned.h, 1)
                        run_steps(dve, body, T2)

                    @block.scalar
                    def _(act):
                        def body(t, par, i):
                            act.wait_ge(o_ps.h, o_ps.at(t + 1))
                            if known_ge(t, 2):
                                act.wait_ge(stored[par].h, stored[par].at(i * 16))
                            nc.scalar.activation(o[:, par, :, :], bank[2 + par][:].rearrange("p (c w) -> p c w", w=P),
                                                 ACT.Copy).then_inc(o_ok.h, 1)
                        run_steps(act, body, T2)
                tmp_ok.passed(1)
                for j in range(2):
                    for s, n in ((idx_in, 16), (keep_in, 32), (gathered, 32 * CH), (stored, 16)):
                        s[j].passed(n * T2 // 2)
                for s in (xT, scanned, o_ps, o_ok):
                    s.passed(T2)

        def layer3_edges():
            EF = 32
            with ExitStack() as ctx:
                wab = sb(ctx, "wab3", [P, HID])
                wc = sb(ctx, "wc3", [EF + 1, HID])
                gb = sb(ctx, "gb3", [P, 2])
                cut = sb(ctx, "cut3", [P, 2])
                half_neg = sb(ctx, "half_neg3", [P, CH])
                idx = sb(ctx, "idx3", [P, 2, 2 * CH], I32)
                gx = sb(ctx, "gx3", [P, 2, CH, 2 * D])
                ea = sb(ctx, "ea3", [EF + 1, 2, SC])
                hold = sb(ctx, "hold3", [P, 2, SC])
                keep = sb(ctx, "keep3", [P, 2, SC])
                pair = sb(ctx, "pair3", [P, 2, SC])
                sq = sb(ctx, "sq3", [P, 2, SC])
                ssum = sb(ctx, "ssum3", [P, 2, CH])
                var = sb(ctx, "var3", [P, 2, CH])
                rstd = sb(ctx, "rstd3", [P, 2, CH])
                nrm = sb(ctx, "nrm3", [P, 2, SC])
                si = sb(ctx, "si3", [P, 2, SC])
                sums = sb(ctx, "sums3", [P, 2, SC])
                o = sb(ctx, "o3", [P, 2, CH, HID])
                load_all([(wab[:], a["W_msg1"][0:2 * D, :]), (wc[0:EF, :], a["W_msg1"][2 * D:2 * D + EF, :]),
                          (wc[EF:EF + 1, :], a["b_msg1"]), (gb[:, 0:1], a["g_msg"]), (gb[:, 1:2], a["be_msg"])])
                with nc.Block() as block:
                    @block.vector
                    def _(dve):
                        for w, n, k in ((wab, P, 0), (wc, EF + 1, 1)):
                            chain(dve, nc.vector.reduce_sum(cut[0:n, k:k + 1], w[:], AX_X))
                            chain(dve, nc.vector.tensor_scalar(cut[0:n, k:k + 1], cut[0:n, k:k + 1], 1.0 / HID, None, ALU.mult))
                            chain(dve, nc.vector.tensor_scalar(w[:], w[:], cut[0:n, k:k + 1], None, ALU.subtract))
                        chain(dve, nc.vector.memset(half_neg[:], -0.5))
                        chain(dve, nc.vector.memset(ea[EF:EF + 1, :, :], 1.0))
                        chain(dve, nc.vector.memset(sums[:, 1, :], 0.0))
                        chain(dve, nc.vector.memset(pair[D:P, 1, :], 0.0))
                bA, bH, bT, bO = (bank[2 * k:2 * k + 2] for k in range(4))
                idx_in, ea_in, hold_in, keep_in, dst_in, gathered, stored = ([S(f"{n}{j}") for j in range(2)] for n in (
                    "idx_in", "feat_in", "hold_in", "rst_in", "sh_in", "gathered", "stored"))
                aT, src_ok, dst_ok, h_ps, sq_ok, ssum_ok, var_ok, rstd_ok, nrm_ok = (S(n) for n in (
                    "xT", "hid_ok", "z_ok", "h_ps", "wk_ok", "v_ps", "wv_ok", "pd_ok", "kw_ok"))
                t_ps, si_ok, scanned, o_ps, o_ok = (S(n) for n in ("k_ps", "pv_ok", "scanned", "o_ps", "o_ok"))

                def gathers(par):
                    for j in range(CH):
                        yield gx[:, par, j, 0:D], tab_row, idx[:, par, j:j + 1]

                with nc.Block() as block:
                    @block.sync
                    def _(sp):
                        def body(t, par, i):
                            old = 1 - par
                            if known_lt(t, T - 1):
                                if known_ge(t, 1):
                                    sp.wait_ge(gathered[old].h, gathered[old].at((i + par) * (16 * CH)))
                                sp.dma_start(idx[:, old, :], a["idx"][bass.ds(t + 1, 1)].rearrange("t p j -> p (t j)")).then_inc(idx_in[old].h, 16)
                                if known_ge(t, 1):
                                    sp.wait_ge(aT.h, aT.at(t))
                                    nc.sync.sem_inc(S("sp_turn").h, 1)
                                sp.dma_start(gx[:, old, :, D:2 * D], dst_first[bass.ds(t * SC + SC, SC), :].rearrange("(c p) w -> p c w", p=P)
                                             ).then_inc(dst_in[old].h, 16)
                                if known_ge(t, 1):
                                    sp.wait_ge(dst_ok.h, dst_ok.at(t))
                                    nc.sync.sem_inc(S("sp_turn").h, 1)
                                sp.dma_start(hold[D:P, old, :], edges(keep_mul, t + 1).partition_broadcast(D)).then_inc(hold_in[old].h, 16)
                            if known_ge(t, 0) and known_lt(t, T):
                                if known_ge(t, 2):
                                    sp.wait_ge(h_ps.h, h_ps.at(t - 1))
                                    nc.sync.sem_inc(S("sp_turn").h, 1)
                                sp.dma_start(ea[0:EF, par, :], a["ea"][:, bass.ds(t * SC, SC)]).then_inc(ea_in[par].h, 16)
                            if known_ge(t, 3):
                                u = t - 3
                                if known_ge(t, 5):
                                    sp.wait_ge(scanned.h, scanned.at(t - 4))
                                sp.dma_start(keep[:, old, :], edges(keep_mul, u).partition_broadcast(P)).then_inc(keep_in[old].h, 16)
                            if known_ge(t, 5):
                                u = t - 5
                                sp.wait_ge(o_ok.h, o_ok.at(u + 1))
                                sp.dma_start(rows3[bass.ds(u * SC, SC), :].rearrange("(c p) w -> p c w", p=P),
                                             o[:, old, :, :]).then_inc(stored[old].h, 16)
                        run_steps(sp, body, T, before=1, after=3, first=6)
                        for u in (T - 2, T - 1):
                            sp.wait_ge(o_ok.h, o_ok.at(u + 1))
                            sp.dma_start(rows3[u * SC:(u + 1) * SC, :].rearrange("(c p) w -> p c w", p=P),
                                         o[:, u % 2, :, :]).then_inc(stored[u % 2].h, 16)
                        for j in range(2):
                            sp.wait_ge(stored[j].h, stored[j].at(16 * T2))

                    @block.gpsimd
                    def _(pool):
                        def body(t, par, i):
                            old = 1 - par
                            gather_step(pool, t, par, i, gathers, T, idx_in, (aT,), gathered)
                            if known_ge(t, 3):
                                pool.wait_ge(var_ok.h, var_ok.at(t - 2))
                                if known_ge(t, 5):
                                    pool.wait_ge(nrm_ok.h, nrm_ok.at(t - 4))
                                nc.gpsimd.tensor_tensor(rstd[:, old, :], var[:, old, :], half_neg[:], ALU.pow).then_inc(rstd_ok.h, 1)
                        run_steps(pool, body, T, after=3, first=6)

                    @block.tensor
                    def _(pe):
                        def body(t, par, i):
                            old = 1 - par
                            if known_lt(t, T - 1):
                                pe.wait_ge(gathered[old].h, gathered[old].at((i + par + 1) * (16 * CH)))
                                pe.wait_ge(dst_in[old].h, dst_in[old].at((i + par + 1) * 16))
                                if known_ge(t, 1):
                                    pe.wait_ge(src_ok.h, src_ok.at(t))
                                    pe.wait_ge(dst_ok.h, dst_ok.at(t))
                                for c in range(CH):
                                    mm = nc.tensor.transpose(bA[old][:, c * P:(c + 1) * P], gx[:, old, c, :], ident[:])
                                mm.then_inc(aT.h, 1)
                            if known_ge(t, 2) and known_lt(t, T + 2):
                                pe.wait_ge(nrm_ok.h, nrm_ok.at(t - 1))
                                if known_ge(t, 4):
                                    pe.wait_ge(si_ok.h, si_ok.at(t - 3))
                                for c in range(CH):
                                    mm = nc.tensor.transpose(bT[par][:, c * P:(c + 1) * P], nrm[:, par, c * P:(c + 1) * P], ident[:])
                                mm.then_inc(t_ps.h, 1)
                            if known_ge(t, 0) and known_lt(t, T):
                                pe.wait_ge(src_ok.h, src_ok.at(t + 1))
                                pe.wait_ge(dst_ok.h, dst_ok.at(t + 1))
                                pe.wait_ge(ea_in[par].h, ea_in[par].at((i + 1) * 16))
                                if known_ge(t, 2):
                                    pe.wait_ge(nrm_ok.h, nrm_ok.at(t - 1))
                                for c in range(CH):
                                    cut_c = slice(c * P, (c + 1) * P)
                                    nc.tensor.matmul(bH[par][:, cut_c], pair[:, par, cut_c], wab[:], start=True, stop=False)
                                    mm = nc.tensor.matmul(bH[par][:, cut_c], ea[:, par, cut_c], wc[:], start=False, stop=True)
                                mm.then_inc(h_ps.h, 1)
                            if known_ge(t, 3):
                                pe.wait_ge(scanned.h, scanned.at(t - 2))
                                if known_ge(t, 5):
                                    pe.wait_ge(o_ok.h, o_ok.at(t - 4))
                                for c in range(CH):
                                    mm = nc.tensor.transpose(bO[old][:, c * P:(c + 1) * P], sums[:, old, c * P:(c + 1) * P], ident[:])
                                mm.then_inc(o_ps.h, 1)
                        run_steps(pe, body, T, before=1, after=3, first=6)

                    @block.scalar
                    def _(act):
                        def body(t, par, i):
                            old = 1 - par
                            if known_ge(t, 1) and known_lt(t, T + 1):
                                act.wait_ge(h_ps.h, h_ps.at(t))
                                if known_ge(t, 3):
                                    act.wait_ge(ssum_ok.h, ssum_ok.at(t - 2))
                                nc.scalar.activation(sq[:, old, :], bH[old][:], ACT.Square).then_inc(sq_ok.h, 1)
                            if known_ge(t, 4):
                                act.wait_ge(o_ps.h, o_ps.at(t - 3))
                                if known_ge(t, 6):
                                    act.wait_ge(stored[par].h, stored[par].at((i - 2) * 16))
                                nc.scalar.activation(o[:, par, :, :], bO[par][:].rearrange("p (c w) -> p c w", w=P), ACT.Copy).then_inc(o_ok.h, 1)
                            if known_lt(t, T - 1):
                                act.wait_ge(aT.h, aT.at(t + 2))
                                if known_ge(t, 1):
                                    act.wait_ge(h_ps.h, h_ps.at(t))
                                nc.scalar.activation(pair[0:D, old, :], bA[old][0:D, :], ACT.Copy).then_inc(src_ok.h, 1)
                            if known_ge(t, 2) and known_lt(t, T + 2):
                                act.wait_ge(t_ps.h, t_ps.at(t - 1))
                                if known_ge(t, 4):
                                    act.wait_ge(scanned.h, scanned.at(t - 3))
                                nc.scalar.activation(si[:, par, :], bT[par][:], ACT.Silu, scale=gb[:, 0:1], bias=gb[:, 1:2]).then_inc(si_ok.h, 1)
                        run_steps(act, body, T, before=1, after=4, first=6)

                    @block.vector
                    def _(dve):
                        def body(t, par, i):
                            old = 1 - par
                            if known_ge(t, 2) and known_lt(t, T + 2):
                                dve.wait_ge(rstd_ok.h, rstd_ok.at(t - 1))
                                if known_ge(t, 4):
                                    dve.wait_ge(t_ps.h, t_ps.at(t - 3))
                                nc.vector.tensor_tensor(nrm[:, par, :].rearrange("p (c w) -> p c w", w=P),
                                                        bH[par][:].rearrange("p (c w) -> p c w", w=P),
                                                        rstd[:, par, :].unsqueeze(2).to_broadcast([P, CH, P]), ALU.mult).then_inc(nrm_ok.h, 1)
                            if known_ge(t, 1) and known_lt(t, T + 1):
                                dve.wait_ge(sq_ok.h, sq_ok.at(t))
                                nc.vector.reduce_sum(ssum[:, old, :], sq[:, old, :].rearrange("p (c w) -> p c w", w=P), AX_X).then_inc(ssum_ok.h, 1)
                                dve.wait_ge(ssum_ok.h, ssum_ok.at(t))
                                if known_ge(t, 3):
                                    dve.wait_ge(rstd_ok.h, rstd_ok.at(t - 2))
                                nc.vector.tensor_scalar(var[:, old, :], ssum[:, old, :], 1.0 / HID, EPS, ALU.mult, ALU.add).then_inc(var_ok.h, 1)
                            if known_lt(t, T - 1):
                                dve.wait_ge(aT.h, aT.at(t + 2))
                                dve.wait_ge(hold_in[old].h, hold_in[old].at((i + par + 1) * 16))
                                if known_ge(t, 1):
                                    dve.wait_ge(h_ps.h, h_ps.at(t))
                                if known_ge(t, 0):
                                    dve.wait_ge(dst_ok.h, dst_ok.at(t + 1))
                                nc.vector.tensor_tensor_scan(pair[D:P, old, :], hold[D:P, old, :], bA[old][D:P, :],
                                                             pair[D:P, par, SC - 1:SC], ALU.mult, ALU.add).then_inc(dst_ok.h, 1)
                            if known_ge(t, 3):
                                dve.wait_ge(si_ok.h, si_ok.at(t - 2))
                                dve.wait_ge(keep_in[old].h, keep_in[old].at((i + par - 1) * 16))
                                if known_ge(t, 5):
                                    dve.wait_ge(o_ps.h, o_ps.at(t - 4))
                                if known_ge(t, 4):
                                    dve.wait_ge(scanned.h, scanned.at(t - 3))
                                nc.vector.tensor_tensor_scan(sums[:, old, :], keep[:, old, :], si[:, old, :],
                                                             sums[:, par, SC - 1:SC], ALU.mult, ALU.add).then_inc(scanned.h, 1)
                        run_steps(dve, body, T, before=1, after=3, first=6)
                for j in range(2):
                    for s, n in ((idx_in, 16), (ea_in, 16), (hold_in, 16), (keep_in, 16), (dst_in, 16), (gathered, 16 * CH), (stored, 16)):
                        s[j].passed(n * T2)
                for s in (aT, src_ok, dst_ok, h_ps, sq_ok, ssum_ok, var_ok, rstd_ok, nrm_ok, t_ps, si_ok, scanned, o_ps, o_ok):
                    s.passed(T)

        def vector_step(*ops):
            with nc.Block() as block:
                @block.vector
                def _(dve):
                    for op in ops:
                        chain(dve, op())

        def add_back(bT):
            turn([(bT, tmp_n[:, :, 0:D], D, True)])
            vector_step(lambda: nc.vector.tensor_tensor(xn[:], xn[:], tmp_n[:, :, 0:D], ALU.add))

        prepare()

        pre_norm()
        turn([(hn[:], hT[:], D, False)])
        with ExitStack() as ctx:
            wq = sb(ctx, "wq", [D, P])
            load_all([(wq[:], a["Wq"])])
            product_rows([(hT[:], wq[:])], P, tmp_n[:])
            store_tables([(node_rows(tab_q, P), tmp_n[:]), (node_rows(tab_dup, 2 * D)[:, :, 0:D], hn[:]),
                          (node_rows(tab_dup, 2 * D)[:, :, D:2 * D], hn[:])])
        layer0_edges()
        with ExitStack() as ctx:
            g0 = sb(ctx, "g0", [P, NB, W0])
            rden = sb(ctx, "rden0", [P, NB, HEADS0])
            upd = sb(ctx, "upd0", [P, NB, P])
            updT = sb(ctx, "updT0", [P, NP])
            sumT = sb(ctx, "sumT0", [D, NP])
            bnT = sb(ctx, "bnT0", [D, NP])
            scT = sb(ctx, "scT0", [D, NP])
            w_out = sb(ctx, "w_out0", [P, D])
            w_self = sb(ctx, "w_self0", [D, D])
            gb = sb(ctx, "gb0", [D, 2])
            read_rows([(rows0, last_row, g0)],
                      [(w_out[:], a["W_out"]), (w_self[:], a["W_self"]), (gb[:, 0:1], a["gamma0"]), (gb[:, 1:2], a["beta0"])])
            vector_step(
                lambda: nc.vector.tensor_scalar(rden[:], g0[:, :, P:W0], 1e-16, None, ALU.add),
                lambda: nc.vector.reciprocal(rden[:], rden[:]),
                *[(lambda h=h: nc.vector.tensor_tensor(
                    upd[:, :, h * DH0:(h + 1) * DH0], g0[:, :, h * DH0:(h + 1) * DH0],
                    rden[:, :, h:h + 1].to_broadcast([P, NB, DH0]), ALU.mult)) for h in range(HEADS0)])
            turn([(upd[:], updT[:], P, False)])
            product_T([(w_out[:], updT[:]), (w_self[:], hT[:])], D, sumT[:])
            batch_norm(sumT[:], gb[:, 0:1], gb[:, 1:2], bnT[:], scT[:])
            add_back(bnT[:])

        pre_norm()
        turn([(hn[:], hT[:], D, False)])
        with ExitStack() as ctx:
            ww = sb(ctx, "ww", [D, D])
            wb = sb(ctx, "wb", [P, D])
            load_all([(ww[:], a["W_w"]), (wb[:], a["W_b"].partition_broadcast(P))])
            product_rows([(hT[:], ww[:])], D, tmp_n[:, :, 0:D], bias=wb[:])
            store_tables([(node_rows(tab_row, D), tmp_n[:, :, 0:D])])
        layer1_edges()
        with ExitStack() as ctx:
            g1 = sb(ctx, "g1", [P, NB, W1])
            rden = sb(ctx, "rden1", [P, NB, HEADS1])
            aggT = [sb(ctx, f"aggT1{g}", [P, NP]) for g in range(2)]
            sumT = sb(ctx, "sumT1", [D, NP])
            pw = sb(ctx, "pw1", [P, 2, D])
            rows = sb(ctx, "brow1", [P, 3, D])
            zc = sb(ctx, "zc1", [P, NB, D])
            read_rows([(rows1, last_row, g1)],
                      [(pw[:, g, :], a["proj_w"][g * P:(g + 1) * P, :]) for g in range(2)]
                      + [(rows[:, k, :], a[n].partition_broadcast(P)) for k, n in enumerate(("proj_b", "ln_g", "ln_b"))])
            vector_step(
                lambda: nc.vector.tensor_scalar(rden[:], g1[:, :, 2 * P:W1], 1e-8, None, ALU.add),
                lambda: nc.vector.reciprocal(rden[:], rden[:]),
                *[(lambda h=h: nc.vector.tensor_tensor(
                    g1[:, :, h * D:(h + 1) * D], g1[:, :, h * D:(h + 1) * D],
                    rden[:, :, h:h + 1].to_broadcast([P, NB, D]), ALU.mult)) for h in range(HEADS1)])
            turn([(g1[:, :, g * P:(g + 1) * P], aggT[g][:], P, False) for g in range(2)])
            product_T([(pw[:, g, :], aggT[g][:]) for g in range(2)], D, sumT[:])
            turn([(sumT[:], tmp_n[:, :, 0:D], D, True)])
            row = lambda k: rows[:, k, :].unsqueeze(1).to_broadcast([P, NB, D])
            rs_sem, sd_sem = S("var_ready"), S("root_ready")
            with nc.Block() as block:
                @block.vector
                def _(dve):
                    z1 = tmp_n[:, :, 0:D]
                    chain(dve, nc.vector.tensor_tensor(z1, z1, row(0), ALU.add))
                    chain(dve, nc.vector.tensor_tensor(z1, z1, hn[:], ALU.add))
                    norm_rows(dve, z1, D, zc[:], tmp_n[:, :, D:2 * D], rs_sem, sd_sem)
                    chain(dve, nc.vector.tensor_tensor(zc[:], zc[:], row(1), ALU.mult))
                    chain(dve, nc.vector.tensor_tensor(zc[:], zc[:], row(2), ALU.add))
                    chain(dve, nc.vector.tensor_scalar(zc[:], zc[:], 0.0, None, ALU.max))
                    nc.vector.tensor_tensor(xn[:], xn[:], zc[:], ALU.add)

                @block.scalar
                def _(act):
                    root(act, rs_sem, sd_sem)
            rs_sem.passed(1)
            sd_sem.passed(1)

        pre_norm()
        with ExitStack() as ctx:
            w12 = sb(ctx, "w12", [D, 6, D])
            gb = sb(ctx, "gb2", [D, 6])
            scale = sb(ctx, "scale2", [P, 3])
            agg = sb(ctx, "agg2", [P, NB, D])
            more = sb(ctx, "more2", [P, NB, D])
            carry = sb(ctx, "carry2", [P, D])
            zT = sb(ctx, "zT2", [D, NP])
            uT = sb(ctx, "uT2", [D, NP])
            load_all([(w12[:, 0:3, :], a["W1T"].rearrange("l i o -> i l o")), (w12[:, 3:6, :], a["W2T"].rearrange("l i o -> i l o")),
                      (gb[:, 0:3], a["gamma2"]), (gb[:, 3:6], a["beta2"]), (scale[:], a["eps2"].partition_broadcast(P))])
            vector_step(lambda: nc.vector.tensor_scalar(scale[:], scale[:], 1.0, None, ALU.add))
            for layer in range(3):
                store_tables([(node_rows(tab_row, D), hn[:])])
                layer2_edges(layer)
                halves = rows2.rearrange("e (h w) -> (e h) w", h=2)
                read_rows([(halves, last_row2, agg)],
                          [(carry[:], halves[EP - 2:EP - 1, :].rearrange("r w -> (r w)").partition_broadcast(P))])
                vector_step(
                    lambda: nc.vector.tensor_tensor(more[:], carry[:].unsqueeze(1).to_broadcast([P, NB, D]),
                                                    crosses[:].unsqueeze(2).to_broadcast([P, NB, D]), ALU.mult),
                    lambda: nc.vector.tensor_tensor(agg[:], agg[:], more[:], ALU.add),
                    lambda: nc.vector.scalar_tensor_tensor(out=agg[:], in0=hn[:], scalar=scale[:, layer:layer + 1], in1=agg[:],
                                                           op0=ALU.mult, op1=ALU.add))
                turn([(agg[:], zT[:], D, False)])
                product_T([(w12[:, layer, :], zT[:])], D, uT[:], ACT.Relu)
                product_T([(w12[:, 3 + layer, :], uT[:])], D, zT[:], ACT.Relu)
                batch_norm(zT[:], gb[:, layer:layer + 1], gb[:, 3 + layer:4 + layer], uT[:], hT[:])
                turn([(uT[:], hn[:], D, True)])
            vector_step(lambda: nc.vector.tensor_tensor(xn[:], xn[:], hn[:], ALU.add))

        pre_norm()
        turn([(hn[:], hT[:], D, False)])
        store_tables([(node_rows(tab_row, D), hn[:])])
        put_first_rows(hn)
        layer3_edges()
        with ExitStack() as ctx:
            g3 = sb(ctx, "g3", [P, NB, HID])
            gT = sb(ctx, "gT3", [P, NP])
            agg = sb(ctx, "agg3", [P, NB, HID])
            wm2 = sb(ctx, "wm2", [HID, HID])
            wu1a = sb(ctx, "wu1a", [D, HID])
            wu1b = sb(ctx, "wu1b", [HID, HID])
            wu2 = sb(ctx, "wu2", [HID, D])
            rows = sb(ctx, "brow3", [P, 2, HID])
            gb = sb(ctx, "gb3u", [HID, 2])
            b_u2 = sb(ctx, "b_u2", [P, D])
            read_rows([(rows3, last_row, g3)],
                      [(wm2[:], a["W_msg2"]), (wu1a[:], a["W_upd1"][0:D, :]), (wu1b[:], a["W_upd1"][D:D + HID, :]),
                      (wu2[:], a["W_upd2"]), (b_u2[:], a["b_upd2"].partition_broadcast(P))]
                     + [(rows[:, k, :], a[n].partition_broadcast(P)) for k, n in enumerate(("b_msg2", "b_upd1"))]
                      + [(gb[:, k:k + 1], a[n]) for k, n in enumerate(("g_upd", "be_upd"))])
            turn([(g3[:], gT[:], P, False)])
            product_rows([(gT[:], wm2[:])], HID, agg[:])
            row = lambda k: rows[:, k, :].unsqueeze(1).to_broadcast([P, NB, HID])
            vector_step(
                lambda: nc.vector.tensor_tensor(g3[:], row(0), degree[:].unsqueeze(2).to_broadcast([P, NB, HID]), ALU.mult),
                lambda: nc.vector.tensor_tensor(agg[:], agg[:], g3[:], ALU.add))
            turn([(agg[:], gT[:], P, False)])
            product_rows([(hT[:], wu1a[:]), (gT[:], wu1b[:])], HID, agg[:], bias=rows[:, 1, :])
            rs_sem, sd_sem = S("var_ready"), S("root_ready")
            with nc.Block() as block:
                @block.vector
                def _(dve):
                    norm_rows(dve, agg[:], HID, g3[:], tmp_n[:], rs_sem, sd_sem)

                @block.scalar
                def _(act):
                    root(act, rs_sem, sd_sem)
            rs_sem.passed(1)
            sd_sem.passed(1)
            turn([(g3[:], gT[:], P, False)], ACT.Silu, scale=gb[:, 0:1], bias=gb[:, 1:2])
            product_rows([(gT[:], wu2[:])], D, tmp_n[:, :, 0:D], bias=b_u2[:])
            vector_step(
                lambda: nc.vector.tensor_tensor(hn[:], hn[:], tmp_n[:, :, 0:D], ALU.add),
                lambda: nc.vector.tensor_tensor(xn[:], xn[:], hn[:], ALU.add))
            store_tables([(out.rearrange("(p b) w -> p b w", b=NB), xn[0:PV])])


def constants():
    p = np.arange(P)
    headsum = (p[:, None] // DH0 == p[None, :] // DH0).astype(np.float32)
    pick1 = (p[:, None] == 32 * np.arange(HEADS1)[None, :]).astype(np.float32)
    spread1 = (p[:, None] == 32 * (np.arange(2 * P)[None, :] // D)).astype(np.float32)
    return {"ident": np.eye(P, dtype=np.float32), "headsum": headsum, "pick1": pick1, "spread1": spread1}


def lay_out(i):
    c = np.ascontiguousarray
    pad_e = EP - E
    src = np.pad(np.asarray(i["src"]), (0, pad_e))
    dst = np.pad(np.asarray(i["dst"]), (0, pad_e), constant_values=N)
    by_step = lambda v, steps: v.reshape(steps, CH, P).transpose(0, 2, 1)
    before = np.concatenate([np.full(1, -1, dst.dtype), dst[:-1]])
    col = lambda n: c(np.asarray(i[n]).reshape(-1, 1))
    wide = lambda n: c(np.pad(np.asarray(i[n]), ((0, pad_e), (0, 0))).T)
    return {
        "x": np.pad(np.asarray(i["x"]), ((0, NP - N), (0, 0))),
        "idx": c(np.concatenate([by_step(src, T), by_step(dst, T)], axis=2)),
        "idx_halves": c(np.concatenate([by_step(src[:HALF], T2), by_step(src[HALF:], T2)], axis=2)),
        "dst_rows": np.concatenate([dst, np.full(P, 2 * NP, dst.dtype)]).reshape(NC_ + 1, P),
        "chunk_last": c(dst[P - 1::P]),
        "dst_now": dst.reshape(P, NC_), "dst_before": before.reshape(P, NC_),
        "edge_weight": np.pad(np.asarray(i["edge_weight"]), (0, pad_e)).reshape(P, NC_),
        "ef": wide("edge_attr_64"), "sh": wide("edge_attr_9"), "ea": wide("edge_attr_32"),
        "Wq": c(i["L0_gnn_Wq"]), "Cqk": c(np.asarray(i["L0_gnn_Cqk"]).transpose(1, 0, 2)),
        "Cv": c(np.asarray(i["L0_gnn_Cv"]).transpose(1, 0, 2)),
        "k_w1": c(i["L0_gnn_k_w1"]), "v_w1": c(i["L0_gnn_v_w1"]), "k_w2": c(i["L0_gnn_k_w2"]), "v_w2": c(i["L0_gnn_v_w2"]),
        "k_b1": col("L0_gnn_k_b1"), "v_b1": col("L0_gnn_v_b1"), "k_b2": col("L0_gnn_k_b2"), "v_b2": col("L0_gnn_v_b2"),
        "W_out": c(i["L0_gnn_W_out"]), "W_self": c(i["L0_gnn_W_self"]),
        "gamma0": col("L0_gnn_gamma"), "beta0": col("L0_gnn_beta"),
        "W_w": c(i["L1_gnn_W_w"]), "W_b": c(i["L1_gnn_W_b"]), "attn_w": c(i["L1_gnn_attn_w"]), "attn_b": c(i["L1_gnn_attn_b"]),
        "decay_rate": c(i["L1_gnn_decay_rate"]),
        "proj_w": c(np.asarray(i["L1_gnn_proj_w"]).reshape(D, HEADS1, D).transpose(1, 0, 2)).reshape(HEADS1 * D, D),
        "proj_b": c(i["L1_gnn_proj_b"]), "ln_g": c(i["L1_gnn_ln_g"]), "ln_b": c(i["L1_gnn_ln_b"]),
        "W1T": c(np.asarray(i["L2_gnn_W1"]).transpose(0, 2, 1)), "W2T": c(np.asarray(i["L2_gnn_W2"]).transpose(0, 2, 1)),
        "gamma2": c(np.asarray(i["L2_gnn_gamma"]).T), "beta2": c(np.asarray(i["L2_gnn_beta"]).T), "eps2": c(i["L2_gnn_eps"]),
        "W_msg1": c(i["L3_gnn_W_msg1"]), "b_msg1": np.asarray(i["L3_gnn_b_msg1"]).reshape(1, HID), "g_msg": col("L3_gnn_g_msg"), "be_msg": col("L3_gnn_be_msg"),
        "W_msg2": c(i["L3_gnn_W_msg2"]), "b_msg2": c(i["L3_gnn_b_msg2"]),
        "W_upd1": c(i["L3_gnn_W_upd1"]), "b_upd1": c(i["L3_gnn_b_upd1"]), "g_upd": col("L3_gnn_g_upd"),
        "be_upd": col("L3_gnn_be_upd"), "W_upd2": c(i["L3_gnn_W_upd2"]), "b_upd2": c(i["L3_gnn_b_upd2"]),
    }


def kernel(**inputs):
    import concourse.bacc as bacc
    from concourse.bass_utils import run_bass_kernel_spmd as run

    nc = bacc.Bacc("TRN2", target_bir_lowering=False, num_devices=1)
    arrays, aps = {}, {}
    for name, value in {**lay_out(inputs), **constants()}.items():
        value = np.ascontiguousarray(value)
        arrays[f"in_{name}"] = value
        aps[name] = nc.dram_tensor(f"in_{name}", value.shape, mybir.dt.from_np(value.dtype), kind="ExternalInput").ap()
    out = nc.dram_tensor("out_0", (N, D), F32, kind="ExternalOutput").ap()
    build(nc, aps, out)
    return run(nc, [arrays], core_ids=[0]).results[0]["out_0"]
```
